# Optimizing a Trainium2 kernel written in Bass

```python
import numpy as np
import jax
import jax.numpy as jnp

def _softmax(x, axis=-1):
    return jax.nn.softmax(x, axis=axis)

def _gelu(x):
    return jax.nn.gelu(x, approximate=True)

def _silu(x):
    return jax.nn.silu(x)

def _sigmoid(x):
    return jax.nn.sigmoid(x)

def _layernorm(x, axis=-1, eps=1e-05):
    m = jnp.mean(x, axis=axis, keepdims=True)
    v = jnp.var(x, axis=axis, keepdims=True)
    return (x - m) / jnp.sqrt(v + eps)

def _scatter_add(tgt, idx, src, axis=0):
    return tgt.at[idx].add(src)

def _segment_sum(src, seg, n):
    return jax.ops.segment_sum(src, seg, n)
kernel_name = 'mk_seq_preln_d2_jaxref_r8_6cfa47'

def setup_inputs(seed: int=0):
    np.random.seed(seed)
    _w = jnp.asarray

    def _L0_attn_setup():
        import jax, jax.numpy as jnp
        import numpy as np
        EPS = 1e-15
        HEAD_DIM = 32
        PAD_VAL = 1.0
        key = jax.random.key(seed)
        k1, k2, k3, k4 = jax.random.split(key, 4)
        B, N, C = (2, 512, 256)
        s = 1.0 / np.sqrt(C).astype(np.float32)
        x = jax.random.normal(k1, (B, N, C), jnp.float32)
        w_qkv = jax.random.normal(k2, (3 * C, C), jnp.float32) * s
        w_proj = jax.random.normal(k3, (C, C), jnp.float32) * s
        b_proj = jax.random.normal(k4, (C,), jnp.float32) * 0.01
        return {'x': x, 'w_qkv': w_qkv, 'w_proj': w_proj, 'b_proj': b_proj}
    _L0_attn_in = _L0_attn_setup()

    def _L0_ffn_setup():
        import jax, jax.numpy as jnp
        import numpy as np
        H = 256
        key = jax.random.key(seed)
        ks = jax.random.split(key, 10)
        s = 1.0 / np.sqrt(H)
        x = jax.random.normal(ks[0], (4, 256, H), dtype=jnp.float32)
        Wg = jax.random.uniform(ks[1], (2, H), jnp.float32, -s, s)
        W0a = jax.random.uniform(ks[2], (2 * H, H), jnp.float32, -s, s)
        b0a = jax.random.uniform(ks[3], (2 * H,), jnp.float32, -s, s)
        W0b = jax.random.uniform(ks[4], (H, 2 * H), jnp.float32, -s, s)
        b0b = jax.random.uniform(ks[5], (H,), jnp.float32, -s, s)
        W1a = jax.random.uniform(ks[6], (2 * H, H), jnp.float32, -s, s)
        b1a = jax.random.uniform(ks[7], (2 * H,), jnp.float32, -s, s)
        W1b = jax.random.uniform(ks[8], (H, 2 * H), jnp.float32, -s, s)
        b1b = jax.random.uniform(ks[9], (H,), jnp.float32, -s, s)
        return {'x': x, 'Wg': Wg, 'W0a': W0a, 'b0a': b0a, 'W0b': W0b, 'b0b': b0b, 'W1a': W1a, 'b1a': b1a, 'W1b': W1b, 'b1b': b1b}
    _L0_ffn_in = _L0_ffn_setup()

    def _L1_attn_setup():
        import jax, jax.numpy as jnp
        import numpy as np
        import math
        N_Q = 128
        N_K = 128
        N_V = 128
        D_MODEL = 256
        N_HEADS = 16
        B, T = (8, 512)
        key = jax.random.key(seed)
        ks = jax.random.split(key, 9)
        s = 0.02
        return {'x': jax.random.normal(ks[0], (B, T, D_MODEL), dtype=jnp.float32), 'Wq': jax.random.normal(ks[1], (D_MODEL, N_Q * N_HEADS), dtype=jnp.float32) * s, 'bq': jnp.zeros((N_Q * N_HEADS,), dtype=jnp.float32), 'Wk': jax.random.normal(ks[2], (D_MODEL, N_K * N_HEADS), dtype=jnp.float32) * s, 'bk': jnp.zeros((N_K * N_HEADS,), dtype=jnp.float32), 'Wv': jax.random.normal(ks[3], (D_MODEL, N_V * N_HEADS), dtype=jnp.float32) * s, 'bv': jnp.zeros((N_V * N_HEADS,), dtype=jnp.float32), 'Wo': jax.random.normal(ks[4], (N_V * N_HEADS, D_MODEL), dtype=jnp.float32) * s, 'bo': jnp.zeros((D_MODEL,), dtype=jnp.float32)}
    _L1_attn_in = _L1_attn_setup()

    def _L1_ffn_setup():
        import jax, jax.numpy as jnp
        import numpy as np
        EPS = 1e-08

        def _bit_quant(w):
            scale = jnp.maximum(jnp.mean(jnp.abs(w)), EPS)
            w_ternary = jnp.clip(jnp.round(w / scale), -1.0, 1.0)
            return w + jax.lax.stop_gradient(w_ternary - w)
        key = jax.random.key(seed)
        k = jax.random.split(key, 5)
        emb, dff = (256, 1024)
        B, S = (4, 256)
        x = jax.random.normal(k[0], (B, S, emb), dtype=jnp.float32)
        w1 = jax.random.normal(k[1], (dff, emb), dtype=jnp.float32) * 0.02
        b1 = jax.random.normal(k[2], (dff,), dtype=jnp.float32) * 0.02
        w2 = jax.random.normal(k[3], (emb, dff), dtype=jnp.float32) * 0.02
        b2 = jax.random.normal(k[4], (emb,), dtype=jnp.float32) * 0.02
        return {'x': x, 'w1': w1, 'b1': b1, 'w2': w2, 'b2': b2}
    _L1_ffn_in = _L1_ffn_setup()
    _d = {'L0_attn_x': _L0_attn_in['x'], 'L0_attn_w_qkv': _L0_attn_in['w_qkv'], 'L0_attn_w_proj': _L0_attn_in['w_proj'], 'L0_attn_b_proj': _L0_attn_in['b_proj'], 'L0_ffn_Wg': _L0_ffn_in['Wg'], 'L0_ffn_W0a': _L0_ffn_in['W0a'], 'L0_ffn_b0a': _L0_ffn_in['b0a'], 'L0_ffn_W0b': _L0_ffn_in['W0b'], 'L0_ffn_b0b': _L0_ffn_in['b0b'], 'L0_ffn_W1a': _L0_ffn_in['W1a'], 'L0_ffn_b1a': _L0_ffn_in['b1a'], 'L0_ffn_W1b': _L0_ffn_in['W1b'], 'L0_ffn_b1b': _L0_ffn_in['b1b'], 'L1_attn_Wq': _L1_attn_in['Wq'], 'L1_attn_bq': _L1_attn_in['bq'], 'L1_attn_Wk': _L1_attn_in['Wk'], 'L1_attn_bk': _L1_attn_in['bk'], 'L1_attn_Wv': _L1_attn_in['Wv'], 'L1_attn_bv': _L1_attn_in['bv'], 'L1_attn_Wo': _L1_attn_in['Wo'], 'L1_attn_bo': _L1_attn_in['bo'], 'L1_ffn_w1': _L1_ffn_in['w1'], 'L1_ffn_b1': _L1_ffn_in['b1'], 'L1_ffn_w2': _L1_ffn_in['w2'], 'L1_ffn_b2': _L1_ffn_in['b2']}
    _x0 = _d['L0_attn_x']
    _d['L0_attn_x'] = jax.random.normal(jax.random.fold_in(jax.random.key(seed), 1), (2, 1024, 256), dtype=_x0.dtype)
    del _x0
    return _d

def reference(L0_attn_x, L0_attn_w_qkv, L0_attn_w_proj, L0_attn_b_proj, L0_ffn_Wg, L0_ffn_W0a, L0_ffn_b0a, L0_ffn_W0b, L0_ffn_b0b, L0_ffn_W1a, L0_ffn_b1a, L0_ffn_W1b, L0_ffn_b1b, L1_attn_Wq, L1_attn_bq, L1_attn_Wk, L1_attn_bk, L1_attn_Wv, L1_attn_bv, L1_attn_Wo, L1_attn_bo, L1_ffn_w1, L1_ffn_b1, L1_ffn_w2, L1_ffn_b2):

    def _L0_attn_ref(x, w_qkv, w_proj, b_proj):
        import jax, jax.numpy as jnp
        import numpy as np
        EPS = 1e-15
        HEAD_DIM = 32
        PAD_VAL = 1.0
        B, N, C = x.shape
        d = HEAD_DIM
        h = C // d
        qkv = (x @ w_qkv.T).reshape(B, N, 3, C)
        q, k, v = (qkv[:, :, 0], qkv[:, :, 1], qkv[:, :, 2])

        def to_heads(t):
            return t.reshape(B, N, h, d).transpose(0, 2, 3, 1)
        q = jax.nn.relu(to_heads(q))
        k = jax.nn.relu(to_heads(k))
        v = to_heads(v)
        v_pad = jnp.pad(v, ((0, 0), (0, 0), (0, 1), (0, 0)), constant_values=PAD_VAL)
        vk = jnp.einsum('bhen,bhdn->bhed', v_pad, k)
        out = jnp.einsum('bhed,bhdn->bhen', vk, q)
        out = out[:, :, :-1] / (out[:, :, -1:] + EPS)
        out = out.reshape(B, C, N).transpose(0, 2, 1)
        return out @ w_proj.T + b_proj

    def _L0_ffn_ref(x, Wg, W0a, b0a, W0b, b0b, W1a, b1a, W1b, b1b):
        import jax, jax.numpy as jnp
        import numpy as np
        H = 256
        scores = jax.nn.softmax(jnp.einsum('bsh,eh->bse', x, Wg), axis=-1)
        top_expert = jnp.argmax(scores, axis=-1)
        h0 = jax.nn.gelu(jnp.einsum('bsh,fh->bsf', x, W0a) + b0a, approximate=False)
        out0 = jnp.einsum('bsf,hf->bsh', h0, W0b) + b0b
        h1 = jax.nn.relu(jnp.einsum('bsh,fh->bsf', x, W1a) + b1a)
        out1 = jnp.einsum('bsf,hf->bsh', h1, W1b) + b1b
        mask0 = (top_expert == 0).astype(x.dtype)[..., None]
        return out0 * mask0 + out1 * (1.0 - mask0)

    def _L1_attn_ref(x, Wq, bq, Wk, bk, Wv, bv, Wo, bo):
        import jax, jax.numpy as jnp
        import numpy as np
        import math
        N_Q = 128
        N_K = 128
        N_V = 128
        D_MODEL = 256
        N_HEADS = 16
        B, T = (8, 512)
        Bx, Tx, _ = x.shape
        q = (x @ Wq + bq).reshape(Bx, Tx, N_Q, N_HEADS)
        k = (x @ Wk + bk).reshape(Bx, Tx, N_K, N_HEADS)
        v = (x @ Wv + bv).reshape(Bx, Tx, N_V, N_HEADS)
        q = jnp.transpose(q, (0, 3, 2, 1))
        k = jnp.transpose(k, (0, 3, 1, 2))
        v = jnp.transpose(v, (0, 3, 2, 1))
        att = jax.nn.softmax(q @ k / math.sqrt(N_K), axis=-1)
        y = att @ v
        y = jnp.transpose(y, (0, 2, 1, 3)).reshape(Bx, -1, N_V * N_HEADS)
        return y @ Wo + bo

    def _L1_ffn_ref(x, w1, b1, w2, b2):
        import jax, jax.numpy as jnp
        import numpy as np
        EPS = 1e-08

        def _bit_quant(w):
            scale = jnp.maximum(jnp.mean(jnp.abs(w)), EPS)
            w_ternary = jnp.clip(jnp.round(w / scale), -1.0, 1.0)
            return w + jax.lax.stop_gradient(w_ternary - w)
        w1q = _bit_quant(w1)
        w2q = _bit_quant(w2)
        h = jnp.einsum('bsd,fd->bsf', x, w1q) + b1
        h = jax.nn.gelu(h, approximate=False)
        return jnp.einsum('bsf,df->bsd', h, w2q) + b2
    x = L0_attn_x
    x = x + _L0_attn_ref(_layernorm(x, axis=-1), L0_attn_w_qkv, L0_attn_w_proj, L0_attn_b_proj)
    x = x + _L0_ffn_ref(_layernorm(x, axis=-1), L0_ffn_Wg, L0_ffn_W0a, L0_ffn_b0a, L0_ffn_W0b, L0_ffn_b0b, L0_ffn_W1a, L0_ffn_b1a, L0_ffn_W1b, L0_ffn_b1b)
    x = x + _L1_attn_ref(_layernorm(x, axis=-1), L1_attn_Wq, L1_attn_bq, L1_attn_Wk, L1_attn_bk, L1_attn_Wv, L1_attn_bv, L1_attn_Wo, L1_attn_bo)
    x = x + _L1_ffn_ref(_layernorm(x, axis=-1), L1_ffn_w1, L1_ffn_b1, L1_ffn_w2, L1_ffn_b2)
    return x

_drawn_inputs = setup_inputs


def setup_inputs(seed=0):
    import zlib

    import numpy as np

    out = dict(_drawn_inputs(seed))
    spreads = {'L1_attn_bq': (0.0, 0.1),
     'L1_attn_bk': (0.0, 0.1),
     'L1_attn_bv': (0.0, 0.533),
     'L1_attn_bo': (0.0, 0.1)}
    factors = {'L0_attn_b_proj': 3.268,
     'L0_ffn_b0a': 5.438,
     'L0_ffn_b1a': 4.548,
     'L1_ffn_b1': 39.981,
     'L1_ffn_b2': 64.0}
    for name, (base, spread) in spreads.items():
        noise = np.random.default_rng([zlib.crc32(name.encode()), seed]).standard_normal(out[name].shape)
        drawn = base * np.exp(spread * noise) if base else spread * noise
        out[name] = jnp.asarray(drawn.astype(out[name].dtype))
    for name, factor in factors.items():
        out[name] = (out[name] * factor).astype(out[name].dtype)
    return out
```

```python
from contextlib import ExitStack

import concourse.bass as bass
from concourse import mybir
from concourse.alu_op_type import AluOpType as ALU

ACT = mybir.ActivationFunctionType
AX = mybir.AxisListType
F32 = mybir.dt.float32
F32R = mybir.dt.float32r


P = 128
B, T, C = 2, 1024, 256
NT = B * T // P
CH = C // P
G = 512
NG = B * T // G
TPG = G // P
EPS_LN = 1e-5

H0, D0 = 8, 32
HPH = P // D0
VW = D0 + 1
EPS_A = 1e-15

H1, D1 = 16, 128
SCALE = float(D1) ** -0.5
TB = T // P
QH = 4
QUADS = H1 // QH
XW = C + 2

F0, F1 = 512, 1024
FT = 4

def transformer(nc, x_in, wqkv, wproj, bproj, wg, w0a, b0a, w0b, b0b, w1a, b1a, w1b, b1b,
                wq, wk, wv, wo, bq, bk, bqc, bvc, bo, f1, fb1, f2, fb2, ident_in, out):
    with ExitStack() as ctx:
        base = nc.sbuf_base
        top = [(base + 31) // 32 * 32]

        def place(name, shape, dt, at=None):
            size = 4
            for n in shape[1:]:
                size *= n
            where = top[0] if at is None else at[0]
            where = (where + 31) // 32 * 32
            t = nc.alloc_sbuf_tensor_at(name, shape, dt, offset=where)
            (top if at is None else at)[0] = where + size
            return t

        def sem(name):
            return ctx.enter_context(nc.semaphore(name))

        x = place("x", [P, NT, C], F32)
        base_x = top[0]
        xTh = place("xTh", [P, CH, B * T], F32R)
        xTl = place("xTl", [P, CH, B * T], F32R)
        top[0] = base_x + 2 * NT * XW * 4
        ident = place("ident", [P, P], F32)
        ones = place("ones", [P, P], F32R)
        onesf = place("onesf", [P, P], F32)
        mhalf = place("mhalf", [P, TPG], F32)
        stats = place("stats", [P, TPG, 6], F32)
        mv = place("mv", [P, TPG, 2], F32)
        vare = place("vare", [P, TPG], F32)
        rstd = place("rstd", [P, TPG], F32)
        b0as = place("b0as", [P, FT], F32)
        b1as = place("b1as", [P, FT], F32)
        fb1s = place("fb1s", [P, F1 // P], F32)
        rows1 = place("rows1", [P, 2, C], F32)
        xn = place("xn", [P, 2 * TPG, C], F32, [nc.sbuf_usable_end // 32 * 32 - 2 * TPG * C * 4])
        end = nc.sbuf_usable_end // 32 * 32 - 2 * TPG * C * 4

        a0 = [top[0]]
        raw_cols = {"qkv": 2 * 768, "proj": 2 * C, "w0a": 2 * F0, "w1a": 2 * F0, "w0b": 4 * C, "w1b": 4 * C}
        wshape = {"qkv": [P, 2, 768], "proj": [P, 2, C], "w0a": [P, 2, F0], "w1a": [P, 2, F0],
                  "w0b": [P, 4, C], "w1b": [P, 4, C]}
        wh0 = {k: place(f"{k}_h", s, F32R, a0) for k, s in wshape.items()}
        wl0 = {k: place(f"{k}_l", s, F32R, a0) for k, s in wshape.items()}
        wgs = place("wgs", [P, CH, 2], F32, a0)
        wgh = place("wgh", [P, CH, 2], F32R, a0)
        wgl = place("wgl", [P, CH, 2], F32R, a0)
        mask = place("mask", [P, NT, 2], F32, a0)
        rows0 = place("rows0", [P, 3, C], F32, a0)
        phase = [a0[0]]
        raw0 = {k: place(f"{k}_raw", s, F32, phase) for k, s in wshape.items()}
        Kh = place("Kh", [P, 2, C], F32R, phase)
        Kl = place("Kl", [P, 2, C], F32R, phase)
        Vh0 = place("Vh0", [P, 2, H0, VW], F32R, phase)
        Vl0 = place("Vl0", [P, 2, H0, VW], F32R, phase)
        Qh = place("Qh", [P, CH, T], F32R, phase)
        Ql = place("Ql", [P, CH, T], F32R, phase)
        BD = place("BD", [P, CH, 2, P], F32, phase)
        BDh = place("BDh", [P, CH, 2, P], F32R, phase)
        BDl = place("BDl", [P, CH, 2, P], F32R, phase)
        den = place("den", [P, G], F32, phase)
        rden = place("rden", [P, G], F32, phase)
        o32 = place("o32", [P, 2, G], F32, phase)
        Oh = place("Oh", [P, CH, T], F32R, phase)
        Ol = place("Ol", [P, CH, T], F32R, phase)
        assert phase[0] <= end, phase[0] - end

        def ffn_buffers(tag, at):
            return (place(f"hf{tag}", [P, 2, G], F32, at),
                    [place(f"hh{tag}{e}", [P, FT, G], F32R, at) for e in range(2)],
                    [place(f"hl{tag}{e}", [P, FT, G], F32R, at) for e in range(2)])

        ff0 = ffn_buffers("0", [a0[0]])
        b1_ = [top[0]]
        f1raw = place("f1raw", [P, CH, F1], F32, b1_)
        f2raw = place("f2raw", [P, F1 // P, C], F32, b1_)
        f1t = place("f1t", [P, CH, F1], F32R, b1_)
        f2t = place("f2t", [P, F1 // P, C], F32R, b1_)
        neg = place("neg", [P, CH, F1], F32, b1_)
        asum = place("asum", [P, 2], F32, b1_)
        thr = place("thr", [P, 2], F32, b1_)
        nthr = place("nthr", [P, 2], F32, b1_)
        ff1 = ffn_buffers("1", b1_)

        c0 = [base_x]
        xrh = place("xrh", [P, NT, XW], F32R, c0)
        xrl = place("xrl", [P, NT, XW], F32R, c0)
        c0 = [max(top[0], c0[0])]
        Gh = place("Gh", [P, B, CH, C], F32R, c0)
        Gl = place("Gl", [P, B, CH, C], F32R, c0)
        Rh = place("Rh", [P, CH, 2, B, C], F32R, c0)
        Rl = place("Rl", [P, CH, 2, B, C], F32R, c0)
        sx = place("sx", [P, CH, B], F32, c0)
        sxh = place("sxh", [P, CH, B], F32R, c0)
        sxl = place("sxl", [P, CH, B], F32R, c0)
        wosum = place("wosum", [P, 2, C], F32, c0)
        bqr = place("bqr", [P, H1 * D1], F32, c0)
        bkr = place("bkr", [P, H1 * D1], F32, c0)
        bqcs = place("bqcs", [P, H1], F32, c0)
        bvcs = place("bvcs", [P, H1], F32, c0)
        raw = {k: place(f"raw{k}", [P, CH, 512], F32, c0) for k in "qkv"}
        wh = {k: place(f"wh{k}", [P, CH, 512], F32R, c0) for k in "qkv"}
        wl = {k: place(f"wl{k}", [P, CH, 512], F32R, c0) for k in "qkv"}
        Bf = place("Bf", [P, 2, 512], F32, c0)
        Bh = place("Bh", [P, B, CH, 512], F32R, c0)
        Bl = place("Bl", [P, B, CH, 512], F32R, c0)
        ac = place("ac", [P, QH, B], F32, c0)
        d0 = [c0[0]]
        woraw = place("woraw", [P, TB, 2 * C], F32, c0)
        woh = place("woh", [P, TB, 2 * C], F32R, c0)
        wol = place("wol", [P, TB, 2 * C], F32R, c0)
        S = place("S", [P, B, QH, D1], F32, d0)
        mx = place("mx", [P, B, QH], F32, d0)
        nmx = place("nmx", [P, B, QH], F32, d0)
        ssum = place("ssum", [P, B, QH], F32, d0)
        rs = place("rs", [P, B, QH], F32, d0)
        PTh = place("PTh", [P, B, QH, D1], F32R, d0)
        PTl = place("PTl", [P, B, QH, D1], F32R, d0)
        Zf = place("Zf", [P, 2, 2 * C], F32, d0)
        Zh = place("Zh", [P, QH, B, C], F32R, d0)
        Zl = place("Zl", [P, QH, B, C], F32R, d0)
        assert max(c0[0], d0[0], b1_[0]) <= end, (c0[0], d0[0], b1_[0], end)

        ps = ctx.enter_context(nc.psum_tensor("ps", [P, 8, 512], F32))
        LNB = 6

        x_in_s = [sem(f"x_loaded{g}") for g in range(NG)]
        cst_in = sem("constants_loaded")
        w0_in = {k: sem(f"{k}_loaded") for k in wshape}
        w0_hi = sem("weights0_hi")
        w0_lo = sem("weights0_lo")
        ones_set = sem("ones_set")
        dve_chain = sem("dve_chain")
        var_ready, rstd_ready = sem("var_ready"), sem("rstd_ready")
        xn_ready = sem("xn_ready")
        xT_filled, xT_hi, xT_lo = sem("xT_filled"), sem("xT_hi"), sem("xT_lo")
        x_biased = sem("x_biased")
        kv_filled, kv_hi, kv_lo, kv_used = sem("kv_filled"), sem("kv_hi"), sem("kv_lo"), sem("kv_used")
        q_filled, q_hi, q_lo = sem("q_filled"), sem("q_hi"), sem("q_lo")
        bd_done, bd_hi, bd_lo = sem("bd_done"), sem("bd_hi"), sem("bd_lo")
        nd_filled, o_norm, o_hi, o_lo = sem("nd_filled"), sem("o_norm"), sem("o_hi"), sem("o_lo")
        pr_filled, x1_added = sem("proj_filled"), sem("x1_added")
        gate_filled, mask_ready = sem("gate_filled"), sem("mask_ready")
        h_filled = [sem(f"h_filled{s}") for s in range(2)]
        h_act = [sem(f"h_activated{s}") for s in range(2)]
        h_hi = [sem(f"h_hi{s}") for s in range(2)]
        h_lo = [sem(f"h_lo{s}") for s in range(2)]
        y_filled = [sem(f"y_filled{s}") for s in range(2)]
        y_added = [sem(f"y_added{s}") for s in range(2)]
        f_in, f_abs, f_sum, f_tern = sem("ffn_loaded"), sem("f_abs"), sem("f_sum"), sem("f_ternary")
        stored = sem("stored")
        wo_in, bias_in, wo_hi, wo_lo = sem("wo_loaded"), sem("biases_loaded"), sem("wo_hi"), sem("wo_lo")
        xr_hi, xr_lo, xr_one = sem("rows_hi"), sem("rows_lo"), sem("rows_ones")
        ws_filled, ws_read = sem("wosum_filled"), sem("wosum_read")
        gr_filled, gr_hi, gr_lo = sem("gram_filled"), sem("gram_hi"), sem("gram_lo")
        sx_ready, sx_hi, sx_lo = sem("sx_ready"), sem("sx_hi"), sem("sx_lo")
        raw_in = {k: sem(f"raw{k}_loaded") for k in "qkv"}
        w_hi = {k: sem(f"w{k}_hi") for k in "qkv"}
        w_lo = {k: sem(f"w{k}_lo") for k in "qkv"}
        b_filled, b_taken, b_hi, b_lo = sem("b_filled"), sem("b_taken"), sem("b_hi"), sem("b_lo")
        s_filled, s_ready, s_max, s_neg = sem("s_filled"), sem("s_ready"), sem("s_max"), sem("s_neg")
        e_ready, r_ready, p_ready = sem("exp_ready"), sem("rsum_ready"), sem("p_ready")
        t_filled, pt_hi, pt_lo = sem("t_filled"), sem("pt_hi"), sem("pt_lo")
        z_filled, z_ready, z_hi, z_lo = sem("z_filled"), sem("z_ready"), sem("z_hi"), sem("z_lo")
        o_filled, o_added = sem("o_filled"), sem("o_added")

        def wait(eng, s, v):
            if not isinstance(v, int) or v > 0:
                eng.wait_ge(s, v)

        def f32(ap):
            return ap.bitcast(F32)

        def turn(k, g, c):
            return CH * (NG * (k if k < 3 else 2) + g) + c

        def x_final(k, g):
            if k == 0:
                return x_in_s[g], 16
            if k == 1:
                return x1_added, 2 * (g + 1)
            if k == 2:
                return y_added[0], 4 * (g + 1)
            return o_added, B * QUADS

        FFN_ORDER = [("ln", 0)]
        for u in range(2 * NG):
            FFN_ORDER.append(("unit", u))
            if u % 2 == 0 and u // 2 + 1 < NG:
                FFN_ORDER.append(("ln", u // 2 + 1))
        FFN_ORDER.append(("unit", 2 * NG))

        block = ctx.enter_context(nc.Block())

        @block.sync
        def _(sp):
            sp.dma_start(ident[:], ident_in).then_inc(cst_in, 16)
            xv = x_in.rearrange("b (p t) c -> p b t c", p=P)
            for g in range(NG):
                sp.dma_start(x[:, g * TPG:(g + 1) * TPG, :], xv[:, g // 2, g % 2 * TPG:(g % 2 + 1) * TPG, :]).then_inc(x_in_s[g], 16)
                if g == 0:
                    sp.dma_start(raw0["qkv"][:], wqkv.rearrange("(c p) n -> p c n", p=P)).then_inc(w0_in["qkv"], 16)
            for dst, src in ((b0as, b0a), (b1as, b1a), (fb1s, fb1)):
                sp.dma_start(dst[:], src).then_inc(cst_in, 16)
            sp.dma_start(wgs[:], wg.rearrange("(c p) n -> p c n", p=P)).then_inc(cst_in, 16)
            for dst, src in ((rows0[:, 0, :], bproj), (rows0[:, 1, :], b0b), (rows0[:, 2, :], b1b),
                             (rows1[:, 0, :], bo), (rows1[:, 1, :], fb2)):
                sp.dma_start(dst, src.partition_broadcast(P)).then_inc(cst_in, 16)
            for k, src in (("proj", wproj), ("w0a", w0a), ("w0b", w0b), ("w1a", w1a), ("w1b", w1b)):
                sp.dma_start(raw0[k][:], src.rearrange("(c p) n -> p c n", p=P)).then_inc(w0_in[k], 16)

            sp.wait_ge(y_added[0], 4 * NG)
            sp.wait_ge(y_filled[0], 4 * NG)
            wov = wo.rearrange("(s p t) n -> p t s n", s=2, p=P)
            for s in range(2):
                sp.dma_start(woraw[:, :, s * C:(s + 1) * C], wov[:, :, s, :]).then_inc(wo_in, 16)
            sp.dma_start(bqcs[:], bqc).then_inc(bias_in, 16)
            sp.dma_start(bvcs[:], bvc).then_inc(bias_in, 16)
            sp.dma_start(bqr[:], bq.partition_broadcast(P)).then_inc(bias_in, 16)
            sp.dma_start(bkr[:], bk.partition_broadcast(P)).then_inc(bias_in, 16)
            for Q in range(QUADS):
                for k, w in (("q", wq), ("k", wk), ("v", wv)):
                    wait(sp, w_lo[k], Q)
                    sp.dma_start(raw[k][:], w.rearrange("(c p) n -> p c n", p=P)[:, :, Q * 512:(Q + 1) * 512])\
                      .then_inc(raw_in[k], 16)
            sp.wait_ge(o_added, B * QUADS)
            sp.dma_start(f1raw[:], f1.rearrange("(c p) n -> p c n", p=P)).then_inc(f_in, 16)
            sp.dma_start(f2raw[:], f2.rearrange("(c p) n -> p c n", p=P)).then_inc(f_in, 16)
            ov = out.rearrange("b (p t) c -> p b t c", p=P)
            for g in range(NG):
                sp.wait_ge(y_added[1], 4 * (g + 1))
                sp.dma_start(ov[:, g // 2, g % 2 * TPG:(g % 2 + 1) * TPG, :], x[:, g * TPG:(g + 1) * TPG, :])\
                  .then_inc(stored, 16)
            sp.wait_ge(stored, 16 * NG)

        @block.gpsimd
        def _(pool):
            nc.gpsimd.memset(onesf[:], 1.0).then_inc(ones_set, 1)
            nc.gpsimd.memset(mhalf[:], -0.5).then_inc(ones_set, 1)
            pool.wait_ge(ones_set, 2)

            def ln(k, g):
                pool.wait_ge(var_ready, NG * k + g + 1)
                nc.gpsimd.tensor_tensor(rstd[:], vare[:], mhalf[:], ALU.pow).then_inc(rstd_ready, 1)

            def unit(s, u, ff):
                hf, hh, hl = ff
                for f in range(FT):
                    i = FT * u + f
                    pool.wait_ge(h_hi[s], i + 1)
                    wait(pool, y_filled[s], 2 * (u - 1))
                    nc.gpsimd.tensor_tensor(hl[u % 2][:, f, :], hf[:, i % 2, :], f32(hh[u % 2][:, f, :]),
                                            ALU.subtract).then_inc(h_lo[s], 1)

            def ffn(s, ff):
                for what, n in FFN_ORDER:
                    if what == "ln":
                        ln(2 * s + 1, n)
                    elif n < 2 * NG:
                        unit(s, n, ff)

            for g in range(NG):
                ln(0, g)
            ffn(0, ff0)
            for g in range(NG):
                ln(2, g)

            def weight_lo(k, Q):
                if Q < QUADS:
                    pool.wait_ge(w_hi[k], Q + 1)
                    nc.gpsimd.tensor_tensor(wl[k][:], raw[k][:], f32(wh[k][:]), ALU.subtract).then_inc(w_lo[k], 1)

            def b_los(Q):
                for i in range(B * CH):
                    n = B * CH * Q + i
                    pool.wait_ge(b_hi, n + 1)
                    nc.gpsimd.tensor_tensor(Bl[:, i // CH, i % CH, :], Bf[:, n % 2, :], f32(Bh[:, i // CH, i % CH, :]),
                                            ALU.subtract).then_inc(b_lo, 1)

            for k in "qkv":
                weight_lo(k, 0)
            b_los(0)
            for Q in range(QUADS):
                weight_lo("q", Q + 1)
                weight_lo("k", Q + 1)
                if Q + 1 < QUADS:
                    b_los(Q + 1)
                for h in range(QH):
                    n = QH * Q + h
                    pool.wait_ge(z_hi, n + 1)
                    nc.gpsimd.tensor_tensor(Zl[:, h, :, :], Zf[:, n % 2, :].rearrange("p (b c) -> p b c", b=B),
                                            f32(Zh[:, h, :, :]), ALU.subtract).then_inc(z_lo, 1)
                weight_lo("v", Q + 1)
            ffn(1, ff1)

        @block.scalar
        def _(act):
            copy = nc.scalar.copy
            act.wait_ge(ones_set, 2)
            nc.scalar.activation(ones[:], onesf[:], ACT.Copy).then_inc(ones_set, 1)

            def round_weight(k):
                act.wait_ge(w0_in[k], 16)
                nc.scalar.activation(wh0[k][:], raw0[k][:], ACT.Copy).then_inc(w0_hi, 1)

            def ln(k, g):
                for c in range(CH):
                    i = turn(k, g, c)
                    act.wait_ge(xT_filled, i + 1)
                    nc.scalar.activation(xTh[:, c, g * G:(g + 1) * G], ps[:, LNB + c, :], ACT.Copy).then_inc(xT_hi, 1)

            def linear_attention(b):
                for t in range(T // P):
                    i = b * (T // P) + t
                    act.wait_ge(kv_filled, i + 1)
                    wait(act, kv_used, i - 1)
                    nc.scalar.activation(Kh[:, i % 2, :], ps[:, i % 2, 0:C], ACT.Relu)
                    nc.scalar.activation(Vh0[:, i % 2, :, 0:D0],
                                         ps[:, i % 2, C:2 * C].rearrange("p (h d) -> p h d", d=D0),
                                         ACT.Copy).then_inc(kv_hi, 1)
                for i in range(4):
                    act.wait_ge(q_filled, 4 * b + i + 1)
                    h, ch = i // 2, i % 2
                    nc.scalar.activation(Qh[:, h, ch * G:(ch + 1) * G], ps[:, 4 + i % 2, :], ACT.Relu).then_inc(q_hi, 1)
                act.wait_ge(bd_done, b + 1)
                nc.scalar.activation(BDh[:], BD[:], ACT.Copy).then_inc(bd_hi, 1)
                for i in range(4):
                    act.wait_ge(o_norm, 4 * b + i + 1)
                    ch, h = i // 2, i % 2
                    nc.scalar.activation(Oh[:, h, ch * G:(ch + 1) * G], o32[:, i % 2, :], ACT.Copy).then_inc(o_hi, 1)

            def unit(s, u, ff):
                hf, hh, hl = ff
                bias = (b0as, b1as)[u % 2] if s == 0 else fb1s
                func = ACT.Relu if s == 0 and u % 2 else ACT.Gelu
                for f in range(FT):
                    i = FT * u + f
                    col = f if s == 0 else FT * (u % 2) + f
                    act.wait_ge(h_filled[s], i + 1)
                    wait(act, h_lo[s], i - 1)
                    nc.scalar.activation(hf[:, i % 2, :], ps[:, i % 3, :], func,
                                         bias=bias[:, col:col + 1]).then_inc(h_act[s], 1)

            def ffn(s, ff):
                for what, n in FFN_ORDER:
                    if what == "ln":
                        ln(2 * s + 1, n)
                    elif n < 2 * NG:
                        unit(s, n, ff)

            round_weight("qkv")
            ln(0, 0)
            ln(0, 1)
            round_weight("proj")
            act.wait_ge(cst_in, 16 * 10)
            nc.scalar.activation(wgh[:], wgs[:], ACT.Copy).then_inc(w0_hi, 1)
            linear_attention(0)
            ln(0, 2)
            ln(0, 3)
            for k in ("w0a", "w0b", "w1a", "w1b"):
                round_weight(k)
            linear_attention(1)
            ffn(0, ff0)

            def weight_hi(k, Q):
                if Q == QUADS:
                    return
                act.wait_ge(raw_in[k], 16 * (Q + 1))
                used, n = {"q": (b_filled, (B * CH + 1) * Q), "k": (s_filled, B * Q), "v": (z_filled, QH * Q)}[k]
                wait(act, used, n)
                nc.scalar.activation(wh[k][:], raw[k][:], ACT.Copy).then_inc(w_hi[k], 1)

            for s in range(2):
                act.wait_ge(wo_in, 32)
                half = slice(s * TB // 2, (s + 1) * TB // 2)
                nc.scalar.activation(woh[:, half, :], woraw[:, half, :], ACT.Copy).then_inc(wo_hi, 1)
            for g in range(NG):
                act.wait_ge(xn_ready, TPG * (2 * NG + g + 1))
                nc.scalar.activation(xrh[:, g * TPG:(g + 1) * TPG, 0:C], xn[:, (g % 2) * TPG:(g % 2 + 1) * TPG, :],
                                     ACT.Copy).then_inc(xr_hi, 1)
                if g == 0:
                    act.wait_ge(ws_filled, 1)
                    nc.scalar.activation(wosum[:], ps[:, 7, :].rearrange("p (s c) -> p s c", s=2),
                                         ACT.Copy).then_inc(ws_read, 1)
                if g % 2:
                    b = g // 2
                    act.wait_ge(gr_filled, b + 1)
                    for c in range(CH):
                        nc.scalar.activation(Gh[:, b, c, :], ps[:, 4 * b + c, 0:C], ACT.Copy).then_inc(gr_hi, 1)
                        nc.scalar.activation(Rh[:, c, :, b, :], ps[:, 4 * b + 2 + c, :].rearrange("p (s c) -> p s c", s=2),
                                             ACT.Copy).then_inc(gr_hi, 1)
                if g == 1:
                    for k in "qkv":
                        weight_hi(k, 0)
            act.wait_ge(sx_ready, B * CH)
            nc.scalar.activation(sxh[:], sx[:], ACT.Copy).then_inc(sx_hi, 1)

            def b_his(Q):
                for i in range(B * CH):
                    n = B * CH * Q + i
                    act.wait_ge(b_taken, (B * CH + 1) * Q + i + 2)
                    wait(act, s_filled, B * Q)
                    nc.scalar.activation(Bh[:, i // CH, i % CH, :], Bf[:, n % 2, :], ACT.Copy).then_inc(b_hi, 1)

            def z_hi_(Q, h):
                n = QH * Q + h
                act.wait_ge(z_ready, n + 1)
                wait(act, o_filled, B * Q)
                nc.scalar.activation(Zh[:, h, :, :], Zf[:, n % 2, :].rearrange("p (b c) -> p b c", b=B),
                                     ACT.Copy).then_inc(z_hi, 1)

            b_his(0)
            for Q in range(QUADS):
                weight_hi("q", Q + 1)
                for b in range(B):
                    act.wait_ge(s_neg, B * Q + b + 1)
                    for h in range(QH):
                        nc.scalar.activation(S[:, b, h, :], S[:, b, h, :], ACT.Exp, bias=nmx[:, b, h:h + 1], scale=SCALE,
                                             accum_out=ssum[:, b, h:h + 1]).then_inc(e_ready, 1)
                weight_hi("k", Q + 1)
                if Q + 1 < QUADS:
                    b_his(Q + 1)
                z_hi_(Q, 0)
                z_hi_(Q, 1)
                for b in range(B):
                    act.wait_ge(t_filled, B * Q + b + 1)
                    wait(act, o_filled, B * (Q - 1) + b + 1)
                    nc.scalar.activation(PTh[:, b, :, :], ps[:, 6 + b, :].rearrange("p (h q) -> p h q", h=QH),
                                         ACT.Copy).then_inc(pt_hi, 1)
                z_hi_(Q, 2)
                z_hi_(Q, 3)
                weight_hi("v", Q + 1)

            ffn(1, ff1)

        @block.vector
        def _(dve):
            chain = [0]

            def link(ins):
                chain[0] += 1
                ins.then_inc(dve_chain, 1)
                dve.wait_ge(dve_chain, chain[0])

            def low_weight(k, n):
                dve.wait_ge(w0_hi, n)
                nc.vector.tensor_tensor(wl0[k][:], raw0[k][:], f32(wh0[k][:]), ALU.subtract).then_inc(w0_lo, 1)

            def ln(k, g):
                if k < 4:
                    s, v = x_final(k, g)
                    dve.wait_ge(s, v)
                for i in range(TPG):
                    last = nc.vector.bn_stats(stats[:, i, :], x[:, g * TPG + i, :])
                link(last)
                for i in range(TPG):
                    last = nc.vector.bn_aggr(mv[:, i, :], stats[:, i, :])
                link(last)
                nc.vector.tensor_scalar(vare[:], mv[:, :, 1], EPS_LN, None, ALU.add).then_inc(var_ready, 1)
                dve.wait_ge(rstd_ready, NG * k + g + 1)
                if k == 2:
                    wait(dve, xr_lo, g - 1)
                else:
                    wait(dve, xT_filled, turn(k, g - 1, 0) if g or k != 3 else CH * NG * 2)
                for i in range(TPG):
                    r = (g % 2) * TPG + i
                    nc.vector.tensor_scalar(xn[:, r, :], x[:, g * TPG + i, :], mv[:, i, 0:1], rstd[:, i:i + 1],
                                            ALU.subtract, ALU.mult).then_inc(xn_ready, 1)
                if k != 1:
                    if k == 0 and g == 0:
                        dve.wait_ge(cst_in, 16 * 10)
                    row = {0: rows0[:, 0:1, :], 2: rows1[:, 0:1, :], 3: rows1[:, 1:2, :]}[k]
                    xs = x[:, g * TPG:(g + 1) * TPG, :]
                    dve.wait_ge(xn_ready, TPG * (NG * k + g + 1))
                    link(nc.vector.tensor_tensor(xs, xs, row.to_broadcast([P, TPG, C]), ALU.add))
                if k == 2:
                    tiles = slice(g * TPG, (g + 1) * TPG)
                    dve.wait_ge(xr_hi, g + 1)
                    nc.vector.tensor_tensor(xrl[:, tiles, 0:C], xn[:, (g % 2) * TPG:(g % 2 + 1) * TPG, :],
                                            f32(xrh[:, tiles, 0:C]), ALU.subtract).then_inc(xr_lo, 1)
                    return
                for c in range(CH):
                    i = turn(k, g, c)
                    dve.wait_ge(xT_hi, i + 1)
                    span = slice(g * G, (g + 1) * G)
                    nc.vector.tensor_tensor(xTl[:, c, span], ps[:, LNB + c, :], f32(xTh[:, c, span]),
                                            ALU.subtract).then_inc(xT_lo, 1)

            def linear_attention(b):
                if b == 0:
                    dve.wait_ge(ones_set, 2)
                    for s in range(2):
                        link(nc.vector.tensor_copy(Vh0[:, s, :, D0:VW], onesf[:, 0:H0].rearrange("p (h a) -> p h a", a=1)))
                        link(nc.vector.tensor_scalar(Vl0[:, s, :, D0:VW], onesf[:, 0:H0].rearrange("p (h a) -> p h a", a=1),
                                                     0.0, None, ALU.mult))
                    link(nc.vector.memset(BD[:], 0.0))
                for t in range(T // P):
                    i = b * (T // P) + t
                    dve.wait_ge(kv_hi, i + 1)
                    wait(dve, kv_used, i - 1)
                    nc.vector.scalar_tensor_tensor(Kl[:, i % 2, :], ps[:, i % 2, 0:C], 0.0, f32(Kh[:, i % 2, :]),
                                                   ALU.max, ALU.subtract)
                    nc.vector.tensor_tensor(Vl0[:, i % 2, :, 0:D0],
                                            ps[:, i % 2, C:2 * C].rearrange("p (h d) -> p h d", d=D0),
                                            f32(Vh0[:, i % 2, :, 0:D0]), ALU.subtract).then_inc(kv_lo, 1)
                for i in range(4):
                    dve.wait_ge(q_hi, 4 * b + i + 1)
                    h, ch = i // 2, i % 2
                    nc.vector.scalar_tensor_tensor(Ql[:, h, ch * G:(ch + 1) * G], ps[:, 4 + i % 2, :], 0.0,
                                                   f32(Qh[:, h, ch * G:(ch + 1) * G]),
                                                   ALU.max, ALU.subtract).then_inc(q_lo, 1)
                dve.wait_ge(kv_used, 8 * (b + 1))
                wait(dve, bd_lo, b)
                for h in range(CH):
                    for r in range(HPH):
                        rs = slice(D0 * r, D0 * r + D0)
                        nc.vector.tensor_copy(BD[rs, h, 0, rs], ps[rs, 2 + h, VW * r:VW * r + D0])
                        last = nc.vector.tensor_copy(BD[rs, h, 1, rs],
                                                     ps[rs, 2 + h, VW * r + D0:VW * r + VW].to_broadcast([D0, D0]))
                last.then_inc(bd_done, 1)
                dve.wait_ge(bd_hi, b + 1)
                nc.vector.tensor_tensor(BDl[:], BD[:], f32(BDh[:]), ALU.subtract).then_inc(bd_lo, 1)
                for i in range(4):
                    ch, h = i // 2, i % 2
                    dve.wait_ge(nd_filled, 4 * b + i + 1)
                    nb = 0 if i % 2 == 0 else 4
                    link(nc.vector.tensor_scalar(den[:], ps[:, nb + 1, :], EPS_A, None, ALU.add))
                    link(nc.vector.reciprocal(rden[:], den[:]))
                    nc.vector.tensor_tensor(o32[:, i % 2, :], ps[:, nb, :], rden[:], ALU.mult).then_inc(o_norm, 1)
                    dve.wait_ge(o_hi, 4 * b + i + 1)
                    nc.vector.tensor_tensor(Ol[:, h, ch * G:(ch + 1) * G], o32[:, i % 2, :],
                                            f32(Oh[:, h, ch * G:(ch + 1) * G]), ALU.subtract).then_inc(o_lo, 1)
                for i in range(4):
                    t = 8 * b + 2 * i
                    dve.wait_ge(pr_filled, 4 * b + i + 1)
                    nc.vector.tensor_tensor(x[:, t:t + 2, :], ps[:, 2 + i % 2, :].rearrange("p (t c) -> p t c", t=2),
                                            x[:, t:t + 2, :], ALU.add).then_inc(x1_added, 1)

            def gate(g):
                dve.wait_ge(gate_filled, g + 1)
                lg = ps[:, 3, 0:2 * TPG].rearrange("p (t e) -> p t e", e=2)
                t0 = g * TPG
                link(nc.vector.tensor_copy(mask[:, t0:t0 + TPG, :], lg))
                l0, l1 = mask[:, t0:t0 + TPG, 0], mask[:, t0:t0 + TPG, 1]
                link(nc.vector.tensor_tensor(l0, l0, l1, ALU.is_ge))
                nc.vector.tensor_scalar(l1, l0, -1.0, 1.0, ALU.mult, ALU.add).then_inc(mask_ready, 1)
                dve.wait_ge(mask_ready, g + 1)
                for e in range(2):
                    for t in range(t0, t0 + TPG):
                        last = nc.vector.scalar_tensor_tensor(x[:, t, :], rows0[:, 1 + e, :], mask[:, t, e:e + 1],
                                                              x[:, t, :], ALU.mult, ALU.add)
                    link(last)

            def unit_out(s, u):
                g, e = u // 2, u % 2
                wait(dve, y_added[s], 2 * u)
                for q in range(2):
                    t = g * TPG + 2 * q
                    dve.wait_ge(y_filled[s], 2 * u + q + 1)
                    if s == 0:
                        nc.vector.scalar_tensor_tensor(x[:, t, :], ps[:, 4 + q, 0:C], mask[:, t, e:e + 1], x[:, t, :],
                                                       ALU.mult, ALU.add)
                        nc.vector.scalar_tensor_tensor(x[:, t + 1, :], ps[:, 4 + q, C:2 * C], mask[:, t + 1, e:e + 1],
                                                       x[:, t + 1, :], ALU.mult, ALU.add).then_inc(y_added[s], 1)
                    else:
                        nc.vector.tensor_tensor(x[:, t:t + 2, :], ps[:, 4 + q, :].rearrange("p (t c) -> p t c", t=2),
                                                x[:, t:t + 2, :], ALU.add).then_inc(y_added[s], 1)

            def unit(s, u, ff):
                hf, hh, hl = ff
                for f in range(FT):
                    i = FT * u + f
                    if u < 2 * NG:
                        dve.wait_ge(h_act[s], i + 1)
                        wait(dve, y_filled[s], 2 * (u - 1))
                        nc.vector.tensor_copy(hh[u % 2][:, f, :], hf[:, i % 2, :]).then_inc(h_hi[s], 1)
                if u:
                    unit_out(s, u - 1)

            def ffn(s, ff):
                for what, n in FFN_ORDER:
                    if what == "ln":
                        ln(2 * s + 1, n)
                        if s == 0:
                            gate(n)
                    else:
                        unit(s, n, ff)

            ln(0, 0)
            ln(0, 1)
            low_weight("qkv", 1)
            low_weight("proj", 2)
            dve.wait_ge(w0_hi, 3)
            nc.vector.tensor_tensor(wgl[:], wgs[:], f32(wgh[:]), ALU.subtract).then_inc(w0_lo, 1)
            linear_attention(0)
            ln(0, 2)
            ln(0, 3)
            for i, k in enumerate(("w0a", "w0b", "w1a", "w1b")):
                low_weight(k, 4 + i)
            linear_attention(1)
            ffn(0, ff0)
            link(nc.vector.tensor_copy(xrh[:, :, C:C + 1], onesf[:, 0:NT].rearrange("p (t a) -> p t a", a=1)))
            link(nc.vector.tensor_scalar(xrh[:, :, C + 1:XW], onesf[:, 0:NT].rearrange("p (t a) -> p t a", a=1), 0.0,
                                         None, ALU.mult))
            link(nc.vector.tensor_scalar(xrl[:, :, C:XW], onesf[:, 0:2 * NT].rearrange("p (t a) -> p t a", a=2), 0.0,
                                         None, ALU.mult))
            for g in range(NG):
                ln(2, g)
                if g == 0:
                    for s in range(2):
                        dve.wait_ge(wo_hi, s + 1)
                        half = slice(s * TB // 2, (s + 1) * TB // 2)
                        nc.vector.tensor_tensor(wol[:, half, :], woraw[:, half, :], f32(woh[:, half, :]),
                                                ALU.subtract).then_inc(wo_lo, 1)

            for b in range(B):
                dve.wait_ge(gr_filled, b + 1)
                for c in range(CH):
                    i = 2 * (CH * b + c)
                    dve.wait_ge(gr_hi, i + 1)
                    nc.vector.tensor_tensor(Gl[:, b, c, :], ps[:, 4 * b + c, 0:C], f32(Gh[:, b, c, :]),
                                            ALU.subtract).then_inc(gr_lo, 1)
                    nc.vector.tensor_copy(sx[:, c, b:b + 1], ps[:, 4 * b + c, C:C + 1]).then_inc(sx_ready, 1)
                    dve.wait_ge(gr_hi, i + 2)
                    nc.vector.tensor_tensor(Rl[:, c, :, b, :], ps[:, 4 * b + 2 + c, :].rearrange("p (s c) -> p s c", s=2),
                                            f32(Rh[:, c, :, b, :]), ALU.subtract).then_inc(gr_lo, 1)
            dve.wait_ge(sx_hi, 1)
            nc.vector.tensor_tensor(sxl[:], sx[:], f32(sxh[:]), ALU.subtract).then_inc(sx_lo, 1)
            dve.wait_ge(bias_in, 64)
            dve.wait_ge(sx_ready, B * CH)

            def sums_and_b(Q, part):
                n0 = (B * CH + 1) * Q
                if part == 0:
                    dve.wait_ge(b_filled, n0 + 1)
                    wait(dve, s_ready, B * Q)
                    nc.vector.scalar_tensor_tensor(
                        ac[:], bqcs[:, Q * QH:(Q + 1) * QH].rearrange("p (h a) -> p h a", a=1).to_broadcast([P, QH, B]),
                        float(T), ps[:, n0 % 2, 0:QH * B].rearrange("p (h b) -> p h b", b=B),
                        ALU.mult, ALU.add).then_inc(b_taken, 1)
                for i in range(2 * part, 2 * part + 2):
                    n = B * CH * Q + i
                    dve.wait_ge(b_filled, n0 + i + 2)
                    wait(dve, b_lo, n - 1)
                    nc.vector.scalar_tensor_tensor(Bf[:, n % 2, :], bqr[:, Q * 512:(Q + 1) * 512],
                                                   sx[:, i % CH, i // CH:i // CH + 1], ps[:, (n0 + i + 1) % 2, :],
                                                   ALU.mult, ALU.add).then_inc(b_taken, 1)

            def score_rows(Q, b):
                n = B * Q + b
                dve.wait_ge(s_filled, n + 1)
                dve.wait_ge(b_taken, (B * CH + 1) * Q + 1)
                wait(dve, t_filled, n - 1)
                for h in range(QH):
                    cols = slice((Q * QH + h) * D1, (Q * QH + h + 1) * D1)
                    last = nc.vector.scalar_tensor_tensor(S[:, b, h, :], bkr[:, cols], ac[:, h, b:b + 1],
                                                          ps[:, 2 + b, h * D1:(h + 1) * D1], ALU.mult, ALU.add)
                last.then_inc(s_ready, 1)
                dve.wait_ge(s_ready, n + 1)
                nc.vector.reduce_max(mx[:, b, :], S[:, b, :, :], AX.X).then_inc(s_max, 1)
                dve.wait_ge(s_max, n + 1)
                nc.vector.tensor_scalar(nmx[:, b, :], mx[:, b, :], -SCALE, None, ALU.mult).then_inc(s_neg, 1)

            def probabilities(Q, b):
                n = B * Q + b
                dve.wait_ge(e_ready, QH * (n + 1))
                nc.vector.reciprocal(rs[:, b, :], ssum[:, b, :]).then_inc(r_ready, 1)
                dve.wait_ge(r_ready, n + 1)
                nc.vector.tensor_tensor(S[:, b, :, :], S[:, b, :, :],
                                        rs[:, b, :].rearrange("p (h a) -> p h a", a=1).to_broadcast([P, QH, D1]),
                                        ALU.mult).then_inc(p_ready, 1)

            def value_rows(Q, h):
                n = QH * Q + h
                dve.wait_ge(z_filled, n + 1)
                wait(dve, z_lo, n - 1)
                nc.vector.scalar_tensor_tensor(Zf[:, n % 2, :].rearrange("p (b c) -> p b c", b=B),
                                               wosum[:, h % 2:h % 2 + 1, :].to_broadcast([P, B, C]), bvcs[:, n:n + 1],
                                               ps[:, 4 + n % 2, :].rearrange("p (b c) -> p b c", b=B),
                                               ALU.mult, ALU.add).then_inc(z_ready, 1)

            sums_and_b(0, 0)
            sums_and_b(0, 1)
            dve.wait_ge(ws_read, 1)
            for Q in range(QUADS):
                for b in range(B):
                    score_rows(Q, b)
                for b in range(B):
                    if Q + 1 < QUADS:
                        sums_and_b(Q + 1, b)
                    probabilities(Q, b)
                value_rows(Q, 0)
                value_rows(Q, 1)
                for b in range(B):
                    n = B * Q + b
                    dve.wait_ge(pt_hi, n + 1)
                    nc.vector.tensor_tensor(PTl[:, b, :, :], ps[:, 6 + b, :].rearrange("p (h q) -> p h q", h=QH),
                                            f32(PTh[:, b, :, :]), ALU.subtract).then_inc(pt_lo, 1)
                value_rows(Q, 2)
                value_rows(Q, 3)
                for b in range(B):
                    t = TB * b + 2 * Q
                    dve.wait_ge(o_filled, B * Q + b + 1)
                    nc.vector.tensor_tensor(x[:, t:t + 2, :], ps[:, 6 + b, :].rearrange("p (t c) -> p t c", t=2),
                                            x[:, t:t + 2, :], ALU.add).then_inc(o_added, 1)

            dve.wait_ge(f_in, 32)
            for i, r in enumerate((f1raw, f2raw)):
                r2 = r[:].rearrange("p a b -> p (a b)")
                link(nc.vector.scalar_tensor_tensor(neg[:].rearrange("p a b -> p (a b)"), r2, -1.0, r2, ALU.mult, ALU.max))
                nc.vector.reduce_sum(asum[:, i:i + 1], neg[:].rearrange("p a b -> p (a b)"), AX.X).then_inc(f_abs, 1)
                dve.wait_ge(f_abs, i + 1)
            dve.wait_ge(f_sum, 1)
            link(nc.vector.tensor_scalar(thr[:], ps[:, 3, 0:2], 1.0 / (C * F1), 1e-8, ALU.mult, ALU.max))
            link(nc.vector.tensor_scalar(thr[:], thr[:], 0.5, None, ALU.mult))
            link(nc.vector.tensor_scalar(nthr[:], thr[:], -1.0, None, ALU.mult))
            for i, (r, t) in enumerate(((f1raw, f1t), (f2raw, f2t))):
                r2, t2 = r[:].rearrange("p a b -> p (a b)"), t[:].rearrange("p a b -> p (a b)")
                n2 = neg[:].rearrange("p a b -> p (a b)")
                link(nc.vector.tensor_scalar(n2, r2, nthr[:, i:i + 1], None, ALU.is_lt))
                last = nc.vector.scalar_tensor_tensor(t2, r2, thr[:, i:i + 1], n2, ALU.is_gt, ALU.subtract)
                last.then_inc(f_tern, 1)
                dve.wait_ge(f_tern, i + 1)
            ffn(1, ff1)

        @block.tensor
        def _(pe):
            mm = nc.tensor.matmul

            def product(dst, terms):
                for i, (a, b) in enumerate(terms):
                    last = mm(dst, a, b, start=(i == 0), stop=(i == len(terms) - 1))
                return last

            def three(ah, al, bh, bl):
                return [(ah, bh), (ah, bl), (al, bh)]

            def ln(k, g):
                for c in range(CH):
                    i = turn(k, g, c)
                    if c == 0:
                        pe.wait_ge(xn_ready, TPG * (NG * k + g + 1))
                    wait(pe, xT_lo, i - 1)
                    for t in range(TPG):
                        last = nc.tensor.transpose(ps[:, LNB + c, t * P:(t + 1) * P],
                                                   xn[:, (g % 2) * TPG + t, c * P:(c + 1) * P], ident[:])
                    last.then_inc(xT_filled, 1)

            def x_tile(t):
                s = slice(t * P, (t + 1) * P)
                return [(xTh[:, c, s], xTl[:, c, s]) for c in range(CH)]

            def linear_attention(b):
                wh_, wl_ = wh0["qkv"], wl0["qkv"]

                def kv_products(i):
                    pe.wait_ge(kv_lo, i + 1)
                    t = i % 8
                    for h in range(CH):
                        ks = slice(h * P, (h + 1) * P)
                        vs = slice(h * HPH, (h + 1) * HPH)
                        terms = three(Kh[:, i % 2, ks], Kl[:, i % 2, ks], Vh0[:, i % 2, vs, :], Vl0[:, i % 2, vs, :])
                        for n, (a, v) in enumerate(terms):
                            last = mm(ps[:, 2 + h, 0:HPH * VW], a, v.rearrange("p h d -> p (h d)"),
                                      start=(t == 0 and n == 0), stop=(t == 7 and n == 2))
                    last.then_inc(kv_used, 1)

                for t in range(8):
                    i = 8 * b + t
                    if t == 0 and b:
                        pe.wait_ge(o_norm, 4 * b)
                    wait(pe, kv_lo, i - 1)
                    terms = []
                    for c, (xh_, xl_) in enumerate(x_tile(i)):
                        terms += three(xh_, xl_, wh_[:, c, C:3 * C], wl_[:, c, C:3 * C])
                    product(ps[:, i % 2, :], terms).then_inc(kv_filled, 1)
                    if t:
                        if t == 1 and b:
                            pe.wait_ge(x1_added, 4 * b)
                        kv_products(i - 1)
                for i in range(4):
                    h, ch = i // 2, i % 2
                    wait(pe, q_lo, 4 * b + i - 1)
                    span = slice(b * T + ch * G, b * T + (ch + 1) * G)
                    terms = []
                    for c in range(CH):
                        ws = slice(h * P, (h + 1) * P)
                        terms += three(wh_[:, c, ws], wl_[:, c, ws], xTh[:, c, span], xTl[:, c, span])
                    product(ps[:, 4 + i % 2, :], terms).then_inc(q_filled, 1)
                    if i == 0:
                        kv_products(8 * b + 7)
                pe.wait_ge(bd_lo, b + 1)
                pe.wait_ge(q_lo, 4 * b + 4)
                for i in range(4):
                    ch, h = i // 2, i % 2
                    nb = 0 if i % 2 == 0 else 4
                    wait(pe, o_norm, 4 * b + i - 1)
                    span = slice(ch * G, (ch + 1) * G)
                    for d in range(2):
                        last = product(ps[:, nb + d, :], three(BDh[:, h, d, :], BDl[:, h, d, :],
                                                              Qh[:, h, span], Ql[:, h, span]))
                    last.then_inc(nd_filled, 1)
                for i in range(4):
                    pe.wait_ge(o_lo, 4 * b + (2 if i < 2 else 4))
                    wait(pe, x1_added, 4 * b + i - 1)
                    for tt in range(2):
                        s = slice((2 * i + tt) * P, (2 * i + tt + 1) * P)
                        terms = []
                        for h in range(CH):
                            terms += three(Oh[:, h, s], Ol[:, h, s], wh0["proj"][:, h, :], wl0["proj"][:, h, :])
                        last = product(ps[:, 2 + i % 2, tt * C:(tt + 1) * C], terms)
                    last.then_inc(pr_filled, 1)

            def gate(g):
                for t in range(TPG):
                    terms = []
                    for c, (xh_, xl_) in enumerate(x_tile(g * TPG + t)):
                        terms += three(xh_, xl_, wgh[:, c, :], wgl[:, c, :])
                    last = product(ps[:, 3, 2 * t:2 * t + 2], terms)
                last.then_inc(gate_filled, 1)

            def unit(s, u, ff):
                hf, hh, hl = ff
                g, e = u // 2, u % 2
                span = slice(g * G, (g + 1) * G)
                if u < 2 * NG:
                    pe.wait_ge(xT_lo, turn(2 * s + 1, g, 1) + 1)
                    if e == 0 and s == 0:
                        if g:
                            pe.wait_ge(mask_ready, g)
                        gate(g)
                    for f in range(FT):
                        i = FT * u + f
                        terms = []
                        wait(pe, h_act[s], i - 2)
                        for c in range(CH):
                            if s == 0:
                                k = ("w0a", "w1a")[e]
                                fs = slice(f * P, (f + 1) * P)
                                terms += three(wh0[k][:, c, fs], wl0[k][:, c, fs], xTh[:, c, span], xTl[:, c, span])
                            else:
                                fs = slice((FT * e + f) * P, (FT * e + f + 1) * P)
                                terms += [(f1t[:, c, fs], xTh[:, c, span]), (f1t[:, c, fs], xTl[:, c, span])]
                        product(ps[:, i % 3, :], terms).then_inc(h_filled[s], 1)
                if u:
                    v = u - 1
                    e = v % 2
                    pe.wait_ge(h_lo[s], FT * u)
                    for q in range(2):
                        wait(pe, y_added[s], 2 * (v - 1) + q + 1)
                        for tt in range(2):
                            ts = slice((2 * q + tt) * P, (2 * q + tt + 1) * P)
                            terms = []
                            for f in range(FT):
                                a, l = hh[e][:, f, ts], hl[e][:, f, ts]
                                if s == 0:
                                    k = ("w0b", "w1b")[e]
                                    terms += three(a, l, wh0[k][:, f, :], wl0[k][:, f, :])
                                else:
                                    w = f2t[:, FT * e + f, :]
                                    terms += [(a, w), (l, w)]
                            last = product(ps[:, 4 + q, tt * C:(tt + 1) * C], terms)
                        last.then_inc(y_filled[s], 1)

            def ffn(s, ff):
                for what, n in FFN_ORDER:
                    if what == "ln":
                        ln(2 * s + 1, n)
                    else:
                        unit(s, n, ff)

            pe.wait_ge(cst_in, 16 * 10)
            pe.wait_ge(ones_set, 3)
            ln(0, 0)
            ln(0, 1)
            pe.wait_ge(w0_lo, 3)
            pe.wait_ge(xT_lo, CH * 2)
            linear_attention(0)
            ln(0, 2)
            ln(0, 3)
            pe.wait_ge(xT_lo, CH * 4)
            linear_attention(1)
            pe.wait_ge(w0_lo, 7)
            pe.wait_ge(x1_added, 8)
            ffn(0, ff0)

            pe.wait_ge(y_added[0], 4 * NG)
            pe.wait_ge(xT_lo, CH * NG * 2)
            pe.wait_ge(wo_lo, 2)
            terms = []
            for t in range(TB):
                terms += [(ones[:], woh[:, t, :]), (ones[:], wol[:, t, :])]
            product(ps[:, 7, :], terms).then_inc(ws_filled, 1)
            for g in range(NG):
                b = g // 2
                pe.wait_ge(xr_lo, g + 1)
                if g == 2:
                    pe.wait_ge(ws_read, 1)
                for t in range(g * TPG, (g + 1) * TPG):
                    first, last_t = t % TB == 0, t % TB == TB - 1
                    for c in range(CH):
                        cs = slice(c * P, (c + 1) * P)
                        for bank, rh, rl, w in ((4 * b + c, xrh[:, t, :], xrl[:, t, :], XW),
                                                (4 * b + 2 + c, woh[:, t % TB, :], wol[:, t % TB, :], 2 * C)):
                            for n, (a, r) in enumerate(three(xrh[:, t, cs], xrl[:, t, cs], rh, rl)):
                                last = mm(ps[:, bank, 0:w], a, r, start=(first and n == 0), stop=(last_t and n == 2))
                if g % 2:
                    last.then_inc(gr_filled, 1)

            def sums_and_b(Q):
                n0 = (B * CH + 1) * Q
                pe.wait_ge(w_lo["q"], Q + 1)
                wait(pe, b_taken, n0 - 1)
                for h in range(QH):
                    terms = []
                    for c in range(CH):
                        ws = slice(h * D1, (h + 1) * D1)
                        terms += three(wh["q"][:, c, ws], wl["q"][:, c, ws], sxh[:, c, :], sxl[:, c, :])
                    last = product(ps[:, n0 % 2, h * B:(h + 1) * B], terms)
                last.then_inc(b_filled, 1)
                for i in range(B * CH):
                    b, co = i // CH, i % CH
                    cs = slice(co * P, (co + 1) * P)
                    wait(pe, b_taken, n0 + i)
                    terms = []
                    for c in range(CH):
                        terms += three(Gh[:, b, c, cs], Gl[:, b, c, cs], wh["q"][:, c, :], wl["q"][:, c, :])
                    product(ps[:, (n0 + i + 1) % 2, :], terms).then_inc(b_filled, 1)

            def score_rows(Q, b):
                n = B * Q + b
                pe.wait_ge(b_lo, B * CH * Q + CH * (b + 1))
                pe.wait_ge(w_lo["k"], Q + 1)
                wait(pe, s_ready, n - 1)
                for h in range(QH):
                    hs = slice(h * D1, (h + 1) * D1)
                    terms = []
                    for c in range(CH):
                        terms += three(Bh[:, b, c, hs], Bl[:, b, c, hs], wh["k"][:, c, hs], wl["k"][:, c, hs])
                    last = product(ps[:, 2 + b, hs], terms)
                last.then_inc(s_filled, 1)

            def value_rows(Q, h):
                n = QH * Q + h
                pe.wait_ge(w_lo["v"], Q + 1)
                wait(pe, z_ready, n - 1)
                hs = slice(h * D1, (h + 1) * D1)
                terms = []
                for c in range(CH):
                    terms += three(wh["v"][:, c, hs], wl["v"][:, c, hs], Rh[:, c, h % 2, :, :].rearrange("p b c -> p (b c)"),
                                   Rl[:, c, h % 2, :, :].rearrange("p b c -> p (b c)"))
                product(ps[:, 4 + n % 2, :], terms).then_inc(z_filled, 1)

            pe.wait_ge(gr_lo, 2 * B * CH)
            pe.wait_ge(sx_lo, 1)
            sums_and_b(0)
            for Q in range(QUADS):
                for b in range(B):
                    score_rows(Q, b)
                if Q + 1 < QUADS:
                    sums_and_b(Q + 1)
                value_rows(Q, 0)
                value_rows(Q, 1)
                for b in range(B):
                    n = B * Q + b
                    pe.wait_ge(p_ready, n + 1)
                    wait(pe, o_added, n - 1)
                    for h in range(QH):
                        last = nc.tensor.transpose(ps[:, 6 + b, h * D1:(h + 1) * D1], S[:, b, h, :], ident[:])
                    last.then_inc(t_filled, 1)
                value_rows(Q, 2)
                value_rows(Q, 3)
                pe.wait_ge(z_lo, QH * (Q + 1))
                for b in range(B):
                    pe.wait_ge(pt_lo, B * Q + b + 1)
                    for pair in range(2):
                        terms = []
                        for h in (2 * pair, 2 * pair + 1):
                            terms += three(PTh[:, b, h, :], PTl[:, b, h, :], Zh[:, h, b, :], Zl[:, h, b, :])
                        last = product(ps[:, 6 + b, pair * C:(pair + 1) * C], terms)
                    last.then_inc(o_filled, 1)

            pe.wait_ge(f_abs, 2)
            mm(ps[:, 3, 0:2], onesf[:], asum[:], start=True, stop=True).then_inc(f_sum, 1)
            pe.wait_ge(f_tern, 2)
            ffn(1, ff1)


def kernel(**inputs):
    import numpy as np
    import concourse.bacc as bacc
    from concourse.bass_utils import run_bass_kernel_spmd

    a = {k: np.asarray(v) for k, v in inputs.items()}
    heads = lambda w: w.reshape(C, D1, H1).transpose(0, 2, 1).reshape(C, H1 * D1)
    columns = lambda v: v.reshape(-1, P).T
    arrays = {
        "x": a["L0_attn_x"],
        "wqkv": a["L0_attn_w_qkv"].T, "wproj": a["L0_attn_w_proj"].T, "bproj": a["L0_attn_b_proj"],
        "wg": a["L0_ffn_Wg"].T,
        "w0a": a["L0_ffn_W0a"].T, "b0a": columns(a["L0_ffn_b0a"]), "w0b": a["L0_ffn_W0b"].T, "b0b": a["L0_ffn_b0b"],
        "w1a": a["L0_ffn_W1a"].T, "b1a": columns(a["L0_ffn_b1a"]), "w1b": a["L0_ffn_W1b"].T, "b1b": a["L0_ffn_b1b"],
        "wq": heads(a["L1_attn_Wq"]), "wk": heads(a["L1_attn_Wk"]), "wv": heads(a["L1_attn_Wv"]), "wo": a["L1_attn_Wo"],
        "bq": a["L1_attn_bq"].reshape(D1, H1).T.reshape(-1), "bk": a["L1_attn_bk"].reshape(D1, H1).T.reshape(-1),
        "bqc": a["L1_attn_bq"].reshape(D1, H1), "bvc": a["L1_attn_bv"].reshape(D1, H1), "bo": a["L1_attn_bo"],
        "f1": a["L1_ffn_w1"].T, "fb1": columns(a["L1_ffn_b1"]), "f2": a["L1_ffn_w2"].T, "fb2": a["L1_ffn_b2"],
        "ident": np.eye(P, dtype=np.float32),
    }
    nc = bacc.Bacc("TRN2", target_bir_lowering=False, num_devices=1)
    data, args = {}, []
    for name, v in arrays.items():
        data[f"in_{name}"] = np.ascontiguousarray(v)
        args.append(nc.dram_tensor(f"in_{name}", v.shape, mybir.dt.from_np(v.dtype), kind="ExternalInput").ap())
    args.append(nc.dram_tensor("out", (B, T, C), F32, kind="ExternalOutput").ap())
    transformer(nc, *args)
    return run_bass_kernel_spmd(nc, [data], core_ids=[0]).results[0]["out"]
```

```python
from contextlib import ExitStack

import concourse.bass as bass
from concourse import mybir
from concourse.alu_op_type import AluOpType as ALU

ACT = mybir.ActivationFunctionType
AX = mybir.AxisListType
F32 = mybir.dt.float32
F32R = mybir.dt.float32r


P = 128
B, T, C = 2, 1024, 256
TB = T // P
NT = B * TB
CH = C // P
G = 512
NG = B * T // G
TPG = G // P
EPS_LN = 1e-5

H0, D0 = 8, 32
HPH = P // D0
VW = D0 + 1
NW = P + HPH
EPS_A = 1e-15

H1, D1 = 16, 128
SCALE = float(D1) ** -0.5
QH = 4
QUADS = H1 // QH
KB = B + B * CH
XW = C + 2

F0, F1 = 512, 1024
FT = 4
UNITS = 2 * NG


def hidden(k, g, e):
    return [("H", k, g, e, f) for f in range(FT)]


def outputs(k, g, e):
    return [("Y", k, g, e, q) for q in range(2)]


def weave(main, *extra):
    plan = []
    for n, item in enumerate(main):
        plan.append(item)
        plan += extra[n] if n < len(extra) else []
    return plan


def make_plan():
    plan = [("W", "qkv"), ("S", 0, 0), ("N", 0, 0), ("T", 0, 0), ("S", 0, 1), ("kv", 0), ("N", 0, 1), ("kv", 1), ("vk", 0),
            ("T", 0, 1), ("kv", 2), ("vk", 1), ("kv", 3), ("vk", 2), ("q", 0), ("S", 0, 2), ("kv", 4), ("vk", 3), ("q", 1),
            ("kv", 5), ("vk", 4), ("N", 0, 2), ("q", 2), ("kv", 6), ("vk", 5), ("q", 3), ("S", 0, 3), ("kv", 7), ("vk", 6),
            ("T", 0, 2), ("vk", 7), ("kv", 8), ("bd", 0), ("N", 0, 3), ("W", "proj")]
    plan += weave([("kv", 9), ("vk", 8), ("kv", 10), ("vk", 9), ("kv", 11), ("vk", 10), ("kv", 12), ("vk", 11), ("kv", 13),
                   ("vk", 12), ("kv", 14), ("vk", 13), ("kv", 15), ("vk", 14)],
                  [("nd", 0), ("T", 0, 3)], [("W", "wg"), ("nd", 1)], [("nd", 2)], [("W", "w0a"), ("nd", 3)],
                  [("OT", 0), ("nd", 4)], [("W", "w0b"), ("nd", 5)], [("nd", 6), ("pr", 0)], [("W", "w1a"), ("nd", 7)],
                  [("pr", 1), ("OT", 1)], [("W", "w1b"), ("S", 1, 0)], [("pr", 2)], [("N", 1, 0)], [("pr", 3), ("S", 1, 1)],
                  [("T", 1, 0)])
    plan += [("q", 4), ("vk", 15), ("q", 5), ("bd", 1), ("N", 1, 1), ("gate", 0), ("q", 6), ("mk", 0)]
    plan += weave(hidden(1, 0, 0), [("q", 7)], [("T", 1, 1)], [("nd", 8)], [("nd", 9)])
    plan += weave(hidden(1, 0, 1), [("nd", 10)], [("nd", 11)], [("OT", 2), ("nd", 12)], [("nd", 13)])
    plan += weave(outputs(1, 0, 0), [("pr", 4), ("nd", 14)], [("pr", 5), ("nd", 15), ("gate", 1)])
    plan += weave(hidden(1, 1, 0), [("OT", 3), ("S", 1, 2)], [("pr", 6)], [("N", 1, 2)], [("pr", 7), ("mk", 1)])
    plan += weave(outputs(1, 0, 1), [("S", 1, 3)], [("wo", 0)])
    plan += weave(hidden(1, 1, 1), [("T", 1, 2)], [], [("wo", 1)], [("wo", 2), ("gate", 2)])
    plan += weave(outputs(1, 1, 0), [("N", 1, 3)], [("wo", 3)])
    plan += weave(hidden(1, 2, 0), [], [], [], [("mk", 2), ("wo", 4)])
    plan += weave(outputs(1, 1, 1), [("S", 2, 0)])
    plan += weave(hidden(1, 2, 1), [("T", 1, 3)], [("N", 2, 0)], [("wo", 5)], [("gate", 3)])
    plan += weave(outputs(1, 2, 0), [("R", 2, 0)], [("S", 2, 1)])
    plan += weave(hidden(1, 3, 0), [("wo", 6)], [("N", 2, 1)], [], [("mk", 3)])
    plan += weave(outputs(1, 2, 1), [("wo", 7)], [("R", 2, 1)])
    plan += weave(hidden(1, 3, 1), [("S", 2, 2)], [], [], [("N", 2, 2), ("ws",)])
    plan += weave(outputs(1, 3, 0), [("R", 2, 2)], [("gr", 0)])
    plan += weave(outputs(1, 3, 1), [], [("S", 2, 3), ("gr", 1), ("N", 2, 3), ("qw", "k", 0), ("ev", 0)])
    plan += [("gr", 2), ("R", 2, 3), ("qw", "v", 0), ("gr", 3), ("qw", "q", 0), ("kb", 0, 0), ("ev", 1), ("kb", 0, 1)]
    plan += weave([("kb", 0, i) for i in range(2, KB)], [], [("z", 0, 0)], [("z", 0, 1)])
    plan.append(("qw", "k", 1))
    between = {0: [[("fa", i)] for i in range(4)], 1: [[("ft", i)] for i in range(4)],
               2: [[("ft", i)] for i in range(4, 8)] + [[("S", 3, 0), ("N", 3, 0)]], 3: []}
    for Q in range(QUADS):
        bt = between[Q] + [[]] * 5
        plan += [("s", Q, 0), ("s", Q, 1)]
        if Q == 1:
            plan.append(("fs",))
        if Q < QUADS - 1:
            plan += [("qw", "q", Q + 1), ("kb", Q + 1, 0)] + [("z", Q, 0)] * (Q > 0) + [("kb", Q + 1, 1), ("p", Q, 0)]
            plan += [("z", Q, 1)] * (Q > 0) + [("p", Q, 1), ("t", Q, 0)] + bt[0] + [("kb", Q + 1, 2), ("z", Q, 2), ("t", Q, 1)]
            plan += bt[1] + [("kb", Q + 1, 3), ("o", Q, 0)] + bt[2] + [("kb", Q + 1, 4), ("z", Q, 3), ("qw", "v", Q + 1)]
            plan += [("kb", Q + 1, 5)] + ([("qw", "k", Q + 2)] if Q + 2 < QUADS else []) + bt[3] + [("o", Q, 1)] + bt[4]
    h = hidden(3, 0, 0)
    plan += [("T", 3, 0), ("z", 3, 0), h[0], ("p", 3, 0), ("z", 3, 1), h[1], ("p", 3, 1), ("t", 3, 0), ("z", 3, 2), h[2],
             ("t", 3, 1), h[3], ("o", 3, 0), ("S", 3, 2), ("z", 3, 3), ("N", 3, 2), ("o", 3, 1)]
    plan += weave(hidden(3, 0, 1), [("T", 3, 2)])
    plan += outputs(3, 0, 0)
    plan += weave(hidden(3, 2, 0), [("S", 3, 1)], [], [("N", 3, 1)])
    plan += outputs(3, 0, 1)
    plan += weave(hidden(3, 2, 1), [("T", 3, 1)], [("S", 3, 3)])
    plan += weave(outputs(3, 2, 0), [("N", 3, 3)])
    plan += hidden(3, 1, 0) + outputs(3, 2, 1)
    plan += weave(hidden(3, 1, 1), [("T", 3, 3)])
    plan += outputs(3, 1, 0) + hidden(3, 3, 0) + outputs(3, 1, 1) + hidden(3, 3, 1) + outputs(3, 3, 0) + outputs(3, 3, 1)
    return plan


PLAN = make_plan()
assert len(set(PLAN)) == len(PLAN)
assert [i[1:] for i in PLAN if i[0] == "S"] == [i[1:] for i in PLAN if i[0] == "N"]
AT = {item: n for n, item in enumerate(PLAN)}


def earlier(kind, item, **fixed):
    return sum(1 for n in PLAN[:AT[item]] if n[0] == kind and all(n[int(k[1:])] == v for k, v in fixed.items()))


def turn(item):
    return earlier("T", item) + earlier("OT", item)


def transformer(nc, x_in, wqkv, wproj, bproj, wg, w0a, b0a, w0b, b0b, w1a, b1a, w1b, b1b,
                wq, wk, wv, wo, bk, bqc, bvc, bo, f1, fb1, f2, fb2, ident_in, out):
    with ExitStack() as ctx:
        def place(name, shape, dt, at):
            where = (at[0] + 31) // 32 * 32
            size = 4
            for n in shape[1:]:
                size *= n
            at[0] = where + size
            return nc.alloc_sbuf_tensor_at(name, shape, dt, offset=where)

        def sem(name):
            return ctx.enter_context(nc.semaphore(name))

        top = [nc.sbuf_base]
        x = place("x", [P, NT, C], F32, top)
        xTh, xTl, xrh, xrl = [], [], [], []
        for b in range(B):
            for name, tr, rows in (("h", xTh, xrh), ("l", xTl, xrl)):
                tr.append(place(f"xT{name}{b}", [P, CH, T], F32R, [top[0]]))
                rows.append(place(f"xr{name}{b}", [P, TB, XW], F32R, top))
        ident = place("ident", [P, P], F32, top)
        ones = place("ones", [P, P], F32R, top)
        onesf = place("onesf", [P, P], F32, top)
        mhalf = place("mhalf", [P, TPG], F32, top)
        stats = place("stats", [P, TPG, 6], F32, top)
        mv = place("mv", [P, 2, TPG, 2], F32, top)
        vare = place("vare", [P, 2, TPG], F32, top)
        rstd = place("rstd", [P, 2, TPG], F32, top)
        b0as = place("b0as", [P, FT], F32, top)
        b1as = place("b1as", [P, FT], F32, top)
        fb1s = place("fb1s", [P, F1 // P], F32, top)
        bqcs = place("bqcs", [P, H1], F32, top)
        bvcs = place("bvcs", [P, H1], F32, top)
        rows1 = place("rows1", [P, 2, C], F32, top)
        sx = place("sx", [P, CH, B], F32, top)
        asum = place("asum", [P, 4], F32, top)
        thr = place("thr", [P, 2], F32, top)
        nthr = place("nthr", [P, 2], F32, top)
        mx = place("mx", [P, QH, B], F32, top)
        nmx = place("nmx", [P, QH, B], F32, top)
        ssum = place("ssum", [P, QH, B], F32, top)
        rs = place("rs", [P, QH, B], F32, top)
        end = nc.sbuf_usable_end // 32 * 32 - 2 * TPG * C * 4
        xn = place("xn", [P, 2 * TPG, C], F32, [end])

        wshape = {"qkv": [P, 2, 3 * C], "proj": [P, 2, C], "w0a": [P, 2, F0], "w1a": [P, 2, F0],
                  "w0b": [P, 4, C], "w1b": [P, 4, C]}
        low = [top[0]]
        wh0, wl0 = {}, {}
        for k, s in wshape.items():
            wh0[k], wl0[k] = place(f"{k}_h", s, F32R, low), place(f"{k}_l", s, F32R, low)
        wgs = place("wgs", [P, CH, 2], F32, low)
        wgp = place("wgp", [P, CH, 4], F32R, low)
        mask = place("mask", [P, NT, 2], F32, low)
        rows0 = place("rows0", [P, 3, C], F32, low)
        rd = place("rd", [P, 2, CH, HPH], F32, low)

        def ffn_buffers(tag, at):
            hf, hh, hl = place(f"hf{tag}", [P, 2, G], F32, at), [], []
            for e in range(2):
                hh.append(place(f"hh{tag}{e}", [P, FT, G], F32R, at))
                hl.append(place(f"hl{tag}{e}", [P, FT, G], F32R, at))
            return hf, hh, hl

        raw_at = [low[0]]
        raw0 = {k: place(f"{k}_raw", s, F32, raw_at) for k, s in wshape.items()}
        mid = [low[0]]
        ff0 = ffn_buffers("0", mid)
        mid[0] = max(mid[0], raw_at[0])
        lin = [mid[0]]
        Kh = place("Kh", [P, 2, C], F32R, lin)
        Kl = place("Kl", [P, 2, C], F32R, lin)
        Vh0 = place("Vh0", [P, 2, H0, VW], F32R, lin)
        Vl0 = place("Vl0", [P, 2, H0, VW], F32R, lin)
        Qh = place("Qh", [P, CH, T], F32R, lin)
        Ql = place("Ql", [P, CH, T], F32R, lin)
        BD = place("BD", [P, CH, NW], F32, lin)
        BDh = place("BDh", [P, CH, NW], F32R, lin)
        BDl = place("BDl", [P, CH, NW], F32R, lin)
        on = place("on", [P, 2 * TPG, C], F32, lin)
        Oh = place("Oh", [P, CH, G], F32R, lin)
        Ol = place("Ol", [P, CH, G], F32R, lin)
        woraw = place("woraw", [P, TB, 2 * C], F32, lin)
        assert lin[0] <= end, (lin[0], end)

        up = [mid[0]]
        woh = place("woh", [P, TB, 2 * C], F32R, up)
        wol = place("wol", [P, TB, 2 * C], F32R, up)
        Gh = place("Gh", [P, B, CH, C], F32R, up)
        Gl = place("Gl", [P, B, CH, C], F32R, up)
        Rh = place("Rh", [P, CH, 2, B, C], F32R, up)
        Rl = place("Rl", [P, CH, 2, B, C], F32R, up)
        wosum = place("wosum", [P, 2, C], F32, up)
        sxh = place("sxh", [P, CH, B, P], F32R, up)
        assert up[0] <= end, (up[0], end)
        ovr = [mid[0]]
        S = place("S", [P, QH, B, D1], F32, ovr)
        PTh = place("PTh", [P, 2, 2, B, D1], F32R, ovr)
        PTl = place("PTl", [P, 2, 2, B, D1], F32R, ovr)
        Zf = place("Zf", [P, 2, 2 * C], F32, ovr)
        Zh = place("Zh", [P, QH, B, C], F32R, ovr)
        Zl = place("Zl", [P, QH, B, C], F32R, ovr)
        assert ovr[0] <= mid[0] + 2 * 4 * TB * 2 * C
        att = [top[0]]
        raw = {k: place(f"raw{k}", [P, CH, 512], F32, att) for k in "kqv"}
        assert att[0] <= top[0] + 4 * 16 * C
        wh, wl = {}, {}
        for k in "kqv":
            wh[k], wl[k] = place(f"wh{k}", [P, CH, 512], F32R, att), place(f"wl{k}", [P, CH, 512], F32R, att)
        bkr = place("bkr", [P, H1 * D1], F32, att)
        sxl = place("sxl", [P, CH, B, P], F32R, att)
        ksum = place("ksum", [P, B, 512], F32, att)
        Bf = place("Bf", [P, 2, 512], F32, att)
        Bh = place("Bh", [P, B, CH, 512], F32R, att)
        Bl = place("Bl", [P, B, CH, 512], F32R, att)
        assert att[0] <= mid[0], (att[0], mid[0])
        fr = [nc.sbuf_base + 4 * NT * C]
        f1raw = place("f1raw", [P, CH, F1], F32, fr)
        f2raw = place("f2raw", [P, F1 // P, C], F32, fr)
        neg = place("neg", [P, 2 * F1], F32, fr)
        assert fr[0] <= nc.sbuf_base + 4 * NT * C + 16 * TB * XW
        fw = [mid[0] - 2 * 8 * F1 - 64]
        f1t = place("f1t", [P, CH, F1], F32R, fw)
        f2t = place("f2t", [P, F1 // P, C], F32R, fw)
        assert att[0] <= mid[0] - 2 * 8 * F1 - 64 and fw[0] <= mid[0], (att[0], mid[0])
        ff1_at = [top[0]]
        ff1 = ffn_buffers("1", ff1_at)
        assert ff1_at[0] <= mid[0] - 2 * 8 * F1 - 64
        FF = {1: ff0, 3: ff1}

        ps = ctx.enter_context(nc.psum_tensor("ps", [P, 8, 512], F32))

        x_in_s = [sem(f"x_loaded{g}") for g in range(NG)]
        id_in, cst_in = sem("identity_loaded"), sem("constants_loaded")
        w0_in = {k: sem(f"{k}_loaded") for k in wshape}
        w0_hi = {k: sem(f"{k}_hi") for k in (*wshape, "wg")}
        w0_lo = {k: sem(f"{k}_lo") for k in (*wshape, "wg")}
        ones_set = sem("ones_set")
        dve_chain = sem("dve_chain")
        var_ready, rstd_ready, xn_ready = sem("var_ready"), sem("rstd_ready"), sem("xn_ready")
        xT_filled, xT_hi, xT_lo = sem("xT_filled"), sem("xT_hi"), sem("xT_lo")
        kv_filled, kv_hi, kv_lo, kv_used = sem("kv_filled"), sem("kv_hi"), sem("kv_lo"), sem("kv_used")
        q_filled, q_hi, q_lo = sem("q_filled"), sem("q_hi"), sem("q_lo")
        bd_done, bd_hi, bd_lo = sem("bd_done"), sem("bd_hi"), sem("bd_lo")
        nd_filled, o_norm = sem("nd_filled"), sem("o_norm")
        pr_filled, x1_added = sem("proj_filled"), sem("x1_added")
        gate_filled, mask_ready = sem("gate_filled"), sem("mask_ready")
        h_filled = {k: sem(f"h_filled{k}") for k in FF}
        h_act = {k: sem(f"h_activated{k}") for k in FF}
        h_hi = {k: sem(f"h_hi{k}") for k in FF}
        h_lo = {k: sem(f"h_lo{k}") for k in FF}
        y_filled = {k: sem(f"y_filled{k}") for k in FF}
        y_added = {k: sem(f"y_added{k}") for k in FF}
        f_in, f_abs, f_sum, f_tern = sem("ffn_loaded"), sem("f_abs"), sem("f_sum"), sem("f_ternary")
        thr_ready = sem("thr_ready")
        stored = sem("stored")
        wo_in, bk_in, wo_hi, wo_lo = sem("wo_loaded"), sem("bk_loaded"), sem("wo_hi"), sem("wo_lo")
        xr_hi, xr_lo, xr_one = sem("rows_hi"), sem("rows_lo"), sem("rows_ones")
        ws_filled, ws_read = sem("wosum_filled"), sem("wosum_read")
        gr_filled, gr_hi, gr_lo = sem("gram_filled"), sem("gram_hi"), sem("gram_lo")
        sx_ready, sx_hi, sx_lo = sem("sx_ready"), sem("sx_hi"), sem("sx_lo")
        raw_in = {k: sem(f"raw{k}_loaded") for k in "qkv"}
        w_hi = {k: sem(f"w{k}_hi") for k in "qkv"}
        w_lo = {k: sem(f"w{k}_lo") for k in "qkv"}
        b_filled, b_taken, b_hi, b_lo = sem("b_filled"), sem("b_taken"), sem("b_hi"), sem("b_lo")
        s_filled, s_ready, s_max, s_neg = sem("s_filled"), sem("s_ready"), sem("s_max"), sem("s_neg")
        e_ready, r_ready, p_ready = sem("exp_ready"), sem("rsum_ready"), sem("p_ready")
        t_filled, pt_hi, pt_lo = sem("t_filled"), sem("pt_hi"), sem("pt_lo")
        z_filled, z_ready, z_hi, z_lo = sem("z_filled"), sem("z_ready"), sem("z_hi"), sem("z_lo")
        o_filled, o_added = sem("o_filled"), sem("o_added")

        def wait(eng, s, v):
            if v > 0:
                eng.wait_ge(s, v)

        def f32(ap):
            return ap.bitcast(F32)

        def x_final(k, g):
            if k == 0:
                return x_in_s[g], 16
            if k == 1:
                return x1_added, 2 * (g + 1)
            if k == 2:
                return y_added[1], 2 * (unit_of(1, g, 1) + 1)
            return o_added, QUADS * (1 + g % 2)

        def unit_of(k, g, e):
            return earlier("H", ("H", k, g, e, 0), _1=k) // FT

        def ring_free(k, g):
            n = earlier("N", ("N", k, g)) - 2
            if n < 0:
                return xn_ready, 0
            k2, g2 = [i[1:] for i in PLAN if i[0] == "N"][n]
            if k2 == 2:
                return xr_lo, g2 + 1
            return xT_filled, CH * (turn(("T", k2, g2)) + 1)

        def buffers_free(eng, k, u):
            if k == 1 and u == 0:
                for w in wshape:
                    eng.wait_ge(w0_lo[w], 1)
            if k == 3 and u == 0:
                for w in "kqv":
                    eng.wait_ge(w_lo[w], QUADS)
                eng.wait_ge(b_filled, KB * QUADS)
            if k == 3 and u == 1:
                eng.wait_ge(s_filled, 2 * QUADS)
                eng.wait_ge(z_filled, QH * QUADS)

        def slot(k, g):
            return earlier("N", ("N", k, g)) % 2

        def span(g):
            return slice(g % 2 * G, (g % 2 + 1) * G)

        def gram_bank(b):
            return 4 if b == 0 else 0

        def key_bank(Q, i):
            return (6 if Q == 0 else 0) + i % 2

        block = ctx.enter_context(nc.Block())

        @block.sync
        def _(sp):
            xv = x_in.rearrange("b (p t) c -> p b t c", p=P)

            def load_x(g):
                sp.dma_start(x[:, g * TPG:(g + 1) * TPG, :],
                             xv[:, g // 2, g % 2 * TPG:(g % 2 + 1) * TPG, :]).then_inc(x_in_s[g], 16)

            load_x(0)
            sp.dma_start(ident[:], ident_in).then_inc(id_in, 16)
            sp.dma_start(raw0["qkv"][:], wqkv.rearrange("(c p) n -> p c n", p=P)).then_inc(w0_in["qkv"], 16)
            load_x(1)
            sp.dma_start(rows0[:, 0, :], bproj.partition_broadcast(P)).then_inc(cst_in, 16)
            load_x(2)
            load_x(3)
            sp.dma_start(raw0["proj"][:], wproj.rearrange("(c p) n -> p c n", p=P)).then_inc(w0_in["proj"], 16)
            sp.dma_start(wgs[:], wg.rearrange("(c p) n -> p c n", p=P)).then_inc(cst_in, 16)
            for dst, src in ((b0as[:], b0a), (b1as[:], b1a), (fb1s[:], fb1), (bqcs[:], bqc), (bvcs[:], bvc),
                             (rows0[:, 1, :], b0b.partition_broadcast(P)), (rows0[:, 2, :], b1b.partition_broadcast(P)),
                             (rows1[:, 0, :], bo.partition_broadcast(P)), (rows1[:, 1, :], fb2.partition_broadcast(P))):
                sp.dma_start(dst, src).then_inc(cst_in, 16)
            for k, src in (("w0a", w0a), ("w0b", w0b), ("w1a", w1a), ("w1b", w1b)):
                sp.dma_start(raw0[k][:], src.rearrange("(c p) n -> p c n", p=P)).then_inc(w0_in[k], 16)
            wov = wo.rearrange("(s p t) n -> p t s n", s=2, p=P)
            for s in range(2):
                sp.dma_start(woraw[:, :, s * C:(s + 1) * C], wov[:, :, s, :]).then_inc(wo_in, 16)

            def load_quad(k, Q):
                w = {"q": wq, "k": wk, "v": wv}[k]
                wait(sp, w_lo[k], Q)
                sp.dma_start(raw[k][:], w.rearrange("(c p) n -> p c n", p=P)[:, :, Q * 512:(Q + 1) * 512])\
                  .then_inc(raw_in[k], 16)

            sp.wait_ge(pr_filled, NT // 2)
            for k in "kqv":
                load_quad(k, 0)
            sp.wait_ge(y_filled[1], 2 * UNITS)
            sp.dma_start(bkr[:], bk.partition_broadcast(P)).then_inc(bk_in, 16)
            sp.wait_ge(gr_filled, B)
            sp.dma_start(f1raw[:], f1.rearrange("(c p) n -> p c n", p=P)).then_inc(f_in, 16)
            sp.dma_start(f2raw[:], f2.rearrange("(c p) n -> p c n", p=P)).then_inc(f_in, 16)
            for Q in range(1, QUADS):
                for k in "kqv":
                    load_quad(k, Q)
            ov = out.rearrange("b (p t) c -> p b t c", p=P)
            for kind, *at in PLAN:
                if kind == "Y" and at[0] == 3 and at[2] == 1:
                    k, g, e, q = at
                    sp.wait_ge(y_added[3], 2 * unit_of(k, g, e) + q + 1)
                    t = g % 2 * TPG + 2 * q
                    sp.dma_start(ov[:, g // 2, t:t + 2, :], x[:, g // 2 * TB + t:g // 2 * TB + t + 2, :])\
                      .then_inc(stored, 16)
            sp.wait_ge(stored, 16 * 2 * NG)

        @block.gpsimd
        def _(pool):
            nc.gpsimd.memset(onesf[:], 1.0).then_inc(ones_set, 1)
            nc.gpsimd.memset(mhalf[:], -0.5).then_inc(ones_set, 1)
            pool.wait_ge(ones_set, 2)
            for item in PLAN:
                kind, *at = item
                if kind == "W":
                    k, = at
                    pool.wait_ge(w0_hi[k], 1)
                    if k == "wg":
                        nc.gpsimd.tensor_tensor(wgp[:, :, 2:4], wgs[:], f32(wgp[:, :, 0:2]),
                                                ALU.subtract).then_inc(w0_lo[k], 1)
                    else:
                        nc.gpsimd.tensor_tensor(wl0[k][:], raw0[k][:], f32(wh0[k][:]),
                                                ALU.subtract).then_inc(w0_lo[k], 1)
                elif kind == "S":
                    n = earlier("S", item)
                    pool.wait_ge(var_ready, n + 1)
                    nc.gpsimd.tensor_tensor(rstd[:, n % 2, :], vare[:, n % 2, :], mhalf[:],
                                            ALU.pow).then_inc(rstd_ready, 1)
                elif kind == "H":
                    k, g, e, f = at
                    u = unit_of(k, g, e)
                    i = FT * u + f
                    hf, hh, hl = FF[k]
                    if f == 0:
                        wait(pool, y_filled[k], 2 * (u - 1))
                        buffers_free(pool, k, u)
                    pool.wait_ge(h_hi[k], i + 1)
                    nc.gpsimd.tensor_tensor(hl[u % 2][:, f, :], hf[:, i % 2, :], f32(hh[u % 2][:, f, :]),
                                            ALU.subtract).then_inc(h_lo[k], 1)
                elif kind == "wo":
                    t, = at
                    pool.wait_ge(wo_hi, t + 1)
                    nc.gpsimd.tensor_tensor(wol[:, t, :], woraw[:, t, :], f32(woh[:, t, :]),
                                            ALU.subtract).then_inc(wo_lo, 1)
                elif kind == "R":
                    k, g = at
                    n = slot(k, g)
                    tiles = slice(g % 2 * TPG, (g % 2 + 1) * TPG)
                    pool.wait_ge(xr_hi, g + 1)
                    nc.gpsimd.tensor_tensor(xrl[g // 2][:, tiles, 0:C], xn[:, n * TPG:(n + 1) * TPG, :],
                                            f32(xrh[g // 2][:, tiles, 0:C]), ALU.subtract).then_inc(xr_lo, 1)
                elif kind == "qw":
                    k, Q = at
                    pool.wait_ge(w_hi[k], Q + 1)
                    nc.gpsimd.tensor_tensor(wl[k][:], raw[k][:], f32(wh[k][:]), ALU.subtract).then_inc(w_lo[k], 1)
                elif kind == "kb" and at[1] < B * CH:
                    Q, i = at
                    n = B * CH * Q + i
                    b, c = i // CH, i % CH
                    pool.wait_ge(b_hi, n + 1)
                    nc.gpsimd.tensor_tensor(Bl[:, b, c, :], Bf[:, n % 2, :], f32(Bh[:, b, c, :]),
                                            ALU.subtract).then_inc(b_lo, 1)
                elif kind == "z":
                    Q, h = at
                    n = QH * Q + h
                    pool.wait_ge(z_hi, n + 1)
                    nc.gpsimd.tensor_tensor(Zl[:, h, :, :], Zf[:, n % 2, :].rearrange("p (b c) -> p b c", b=B),
                                            f32(Zh[:, h, :, :]), ALU.subtract).then_inc(z_lo, 1)

        @block.scalar
        def _(act):
            act.wait_ge(ones_set, 2)
            nc.scalar.activation(ones[:], onesf[:], ACT.Copy).then_inc(ones_set, 1)
            for item in PLAN:
                kind, *at = item
                if kind == "W":
                    k, = at
                    if k == "wg":
                        act.wait_ge(cst_in, 16 * 11)
                        nc.scalar.activation(wgp[:, :, 0:2], wgs[:], ACT.Copy).then_inc(w0_hi[k], 1)
                    else:
                        act.wait_ge(w0_in[k], 16)
                        nc.scalar.activation(wh0[k][:], raw0[k][:], ACT.Copy).then_inc(w0_hi[k], 1)
                elif kind in ("T", "OT"):
                    n = turn(item)
                    for c in range(CH):
                        act.wait_ge(xT_filled, CH * n + c + 1)
                        if kind == "T":
                            k, g = at
                            if k == 3:
                                act.wait_ge(f_tern, 2 * FT)
                            dst = xTh[g // 2][:, c, span(g)]
                        else:
                            wait(act, pr_filled, 2 * at[0])
                            dst = Oh[:, c, :]
                        nc.scalar.activation(dst, ps[:, 6 + c, :], ACT.Copy).then_inc(xT_hi, 1)
                elif kind == "kv":
                    i, = at
                    act.wait_ge(kv_filled, i + 1)
                    wait(act, kv_used, i - 1)
                    nc.scalar.activation(Kh[:, i % 2, :], ps[:, i % 2, 0:C], ACT.Relu)
                    nc.scalar.activation(Vh0[:, i % 2, :, 0:D0],
                                         ps[:, i % 2, C:2 * C].rearrange("p (h d) -> p h d", d=D0),
                                         ACT.Copy).then_inc(kv_hi, 1)
                elif kind == "q":
                    i, = at
                    h, ch = i % 4 // 2, i % 2
                    act.wait_ge(q_filled, i + 1)
                    nc.scalar.activation(Qh[:, h, ch * G:(ch + 1) * G], ps[:, 4, :], ACT.Relu).then_inc(q_hi, 1)
                elif kind == "bd":
                    act.wait_ge(bd_done, at[0] + 1)
                    nc.scalar.activation(BDh[:], BD[:], ACT.Copy).then_inc(bd_hi, 1)
                elif kind == "H":
                    k, g, e, f = at
                    u = unit_of(k, g, e)
                    i = FT * u + f
                    hf, hh, hl = FF[k]
                    bias = (b0as, b1as)[e] if k == 1 else fb1s
                    func = ACT.Relu if k == 1 and e else ACT.Gelu
                    if f == 0:
                        buffers_free(act, k, u)
                    col = f if k == 1 else FT * e + f
                    act.wait_ge(h_filled[k], i + 1)
                    wait(act, h_lo[k], i - 1)
                    nc.scalar.activation(hf[:, i % 2, :], ps[:, i % 2, :], func,
                                         bias=bias[:, col:col + 1]).then_inc(h_act[k], 1)
                elif kind == "wo":
                    t, = at
                    act.wait_ge(pr_filled, NT // 2)
                    act.wait_ge(wo_in, 32)
                    nc.scalar.activation(woh[:, t, :], woraw[:, t, :], ACT.Copy).then_inc(wo_hi, 1)
                elif kind == "R":
                    k, g = at
                    n = slot(k, g)
                    act.wait_ge(xn_ready, TPG * (earlier("N", ("N", k, g)) + 1))
                    act.wait_ge(h_filled[1], FT * (unit_of(1, g // 2 * 2 + 1, 1) + 1))
                    nc.scalar.activation(xrh[g // 2][:, g % 2 * TPG:(g % 2 + 1) * TPG, 0:C],
                                         xn[:, n * TPG:(n + 1) * TPG, :], ACT.Copy).then_inc(xr_hi, 1)
                elif kind == "ws":
                    act.wait_ge(ws_filled, 1)
                    nc.scalar.activation(wosum[:], ps[:, 4, :].rearrange("p (s c) -> p s c", s=2),
                                         ACT.Copy).then_inc(ws_read, 1)
                elif kind == "ev":
                    b, = at
                    act.wait_ge(gr_filled, b + 1)
                    for c in range(CH):
                        nc.scalar.activation(Gh[:, b, c, :], ps[:, gram_bank(b) + c, 0:C], ACT.Copy).then_inc(gr_hi, 1)
                        nc.scalar.activation(Rh[:, c, :, b, :],
                                             ps[:, gram_bank(b) + 2 + c, :].rearrange("p (s c) -> p s c", s=2),
                                             ACT.Copy).then_inc(gr_hi, 1)
                        if b == B - 1:
                            act.wait_ge(sx_ready, CH * b + c + 1)
                    if b == B - 1:
                        nc.scalar.activation(sxh[:], sx[:].rearrange("p c (b a) -> p c b a", a=1).to_broadcast([P, CH, B, P]),
                                             ACT.Copy).then_inc(sx_hi, 1)
                elif kind == "qw":
                    k, Q = at
                    act.wait_ge(raw_in[k], 16 * (Q + 1))
                    if Q == 0:
                        act.wait_ge(y_filled[1], 2 * UNITS)
                    used, n = {"q": (s_filled, 2 * Q), "k": (b_filled, KB * Q), "v": (z_filled, QH * Q)}[k]
                    wait(act, used, n)
                    nc.scalar.activation(wh[k][:], raw[k][:], ACT.Copy).then_inc(w_hi[k], 1)
                elif kind == "kb" and at[1] < B * CH:
                    Q, i = at
                    n = B * CH * Q + i
                    act.wait_ge(b_taken, KB * Q + i + 1)
                    wait(act, s_filled, 2 * Q)
                    nc.scalar.activation(Bh[:, i // CH, i % CH, :], Bf[:, n % 2, :], ACT.Copy).then_inc(b_hi, 1)
                elif kind == "s":
                    Q, a = at
                    act.wait_ge(s_neg, 2 * Q + a + 1)
                    for h in (2 * a, 2 * a + 1):
                        for b in range(B):
                            nc.scalar.activation(S[:, h, b, :], S[:, h, b, :], ACT.Exp, bias=nmx[:, h, b:b + 1],
                                                 scale=SCALE, accum_out=ssum[:, h, b:b + 1]).then_inc(e_ready, 1)
                elif kind == "z":
                    Q, h = at
                    n = QH * Q + h
                    act.wait_ge(z_ready, n + 1)
                    wait(act, o_filled, 2 * (Q - 1) + h // 2 + 1)
                    nc.scalar.activation(Zh[:, h, :, :], Zf[:, n % 2, :].rearrange("p (b c) -> p b c", b=B),
                                         ACT.Copy).then_inc(z_hi, 1)
                elif kind == "t":
                    Q, a = at
                    act.wait_ge(t_filled, 2 * Q + a + 1)
                    wait(act, o_filled, 2 * (Q - 1) + a + 1)
                    nc.scalar.activation(PTh[:, a, :, :, :], ps[:, 6 + a, :].rearrange("p (h b q) -> p h b q", h=2, b=B),
                                         ACT.Copy).then_inc(pt_hi, 1)
                elif kind == "fa":
                    j, = at
                    act.wait_ge(f_in, 32)
                    half = slice(j % 2 * F1, (j % 2 + 1) * F1)
                    wait(act, f_abs, j - 1)
                    nc.scalar.activation(neg[:, half], (f1raw, f2raw)[j // 2][:].rearrange("p a b -> p (a b)")[:, half],
                                         ACT.Abs, accum_out=asum[:, j:j + 1]).then_inc(f_abs, 1)

        @block.vector
        def _(dve):
            chain = [0]

            def link(ins):
                chain[0] += 1
                ins.then_inc(dve_chain, 1)
                dve.wait_ge(dve_chain, chain[0])

            dve.wait_ge(ones_set, 2)
            for s in range(2):
                one = onesf[:, 0:H0].rearrange("p (h a) -> p h a", a=1)
                link(nc.vector.tensor_copy(Vh0[:, s, :, D0:VW], one))
                link(nc.vector.tensor_scalar(Vl0[:, s, :, D0:VW], one, 0.0, None, ALU.mult))
            link(nc.vector.memset(BD[:], 0.0))
            for item in PLAN:
                kind, *at = item
                if kind == "S":
                    k, g = at
                    n = earlier("S", item)
                    dve.wait_ge(*x_final(k, g))
                    for i in range(TPG):
                        last = nc.vector.bn_stats(stats[:, i, :], x[:, g * TPG + i, :])
                    link(last)
                    for i in range(TPG):
                        last = nc.vector.bn_aggr(mv[:, n % 2, i, :], stats[:, i, :])
                    link(last)
                    wait(dve, rstd_ready, n - 1)
                    nc.vector.tensor_scalar(vare[:, n % 2, :], mv[:, n % 2, :, 1], EPS_LN, None,
                                            ALU.add).then_inc(var_ready, 1)
                elif kind == "N":
                    k, g = at
                    n = earlier("N", item)
                    dve.wait_ge(rstd_ready, n + 1)
                    wait(dve, *ring_free(k, g))
                    for i in range(TPG):
                        nc.vector.tensor_scalar(xn[:, (n % 2) * TPG + i, :], x[:, g * TPG + i, :],
                                                mv[:, n % 2, i, 0:1], rstd[:, n % 2, i:i + 1],
                                                ALU.subtract, ALU.mult).then_inc(xn_ready, 1)
                    if k != 1:
                        if n < 1:
                            dve.wait_ge(cst_in, 16 * 11)
                        row = {0: rows0[:, 0:1, :], 2: rows1[:, 0:1, :], 3: rows1[:, 1:2, :]}[k]
                        xs = x[:, g * TPG:(g + 1) * TPG, :]
                        dve.wait_ge(xn_ready, TPG * (n + 1))
                        link(nc.vector.tensor_tensor(xs, xs, row.to_broadcast([P, TPG, C]), ALU.add))
                elif kind in ("T", "OT"):
                    n = turn(item)
                    for c in range(CH):
                        dve.wait_ge(xT_hi, CH * n + c + 1)
                        if kind == "T":
                            hi, lo = (m[at[1] // 2][:, c, span(at[1])] for m in (xTh, xTl))
                        else:
                            hi, lo = Oh[:, c, :], Ol[:, c, :]
                        nc.vector.tensor_tensor(lo, ps[:, 6 + c, :], f32(hi), ALU.subtract).then_inc(xT_lo, 1)
                elif kind == "kv":
                    i, = at
                    dve.wait_ge(kv_hi, i + 1)
                    nc.vector.scalar_tensor_tensor(Kl[:, i % 2, :], ps[:, i % 2, 0:C], 0.0, f32(Kh[:, i % 2, :]),
                                                   ALU.max, ALU.subtract)
                    nc.vector.tensor_tensor(Vl0[:, i % 2, :, 0:D0],
                                            ps[:, i % 2, C:2 * C].rearrange("p (h d) -> p h d", d=D0),
                                            f32(Vh0[:, i % 2, :, 0:D0]), ALU.subtract).then_inc(kv_lo, 1)
                elif kind == "q":
                    i, = at
                    h, ch = i % 4 // 2, i % 2
                    dve.wait_ge(q_hi, i + 1)
                    nc.vector.scalar_tensor_tensor(Ql[:, h, ch * G:(ch + 1) * G], ps[:, 4, :], 0.0,
                                                   f32(Qh[:, h, ch * G:(ch + 1) * G]),
                                                   ALU.max, ALU.subtract).then_inc(q_lo, 1)
                elif kind == "bd":
                    b, = at
                    dve.wait_ge(kv_used, TB * (b + 1))
                    wait(dve, bd_lo, b)
                    for h in range(CH):
                        for r in range(HPH):
                            rs_ = slice(D0 * r, D0 * r + D0)
                            nc.vector.tensor_copy(BD[rs_, h, rs_], ps[rs_, 2 + h, VW * r:VW * r + D0])
                            last = nc.vector.tensor_copy(BD[rs_, h, P + r:P + r + 1],
                                                         ps[rs_, 2 + h, VW * r + D0:VW * r + VW])
                    last.then_inc(bd_done, 1)
                    dve.wait_ge(bd_hi, b + 1)
                    nc.vector.tensor_tensor(BDl[:], BD[:], f32(BDh[:]), ALU.subtract).then_inc(bd_lo, 1)
                elif kind == "nd":
                    t, = at
                    dve.wait_ge(nd_filled, t + 1)
                    if t % TPG == 0 and t >= 2 * TPG:
                        dve.wait_ge(xT_filled, CH * (turn(("OT", t // TPG - 2)) + 1))
                    nd = ps[:, 5, 0:CH * NW].rearrange("p (h n) -> p h n", h=CH)
                    wait(dve, o_norm, t)
                    link(nc.vector.tensor_scalar(rd[:, 0, :, :], nd[:, :, P:NW], EPS_A, None, ALU.add))
                    link(nc.vector.reciprocal(rd[:, 1, :, :], rd[:, 0, :, :]))
                    nc.vector.tensor_tensor(
                        on[:, t % (2 * TPG), :].rearrange("p (h r d) -> p h r d", h=CH, r=HPH),
                        nd[:, :, 0:P].rearrange("p h (r d) -> p h r d", r=HPH),
                        rd[:, 1, :, :].rearrange("p h (r a) -> p h r a", a=1).to_broadcast([P, CH, HPH, D0]),
                        ALU.mult).then_inc(o_norm, 1)
                elif kind == "pr":
                    i, = at
                    t = 2 * i
                    dve.wait_ge(pr_filled, i + 1)
                    nc.vector.tensor_tensor(x[:, t:t + 2, :], ps[:, 4, :].rearrange("p (t c) -> p t c", t=2),
                                            x[:, t:t + 2, :], ALU.add).then_inc(x1_added, 1)
                elif kind == "H":
                    k, g, e, f = at
                    u = unit_of(k, g, e)
                    i = FT * u + f
                    hf, hh, hl = FF[k]
                    if f == 0:
                        wait(dve, y_filled[k], 2 * (u - 1))
                        buffers_free(dve, k, u)
                    dve.wait_ge(h_act[k], i + 1)
                    nc.vector.tensor_copy(hh[u % 2][:, f, :], hf[:, i % 2, :]).then_inc(h_hi[k], 1)
                elif kind == "mk":
                    g, = at
                    dve.wait_ge(gate_filled, g + 1)
                    lg = ps[:, 5, 0:4 * TPG].rearrange("p (t e) -> p t e", e=4)
                    t0 = g * TPG
                    link(nc.vector.tensor_copy(mask[:, t0:t0 + TPG, :], lg[:, :, 0:2]))
                    link(nc.vector.tensor_tensor(mask[:, t0:t0 + TPG, :], mask[:, t0:t0 + TPG, :], lg[:, :, 2:4], ALU.add))
                    l0, l1 = mask[:, t0:t0 + TPG, 0], mask[:, t0:t0 + TPG, 1]
                    link(nc.vector.tensor_tensor(l0, l0, l1, ALU.is_ge))
                    nc.vector.tensor_scalar(l1, l0, -1.0, 1.0, ALU.mult, ALU.add).then_inc(mask_ready, 1)
                    dve.wait_ge(mask_ready, g + 1)
                    for m in range(2):
                        for t in range(t0, t0 + TPG):
                            last = nc.vector.scalar_tensor_tensor(x[:, t, :], rows0[:, 1 + m, :], mask[:, t, m:m + 1],
                                                                  x[:, t, :], ALU.mult, ALU.add)
                        link(last)
                elif kind == "Y":
                    k, g, e, q = at
                    u = unit_of(k, g, e)
                    t = g * TPG + 2 * q
                    wait(dve, y_added[k], 2 * (u - 1) + q + 1)
                    dve.wait_ge(y_filled[k], 2 * u + q + 1)
                    if k == 1:
                        nc.vector.scalar_tensor_tensor(x[:, t, :], ps[:, 2 + q, 0:C], mask[:, t, e:e + 1], x[:, t, :],
                                                       ALU.mult, ALU.add)
                        nc.vector.scalar_tensor_tensor(x[:, t + 1, :], ps[:, 2 + q, C:2 * C],
                                                       mask[:, t + 1, e:e + 1], x[:, t + 1, :],
                                                       ALU.mult, ALU.add).then_inc(y_added[k], 1)
                    else:
                        nc.vector.tensor_tensor(x[:, t:t + 2, :], ps[:, 2 + q, :].rearrange("p (t c) -> p t c", t=2),
                                                x[:, t:t + 2, :], ALU.add).then_inc(y_added[k], 1)
                elif kind == "R" and at[1] % 2 == 0:
                    b = at[1] // 2
                    dve.wait_ge(h_filled[1], FT * (unit_of(1, 2 * b + 1, 1) + 1))
                    one = onesf[:, 0:TB].rearrange("p (t a) -> p t a", a=1)
                    link(nc.vector.tensor_copy(xrh[b][:, :, C:C + 1], one))
                    link(nc.vector.tensor_scalar(xrh[b][:, :, C + 1:XW], one, 0.0, None, ALU.mult))
                    nc.vector.tensor_scalar(xrl[b][:, :, C:XW], onesf[:, 0:2 * TB].rearrange("p (t a) -> p t a", a=2), 0.0,
                                            None, ALU.mult).then_inc(xr_one, 1)
                elif kind == "ev":
                    b, = at
                    dve.wait_ge(gr_filled, b + 1)
                    for c in range(CH):
                        i = 2 * (CH * b + c)
                        dve.wait_ge(gr_hi, i + 1)
                        nc.vector.tensor_tensor(Gl[:, b, c, :], ps[:, gram_bank(b) + c, 0:C], f32(Gh[:, b, c, :]),
                                                ALU.subtract).then_inc(gr_lo, 1)
                        nc.vector.tensor_copy(sx[:, c, b:b + 1], ps[:, gram_bank(b) + c, C:C + 1]).then_inc(sx_ready, 1)
                        dve.wait_ge(gr_hi, i + 2)
                        nc.vector.tensor_tensor(Rl[:, c, :, b, :],
                                                ps[:, gram_bank(b) + 2 + c, :].rearrange("p (s c) -> p s c", s=2),
                                                f32(Rh[:, c, :, b, :]), ALU.subtract).then_inc(gr_lo, 1)
                    if b == B - 1:
                        dve.wait_ge(sx_hi, 1)
                        nc.vector.tensor_tensor(sxl[:], sx[:].rearrange("p c (b a) -> p c b a", a=1).to_broadcast([P, CH, B, P]),
                                                f32(sxh[:]), ALU.subtract).then_inc(sx_lo, 1)
                elif kind == "kb":
                    Q, i = at
                    if Q == 0 and i == 0:
                        dve.wait_ge(bk_in, 16)
                    dve.wait_ge(b_filled, KB * Q + i + 1)
                    row = bkr[:, Q * 512:(Q + 1) * 512]
                    bank = ps[:, key_bank(Q, i), :]
                    if i >= B * CH:
                        wait(dve, s_ready, 2 * Q)
                        nc.vector.scalar_tensor_tensor(ksum[:, i - B * CH, :], row, float(T), bank, ALU.mult,
                                                       ALU.add).then_inc(b_taken, 1)
                    else:
                        n = B * CH * Q + i
                        b, c = i // CH, i % CH
                        wait(dve, b_lo, n - 1)
                        nc.vector.scalar_tensor_tensor(Bf[:, n % 2, :], row, sx[:, c, b:b + 1], bank, ALU.mult,
                                                       ALU.add).then_inc(b_taken, 1)
                elif kind == "s":
                    Q, a = at
                    n = 2 * Q + a
                    dve.wait_ge(s_filled, n + 1)
                    dve.wait_ge(b_taken, KB * (Q + 1))
                    wait(dve, t_filled, n - 1)
                    for h in (2 * a, 2 * a + 1):
                        last = nc.vector.scalar_tensor_tensor(
                            S[:, h, :, :], ksum[:, :, h * D1:(h + 1) * D1], bqcs[:, Q * QH + h:Q * QH + h + 1],
                            ps[:, 2 + a, h % 2 * B * D1:(h % 2 + 1) * B * D1].rearrange("p (b n) -> p b n", b=B),
                            ALU.mult, ALU.add)
                    last.then_inc(s_ready, 1)
                    hs = slice(2 * a, 2 * a + 2)
                    dve.wait_ge(s_ready, n + 1)
                    nc.vector.reduce_max(mx[:, hs, :], S[:, hs, :, :], AX.X).then_inc(s_max, 1)
                    dve.wait_ge(s_max, n + 1)
                    nc.vector.tensor_scalar(nmx[:, hs, :], mx[:, hs, :], -SCALE, None, ALU.mult).then_inc(s_neg, 1)
                elif kind == "p":
                    Q, a = at
                    n = 2 * Q + a
                    hs = slice(2 * a, 2 * a + 2)
                    dve.wait_ge(e_ready, 2 * B * (n + 1))
                    nc.vector.reciprocal(rs[:, hs, :], ssum[:, hs, :]).then_inc(r_ready, 1)
                    dve.wait_ge(r_ready, n + 1)
                    nc.vector.tensor_tensor(S[:, hs, :, :], S[:, hs, :, :],
                                            rs[:, hs, :].rearrange("p h (b a) -> p h b a", a=1).to_broadcast([P, 2, B, D1]),
                                            ALU.mult).then_inc(p_ready, 1)
                elif kind == "z":
                    Q, h = at
                    n = QH * Q + h
                    if n == 0:
                        dve.wait_ge(ws_read, 1)
                    dve.wait_ge(z_filled, n + 1)
                    wait(dve, z_lo, n - 1)
                    nc.vector.scalar_tensor_tensor(Zf[:, n % 2, :].rearrange("p (b c) -> p b c", b=B),
                                                   wosum[:, h % 2:h % 2 + 1, :].to_broadcast([P, B, C]), bvcs[:, n:n + 1],
                                                   ps[:, 4 + n % 2, :].rearrange("p (b c) -> p b c", b=B),
                                                   ALU.mult, ALU.add).then_inc(z_ready, 1)
                elif kind == "t":
                    Q, a = at
                    dve.wait_ge(pt_hi, 2 * Q + a + 1)
                    nc.vector.tensor_tensor(PTl[:, a, :, :, :], ps[:, 6 + a, :].rearrange("p (h b q) -> p h b q", h=2, b=B),
                                            f32(PTh[:, a, :, :, :]), ALU.subtract).then_inc(pt_lo, 1)
                elif kind == "o":
                    Q, a = at
                    dve.wait_ge(o_filled, 2 * Q + a + 1)
                    xs = x[:].rearrange("p (b t) c -> p b t c", b=B)[:, :, 2 * Q + a, :]
                    nc.vector.tensor_tensor(xs, ps[:, 6 + a, :].rearrange("p (b c) -> p b c", b=B), xs,
                                            ALU.add).then_inc(o_added, 1)
                elif kind == "fs":
                    dve.wait_ge(f_sum, 1)
                    link(nc.vector.reduce_sum(thr[:], ps[:, 4, 0:4].rearrange("p (i j) -> p i j", j=2), AX.X))
                    link(nc.vector.tensor_scalar(thr[:], thr[:], 1.0 / (C * F1), 1e-8, ALU.mult, ALU.max))
                    link(nc.vector.tensor_scalar(thr[:], thr[:], 0.5, None, ALU.mult))
                    nc.vector.tensor_scalar(nthr[:], thr[:], -1.0, None, ALU.mult).then_inc(thr_ready, 1)
                elif kind == "ft":
                    j, = at
                    if j == 0:
                        dve.wait_ge(thr_ready, 1)
                    i, part = j // FT, slice(j % FT * G, (j % FT + 1) * G)
                    r, t = ((f1raw, f1t), (f2raw, f2t))[i]
                    r, t = (m[:].rearrange("p a b -> p (a b)")[:, part] for m in (r, t))
                    wait(dve, f_tern, j - FT + 1)
                    link(nc.vector.tensor_scalar(neg[:, part], r, nthr[:, i:i + 1], None, ALU.is_lt))
                    nc.vector.scalar_tensor_tensor(t, r, thr[:, i:i + 1], neg[:, part], ALU.is_gt,
                                                   ALU.subtract).then_inc(f_tern, 1)

        @block.tensor
        def _(pe):
            mm = nc.tensor.matmul

            def product(dst, terms):
                for i, (a, b) in enumerate(terms):
                    last = mm(dst, a, b, start=(i == 0), stop=(i == len(terms) - 1))
                return last

            def three(ah, al, bh, bl):
                return [(ah, bh), (ah, bl), (al, bh)]

            def x_tile(t):
                s = slice(t % TB * P, (t % TB + 1) * P)
                return [(xTh[t // TB][:, c, s], xTl[t // TB][:, c, s]) for c in range(CH)]

            pe.wait_ge(id_in, 16)
            pe.wait_ge(ones_set, 3)
            for item in PLAN:
                kind, *at = item
                if kind in ("T", "OT"):
                    n = turn(item)
                    if kind == "T":
                        pe.wait_ge(xn_ready, TPG * (earlier("N", ("N", *at)) + 1))
                        src, r = xn, slot(*at)
                        wait(pe, o_added, earlier("o", item))
                    else:
                        pe.wait_ge(o_norm, TPG * (at[0] + 1))
                        src, r = on, at[0] % 2
                    for c in range(CH):
                        wait(pe, xT_lo, CH * (n - 1) + c + 1)
                        for t in range(TPG):
                            last = nc.tensor.transpose(ps[:, 6 + c, t * P:(t + 1) * P],
                                                       src[:, r * TPG + t, c * P:(c + 1) * P], ident[:])
                        last.then_inc(xT_filled, 1)
                elif kind == "kv":
                    i, = at
                    if i == 0:
                        pe.wait_ge(w0_lo["qkv"], 1)
                    if i % TPG == 0:
                        pe.wait_ge(xT_lo, CH * (turn(("T", 0, i // TPG)) + 1))
                    wait(pe, kv_lo, i - 1)
                    terms = []
                    for c, (xh_, xl_) in enumerate(x_tile(i)):
                        terms += three(xh_, xl_, wh0["qkv"][:, c, C:3 * C], wl0["qkv"][:, c, C:3 * C])
                    product(ps[:, i % 2, :], terms).then_inc(kv_filled, 1)
                elif kind == "vk":
                    i, = at
                    t = i % TB
                    pe.wait_ge(kv_lo, i + 1)
                    if t == 0:
                        wait(pe, bd_done, i // TB)
                    for h in range(CH):
                        ks, vs = slice(h * P, (h + 1) * P), slice(h * HPH, (h + 1) * HPH)
                        terms = three(Kh[:, i % 2, ks], Kl[:, i % 2, ks], Vh0[:, i % 2, vs, :], Vl0[:, i % 2, vs, :])
                        for n, (a, v) in enumerate(terms):
                            last = mm(ps[:, 2 + h, 0:HPH * VW], a, v.rearrange("p h d -> p (h d)"),
                                      start=(t == 0 and n == 0), stop=(t == TB - 1 and n == 2))
                    last.then_inc(kv_used, 1)
                elif kind == "q":
                    i, = at
                    b, h, ch = i // 4, i % 4 // 2, i % 2
                    wait(pe, q_lo, i)
                    wait(pe, x1_added, earlier("pr", item))
                    if i % 4 == 0 and b:
                        pe.wait_ge(o_norm, TB * b)
                    if h == 0:
                        pe.wait_ge(xT_lo, CH * (turn(("T", 0, 2 * b + ch)) + 1))
                    terms = []
                    for c in range(CH):
                        ws, s = slice(h * P, (h + 1) * P), slice(ch * G, (ch + 1) * G)
                        terms += three(wh0["qkv"][:, c, ws], wl0["qkv"][:, c, ws], xTh[b][:, c, s], xTl[b][:, c, s])
                    product(ps[:, 4, :], terms).then_inc(q_filled, 1)
                elif kind == "nd":
                    t, = at
                    if t % TB == 0:
                        pe.wait_ge(bd_lo, t // TB + 1)
                        pe.wait_ge(q_lo, 4 * (t // TB + 1))
                    wait(pe, o_norm, t)
                    wait(pe, mask_ready, earlier("gate", item))
                    s = slice(t % TB * P, (t % TB + 1) * P)
                    for h in range(CH):
                        last = product(ps[:, 5, h * NW:(h + 1) * NW], three(Qh[:, h, s], Ql[:, h, s],
                                                                           BDh[:, h, :], BDl[:, h, :]))
                    last.then_inc(nd_filled, 1)
                elif kind == "pr":
                    i, = at
                    if i == 0:
                        pe.wait_ge(w0_lo["proj"], 1)
                    pe.wait_ge(xT_lo, CH * (turn(("OT", i // 2)) + 1))
                    pe.wait_ge(q_lo, earlier("q", item))
                    wait(pe, x1_added, i)
                    for tt in range(2):
                        s = slice((2 * (i % 2) + tt) * P, (2 * (i % 2) + tt + 1) * P)
                        terms = []
                        for h in range(CH):
                            terms += three(Oh[:, h, s], Ol[:, h, s], wh0["proj"][:, h, :], wl0["proj"][:, h, :])
                        last = product(ps[:, 4, tt * C:(tt + 1) * C], terms)
                    last.then_inc(pr_filled, 1)
                elif kind == "gate":
                    g, = at
                    if g == 0:
                        pe.wait_ge(w0_lo["wg"], 1)
                    pe.wait_ge(xT_lo, CH * (turn(("T", 1, g)) + 1))
                    wait(pe, o_norm, earlier("nd", item))
                    wait(pe, mask_ready, g)
                    for t in range(TPG):
                        terms = []
                        for c, (xh_, xl_) in enumerate(x_tile(g * TPG + t)):
                            terms += [(xh_, wgp[:, c, :]), (xl_, wgp[:, c, :])]
                        last = product(ps[:, 5, 4 * t:4 * t + 4], terms)
                    last.then_inc(gate_filled, 1)
                elif kind == "H":
                    k, g, e, f = at
                    u = unit_of(k, g, e)
                    i = FT * u + f
                    pe.wait_ge(xT_lo, CH * (turn(("T", k, g)) + 1))
                    if u < 2 and f == 0:
                        if k == 1:
                            pe.wait_ge(w0_lo[("w0a", "w1a")[e]], 1)
                            pe.wait_ge(kv_lo, NT)
                        else:
                            pe.wait_ge(f_tern, 2 * FT)
                            pe.wait_ge(b_taken, KB * QUADS)
                    wait(pe, h_act[k], i - 1)
                    terms = []
                    for c in range(CH):
                        xh_, xl_ = xTh[g // 2][:, c, span(g)], xTl[g // 2][:, c, span(g)]
                        if k == 1:
                            w, fs = ("w0a", "w1a")[e], slice(f * P, (f + 1) * P)
                            terms += three(wh0[w][:, c, fs], wl0[w][:, c, fs], xh_, xl_)
                        else:
                            fs = slice((FT * e + f) * P, (FT * e + f + 1) * P)
                            terms += [(f1t[:, c, fs], xh_), (f1t[:, c, fs], xl_)]
                    product(ps[:, i % 2, :], terms).then_inc(h_filled[k], 1)
                elif kind == "Y":
                    k, g, e, q = at
                    u = unit_of(k, g, e)
                    hf, hh, hl = FF[k]
                    pe.wait_ge(h_lo[k], FT * (u + 1))
                    if u < 2 and q == 0:
                        if k == 1:
                            pe.wait_ge(w0_lo[("w0b", "w1b")[e]], 1)
                            pe.wait_ge(bd_done, B)
                        else:
                            pe.wait_ge(s_ready, 2 * QUADS)
                    wait(pe, y_added[k], 2 * (u - 1) + q + 1)
                    for tt in range(2):
                        ts = slice((2 * q + tt) * P, (2 * q + tt + 1) * P)
                        terms = []
                        for f in range(FT):
                            a, l = hh[u % 2][:, f, ts], hl[u % 2][:, f, ts]
                            if k == 1:
                                w = ("w0b", "w1b")[e]
                                terms += three(a, l, wh0[w][:, f, :], wl0[w][:, f, :])
                            else:
                                w = f2t[:, FT * e + f, :]
                                terms += [(a, w), (l, w)]
                        last = product(ps[:, 2 + q, tt * C:(tt + 1) * C], terms)
                    last.then_inc(y_filled[k], 1)
                elif kind == "ws":
                    pe.wait_ge(wo_lo, TB)
                    pe.wait_ge(x1_added, NT // 2)
                    terms = []
                    for t in range(TB):
                        terms += [(ones[:], woh[:, t, :]), (ones[:], wol[:, t, :])]
                    product(ps[:, 4, :], terms).then_inc(ws_filled, 1)
                elif kind == "gr":
                    g, = at
                    b = g // 2
                    pe.wait_ge(xr_lo, g + 1)
                    pe.wait_ge(xr_one, b + 1)
                    if g == 0:
                        pe.wait_ge(ws_read, 1)
                        pe.wait_ge(mask_ready, NG)
                        pe.wait_ge(xT_lo, CH * (turn(("T", 1, NG - 1)) + 1))
                    if g == 2:
                        pe.wait_ge(h_act[1], FT * UNITS)
                        pe.wait_ge(y_added[1], 2 * UNITS)
                    for t in range(g * TPG, (g + 1) * TPG):
                        i = t % TB
                        for c in range(CH):
                            cs = slice(c * P, (c + 1) * P)
                            for bank, rh, rl, w in ((gram_bank(b) + c, xrh[b][:, i, :], xrl[b][:, i, :], XW),
                                                    (gram_bank(b) + 2 + c, woh[:, i, :], wol[:, i, :], 2 * C)):
                                for n, (a, r) in enumerate(three(xrh[b][:, i, cs], xrl[b][:, i, cs], rh, rl)):
                                    last = mm(ps[:, bank, 0:w], a, r, start=(i == 0 and n == 0),
                                              stop=(i == TB - 1 and n == 2))
                    if g % 2:
                        last.then_inc(gr_filled, 1)
                elif kind == "kb":
                    Q, i = at
                    n = KB * Q + i
                    if Q == 0:
                        pe.wait_ge(gr_lo, 2 * CH * (1 if i < CH else B))
                    if i == 0:
                        pe.wait_ge(w_lo["k"], Q + 1)
                    if n == B * CH:
                        pe.wait_ge(sx_lo, 1)
                    wait(pe, b_taken, n - 1)
                    terms = []
                    for c in range(CH):
                        if i >= B * CH:
                            a = (sxh[:, c, i - B * CH, :], sxl[:, c, i - B * CH, :])
                        else:
                            b, cs = i // CH, slice(i % CH * P, (i % CH + 1) * P)
                            a = (Gh[:, b, c, cs], Gl[:, b, c, cs])
                        terms += three(*a, wh["k"][:, c, :], wl["k"][:, c, :])
                    product(ps[:, key_bank(Q, i), :], terms).then_inc(b_filled, 1)
                elif kind == "s":
                    Q, a = at
                    n = 2 * Q + a
                    pe.wait_ge(b_lo, B * CH * (Q + 1))
                    pe.wait_ge(w_lo["q"], Q + 1)
                    wait(pe, s_ready, n - 1)
                    for h in (2 * a, 2 * a + 1):
                        hs = slice(h * D1, (h + 1) * D1)
                        terms = []
                        for c in range(CH):
                            terms += three(wh["q"][:, c, hs], wl["q"][:, c, hs], Bh[:, :, c, hs], Bl[:, :, c, hs])
                        last = product(ps[:, 2 + a, h % 2 * B * D1:(h % 2 + 1) * B * D1], terms)
                    last.then_inc(s_filled, 1)
                elif kind == "z":
                    Q, h = at
                    n = QH * Q + h
                    pe.wait_ge(w_lo["v"], Q + 1)
                    wait(pe, z_ready, n - 1)
                    wait(pe, thr_ready, earlier("fs", item))
                    hs = slice(h * D1, (h + 1) * D1)
                    terms = []
                    for c in range(CH):
                        r = [m[:, c, h % 2, :, :].rearrange("p b c -> p (b c)") for m in (Rh, Rl)]
                        terms += three(wh["v"][:, c, hs], wl["v"][:, c, hs], *r)
                    product(ps[:, 4 + n % 2, :], terms).then_inc(z_filled, 1)
                elif kind == "t":
                    Q, a = at
                    n = 2 * Q + a
                    pe.wait_ge(p_ready, n + 1)
                    wait(pe, o_added, n - 1)
                    wait(pe, xT_lo, CH * turn(item))
                    for i in range(2 * B):
                        last = nc.tensor.transpose(ps[:, 6 + a, i * D1:(i + 1) * D1], S[:, 2 * a + i // B, i % B, :], ident[:])
                    last.then_inc(t_filled, 1)
                elif kind == "o":
                    Q, a = at
                    pe.wait_ge(z_lo, QH * Q + 2 * a + 2)
                    pe.wait_ge(pt_lo, 2 * Q + a + 1)
                    for b in range(B):
                        terms = []
                        for i in range(2):
                            terms += three(PTh[:, a, i, b, :], PTl[:, a, i, b, :], Zh[:, 2 * a + i, b, :], Zl[:, 2 * a + i, b, :])
                        last = product(ps[:, 6 + a, b * C:(b + 1) * C], terms)
                    last.then_inc(o_filled, 1)
                elif kind == "fs":
                    pe.wait_ge(f_abs, 4)
                    pe.wait_ge(z_ready, earlier("z", item))
                    mm(ps[:, 4, 0:4], onesf[:], asum[:], start=True, stop=True).then_inc(f_sum, 1)


def kernel(**inputs):
    import numpy as np
    import concourse.bacc as bacc
    from concourse.bass_utils import run_bass_kernel_spmd

    a = {k: np.asarray(v) for k, v in inputs.items()}
    heads = lambda w: w.reshape(C, D1, H1).transpose(0, 2, 1).reshape(C, H1 * D1)
    columns = lambda v: v.reshape(-1, P).T
    arrays = {
        "x": a["L0_attn_x"],
        "wqkv": a["L0_attn_w_qkv"].T, "wproj": a["L0_attn_w_proj"].T, "bproj": a["L0_attn_b_proj"],
        "wg": a["L0_ffn_Wg"].T,
        "w0a": a["L0_ffn_W0a"].T, "b0a": columns(a["L0_ffn_b0a"]), "w0b": a["L0_ffn_W0b"].T, "b0b": a["L0_ffn_b0b"],
        "w1a": a["L0_ffn_W1a"].T, "b1a": columns(a["L0_ffn_b1a"]), "w1b": a["L0_ffn_W1b"].T, "b1b": a["L0_ffn_b1b"],
        "wq": heads(a["L1_attn_Wq"]), "wk": heads(a["L1_attn_Wk"]), "wv": heads(a["L1_attn_Wv"]), "wo": a["L1_attn_Wo"],
        "bk": a["L1_attn_bk"].reshape(D1, H1).T.reshape(-1),
        "bqc": a["L1_attn_bq"].reshape(D1, H1), "bvc": a["L1_attn_bv"].reshape(D1, H1), "bo": a["L1_attn_bo"],
        "f1": a["L1_ffn_w1"].T, "fb1": columns(a["L1_ffn_b1"]), "f2": a["L1_ffn_w2"].T, "fb2": a["L1_ffn_b2"],
        "ident": np.eye(P, dtype=np.float32),
    }
    nc = bacc.Bacc("TRN2", target_bir_lowering=False, num_devices=1)
    data, args = {}, []
    for name, v in arrays.items():
        data[f"in_{name}"] = np.ascontiguousarray(v)
        args.append(nc.dram_tensor(f"in_{name}", v.shape, mybir.dt.from_np(v.dtype), kind="ExternalInput").ap())
    args.append(nc.dram_tensor("out", (B, T, C), F32, kind="ExternalOutput").ap())
    transformer(nc, *args)
    return run_bass_kernel_spmd(nc, [data], core_ids=[0]).results[0]["out"]
```

```python
from contextlib import ExitStack

import concourse.bass as bass
from concourse import mybir
from concourse.alu_op_type import AluOpType as ALU

ACT = mybir.ActivationFunctionType
AX = mybir.AxisListType
F32 = mybir.dt.float32
F32R = mybir.dt.float32r


P = 128
B, T, C = 2, 1024, 256
TB = T // P
NT = B * TB
CH = C // P
G = 512
NG = B * T // G
TPG = G // P
EPS_LN = 1e-5

H0, D0 = 8, 32
HPH = P // D0
VW = D0 + 1
NW = P + HPH
EPS_A = 1e-15

H1, D1 = 16, 128
SCALE = float(D1) ** -0.5
QH = 4
QUADS = H1 // QH
KB = B * CH + B
XW = C + 2

F0, F1 = 512, 1024
FT = 4
UNITS = 2 * NG

ORDER = """
# Batch 0: LayerNorm, keys and values, their products; queries.
S.0.0 W.qkv N.0.0 S.0.1 T.0.0 kv.0 N.0.1 kv.1 B.0.0 vk.0 S.0.2 T.0.1 kv.2 vk.1 q.0 kv.3 vk.2 kv.4 N.0.2 vk.3 B.0.1
kv.5 B.0.2 S.0.3 q.1 kv.6 q.2 vk.4 vk.5 kv.7 T.0.2 vk.6 vk.7 bd.0 q.3
# Batch 1's keys and values, with batch 0's numerators and projections between them.
kv.8 kv.9 W.proj nd.0 vk.8 W.wg N.0.3 kv.10 nd.1 vk.9 W.w0a B.0.3 T.0.3 kv.11 nd.2 vk.10 kv.12 W.w0b vk.11 nd.3
kv.13 OT.0 nd.4 kv.14 vk.12 pr.0 nd.5 W.w1a W.w1b pr.1 vk.13 vk.14 S.1.0 nd.6 kv.15 N.1.0 nd.7 T.1.0 q.4 q.5 OT.1
q.6 q.7 vk.15 bd.1
# The experts, with batch 1's attention between their first stages, then Wo's parts and LayerNorm 2.
H.1.0.0.0 pr.2 H.1.0.0.1 gate.0 mk.0 H.1.0.0.2 pr.3 nd.8 S.1.1 H.1.0.0.3 nd.9 H.1.0.1.0 nd.10 N.1.1 H.1.0.1.1 nd.11
H.1.0.1.2 OT.2 nd.12 H.1.0.1.3 pr.4 nd.13 T.1.1 mb.0 Y.1.0.0.0 nd.14 Y.1.0.0.1 pr.5 nd.15 H.1.1.0.0 OT.3 gate.1
H.1.1.0.1 H.1.1.0.2 S.1.2 pr.6 mk.1 Y.1.0.1.0 N.1.2 mb.1 wo.0 H.1.1.0.3 pr.7 H.1.1.1.0 Y.1.0.1.1 T.1.2 H.1.1.1.1
wo.1 Y.1.1.0.0 wo.2 H.1.1.1.2 H.1.1.1.3 gate.2 mk.2 S.1.3 H.1.2.0.0 N.1.3 wo.3 Y.1.1.0.1 Y.1.1.1.0 S.2.0 H.1.2.0.1
H.1.2.0.2 T.1.3 Y.1.1.1.1 H.1.2.0.3 wo.4 mb.2 H.1.2.1.0 gate.3 wo.5 N.2.0 H.1.2.1.1 B.2.0 S.2.1 H.1.2.1.2 H.1.2.1.3
Y.1.2.0.0 N.2.1 H.1.3.0.0 Y.1.2.0.1 H.1.3.0.1 R.2.0 wo.6 H.1.3.0.2 Y.1.2.1.0 mk.3 H.1.3.0.3 mb.3 wo.7 B.2.1
H.1.3.1.0 R.2.1 H.1.3.1.1 Y.1.2.1.1 S.2.2 H.1.3.1.2 N.2.2 H.1.3.1.3 ws Y.1.3.0.0 R.2.2 Y.1.3.0.1 Y.1.3.1.0 Y.1.3.1.1
S.2.3
# Gram matrices and x^T Wo; the first quad's keys.
gr.0 B.2.2 N.2.3 B.2.3 gr.1 qw.k.0 R.2.3 evG.0 qw.v.0 qw.q.0 evR.0 gr.2 gr.3 evG.1 kb.0.0 kb.0.1 kb.0.2 kb.0.3
kb.0.4 evR.1 qw.k.1 fa.0 kb.0.5 fa.1
# Quad 0, with the sums for the ternary weights' scales.
s.0.0 qw.q.1 s.0.1 p.0.0 kb.1.0 z.0.0 fa.2 kb.1.1 z.0.1 p.0.1 kb.1.2 z.0.2 t.0.0 z.0.3 fa.3 kb.1.3 t.0.1 o.0.0
qw.v.1 kb.1.4 fs kb.1.5 qw.k.2 o.0.1
# Quad 1, with ternary weights.
s.1.0 qw.q.2 s.1.1 p.1.0 z.1.0 kb.2.0 z.1.1 kb.2.1 p.1.1 ft.0 t.1.0 z.1.2 ft.1 kb.2.2 z.1.3 kb.2.3 o.1.0 kb.2.4 ft.2
qw.v.2 kb.2.5 qw.k.3 t.1.1 qw.q.3 ft.3
# Quad 2, with LayerNorm 3 of the first group.
s.2.0 o.1.1 s.2.1 z.2.0 kb.3.0 p.2.0 z.2.1 p.2.1 kb.3.1 S.3.0 t.2.0 z.2.2 kb.3.2 ft.4 t.2.1 kb.3.3 o.2.0 z.2.3
qw.v.3 N.3.0 kb.3.4 kb.3.5 T.3.0 ft.5 o.2.1
# Quad 3, with the last part's first hidden tiles.
s.3.0 s.3.1 z.3.0 p.3.0 z.3.1 t.3.0 p.3.1 H.3.0.0.0 z.3.2 z.3.3 ft.6 t.3.1 H.3.0.0.1 H.3.0.0.2 S.3.2 H.3.0.0.3 ft.7
o.3.0
# The last feed-forward part.
H.3.0.1.0 o.3.1 H.3.0.1.1 B.3.0 N.3.2 H.3.0.1.2 H.3.0.1.3 T.3.2 Y.3.0.0.0 B.3.2 Y.3.0.0.1 H.3.2.0.0 S.3.1 H.3.2.0.1
Y.3.0.1.0 H.3.2.0.2 N.3.1 H.3.2.0.3 Y.3.0.1.1 H.3.2.1.0 T.3.1 H.3.2.1.1 H.3.2.1.2 S.3.3 Y.3.2.0.0 H.3.2.1.3 B.3.1
H.3.1.0.0 Y.3.2.0.1 N.3.3 H.3.1.0.1 Y.3.2.1.0 H.3.1.0.2 H.3.1.0.3 Y.3.2.1.1 H.3.1.1.0 H.3.1.1.1 T.3.3 H.3.1.1.2
H.3.1.1.3 Y.3.1.0.0 H.3.3.0.0 B.3.3 Y.3.1.0.1 H.3.3.0.1 H.3.3.0.2 Y.3.1.1.0 H.3.3.0.3 H.3.3.1.0 Y.3.1.1.1 H.3.3.1.1
H.3.3.1.2 H.3.3.1.3 Y.3.3.0.0 Y.3.3.0.1 Y.3.3.1.0 Y.3.3.1.1
"""


def stages(order):
    words = " ".join(line for line in order.splitlines() if not line.startswith("#")).split()
    return [tuple(int(v) if v.isdigit() else v for v in word.split(".")) for word in words]


PLAN = stages(ORDER)
assert len(set(PLAN)) == len(PLAN)
assert [i[1:] for i in PLAN if i[0] == "S"] == [i[1:] for i in PLAN if i[0] == "N"]
AT = {item: n for n, item in enumerate(PLAN)}


def earlier(kind, item, **fixed):
    return sum(1 for n in PLAN[:AT[item]] if n[0] == kind and all(n[int(k[1:])] == v for k, v in fixed.items()))


def turn(item):
    return earlier("T", item) + earlier("OT", item)


def transformer(nc, x_in, wqkv, wproj, bproj, wg, w0a, b0a, w0b, b0b, w1a, b1a, w1b, b1b,
                wq, wk, wv, wo, bk, bqc, bvc, bo, f1, fb1, f2, fb2, ident_in, out):
    with ExitStack() as ctx:
        def place(name, shape, dt, at):
            where = (at[0] + 31) // 32 * 32
            size = 4
            for n in shape[1:]:
                size *= n
            at[0] = where + size
            return nc.alloc_sbuf_tensor_at(name, shape, dt, offset=where)

        def sem(name):
            return ctx.enter_context(nc.semaphore(name))

        top = [nc.sbuf_base]
        x = place("x", [P, NT, C], F32, top)
        xTh, xTl, xrh, xrl = [], [], [], []
        for b in range(B):
            for name, tr, rows in (("h", xTh, xrh), ("l", xTl, xrl)):
                tr.append(place(f"xT{name}{b}", [P, CH, T], F32R, [top[0]]))
                rows.append(place(f"xr{name}{b}", [P, TB, XW], F32R, top))
        ident = place("ident", [P, P], F32, top)
        ones = place("ones", [P, P], F32R, top)
        onesf = place("onesf", [P, P], F32, top)
        mhalf = place("mhalf", [P, TPG], F32, top)
        stats = place("stats", [P, TPG, 6], F32, top)
        mv = place("mv", [P, 2, TPG, 2], F32, top)
        vare = place("vare", [P, 2, TPG], F32, top)
        rstd = place("rstd", [P, 2, TPG], F32, top)
        b0as = place("b0as", [P, FT], F32, top)
        b1as = place("b1as", [P, FT], F32, top)
        fb1s = place("fb1s", [P, F1 // P], F32, top)
        bqcs = place("bqcs", [P, H1], F32, top)
        bvcs = place("bvcs", [P, H1], F32, top)
        rows1 = place("rows1", [P, 2, C], F32, top)
        sx = place("sx", [P, CH, B], F32, top)
        asum = place("asum", [P, 4], F32, top)
        thr = place("thr", [P, 2], F32, top)
        nthr = place("nthr", [P, 2], F32, top)
        mx = place("mx", [P, QH, B], F32, top)
        nmx = place("nmx", [P, QH, B], F32, top)
        ssum = place("ssum", [P, QH, B], F32, top)
        rs = place("rs", [P, QH, B], F32, top)
        end = nc.sbuf_usable_end // 32 * 32 - 2 * TPG * C * 4
        xn = place("xn", [P, 2 * TPG, C], F32, [end])

        wshape = {"qkv": [P, 2, 3 * C], "proj": [P, 2, C], "w0a": [P, 2, F0], "w1a": [P, 2, F0],
                  "w0b": [P, 4, C], "w1b": [P, 4, C]}
        low = [top[0]]
        wh0, wl0 = {}, {}
        for k, s in wshape.items():
            wh0[k], wl0[k] = place(f"{k}_h", s, F32R, low), place(f"{k}_l", s, F32R, low)
        wgs = place("wgs", [P, CH, 2], F32, low)
        wgp = place("wgp", [P, CH, 4], F32R, low)
        mask = place("mask", [P, NT, 2], F32, low)
        rows0 = place("rows0", [P, 3, C], F32, low)
        rd = place("rd", [P, 2, CH, HPH], F32, low)

        def ffn_buffers(tag, at):
            hf, hh, hl = place(f"hf{tag}", [P, 2, G], F32, at), [], []
            for e in range(2):
                hh.append(place(f"hh{tag}{e}", [P, FT, G], F32R, at))
                hl.append(place(f"hl{tag}{e}", [P, FT, G], F32R, at))
            return hf, hh, hl

        raw_at = [low[0]]
        raw0 = {k: place(f"{k}_raw", s, F32, raw_at) for k, s in wshape.items()}
        mid = [low[0]]
        ff0 = ffn_buffers("0", mid)
        mid[0] = max(mid[0], raw_at[0])
        lin = [mid[0]]
        Kh = place("Kh", [P, 2, C], F32R, lin)
        Kl = place("Kl", [P, 2, C], F32R, lin)
        V0 = place("V0", [P, 2, 2, H0, VW], F32R, lin)
        Qh = place("Qh", [P, CH, T], F32R, lin)
        Ql = place("Ql", [P, CH, T], F32R, lin)
        BD = place("BD", [P, CH, NW], F32, lin)
        BDh = place("BDh", [P, CH, NW], F32R, lin)
        BDl = place("BDl", [P, CH, NW], F32R, lin)
        on = place("on", [P, 2 * TPG, C], F32, lin)
        Oh = place("Oh", [P, CH, G], F32R, lin)
        Ol = place("Ol", [P, CH, G], F32R, lin)
        woraw = place("woraw", [P, TB, 2 * C], F32, lin)
        assert lin[0] <= end, (lin[0], end)

        up = [mid[0]]
        woh = place("woh", [P, TB, 2 * C], F32R, up)
        wol = place("wol", [P, TB, 2 * C], F32R, up)
        Gh = place("Gh", [P, B, CH, C], F32R, up)
        Gl = place("Gl", [P, B, CH, C], F32R, up)
        Rh = place("Rh", [P, CH, 2, B, C], F32R, up)
        Rl = place("Rl", [P, CH, 2, B, C], F32R, up)
        wosum = place("wosum", [P, 2, C], F32, up)
        sxh = place("sxh", [P, CH, B, P], F32R, up)
        assert up[0] <= end, (up[0], end)
        ovr = [mid[0]]
        S = place("S", [P, QH, B, D1], F32, ovr)
        PTh = place("PTh", [P, 2, 2, B, D1], F32R, ovr)
        PTl = place("PTl", [P, 2, 2, B, D1], F32R, ovr)
        Zf = place("Zf", [P, 2, 2 * C], F32, ovr)
        Zh = place("Zh", [P, QH, B, C], F32R, ovr)
        Zl = place("Zl", [P, QH, B, C], F32R, ovr)
        assert ovr[0] <= mid[0] + 2 * 4 * TB * 2 * C
        att = [top[0]]
        raw = {k: place(f"raw{k}", [P, CH, 512], F32, att) for k in "kqv"}
        assert att[0] <= top[0] + 4 * 16 * C
        wh, wl = {}, {}
        for k in "kqv":
            wh[k], wl[k] = place(f"wh{k}", [P, CH, 512], F32R, att), place(f"wl{k}", [P, CH, 512], F32R, att)
        bkr = place("bkr", [P, H1 * D1], F32, att)
        sxl = place("sxl", [P, CH, B, P], F32R, att)
        ksum = place("ksum", [P, B, 512], F32, att)
        Bf = place("Bf", [P, 2, 512], F32, att)
        Bh = place("Bh", [P, B, CH, 512], F32R, att)
        Bl = place("Bl", [P, B, CH, 512], F32R, att)
        assert att[0] <= mid[0], (att[0], mid[0])
        fr = [nc.sbuf_base + 4 * NT * C + 8 * TB * XW]
        f1raw = place("f1raw", [P, CH, F1], F32, fr)
        f2raw = place("f2raw", [P, F1 // P, C], F32, fr)
        assert fr[0] <= nc.sbuf_base + 4 * NT * C + 16 * TB * XW
        neg = place("neg", [P, F1], F32, [end + 4 * TPG * C])
        fw = [mid[0] - 2 * 8 * F1 - 64]
        f1t = place("f1t", [P, CH, F1], F32R, fw)
        f2t = place("f2t", [P, F1 // P, C], F32R, fw)
        assert att[0] <= mid[0] - 2 * 8 * F1 - 64 and fw[0] <= mid[0], (att[0], mid[0])
        ff1_at = [top[0]]
        ff1 = ffn_buffers("1", ff1_at)
        assert ff1_at[0] <= mid[0] - 2 * 8 * F1 - 64
        FF = {1: ff0, 3: ff1}

        ps = ctx.enter_context(nc.psum_tensor("ps", [P, 8, 512], F32))

        x_in_s = [sem(f"x_loaded{g}") for g in range(NG)]
        x_rest, wq0_in = sem("x_loaded0_rest"), sem("wq0_loaded")
        id_in, cst_in = sem("identity_loaded"), sem("constants_loaded")
        w0_in = {k: sem(f"{k}_loaded") for k in wshape}
        w0_hi = {k: sem(f"{k}_hi") for k in (*wshape, "wg")}
        w0_lo = {k: sem(f"{k}_lo") for k in (*wshape, "wg")}
        ones_set = sem("ones_set")
        dve_chain = sem("dve_chain")
        var_ready, rstd_ready, xn_ready = sem("var_ready"), sem("rstd_ready"), sem("xn_ready")
        xT_filled, xT_hi, xT_lo = sem("xT_filled"), sem("xT_hi"), sem("xT_lo")
        kv_filled, kv_hi, kv_lo, kv_used = sem("kv_filled"), sem("kv_hi"), sem("kv_lo"), sem("kv_used")
        q_filled, q_hi, q_lo = sem("q_filled"), sem("q_hi"), sem("q_lo")
        bd_done, bd_hi, bd_lo = sem("bd_done"), sem("bd_hi"), sem("bd_lo")
        nd_filled, o_norm = sem("nd_filled"), sem("o_norm")
        pr_filled, x1_added = sem("proj_filled"), sem("x1_added")
        gate_filled, mask_ready = sem("gate_filled"), sem("mask_ready")
        biased = sem("biased")
        h_filled = {k: sem(f"h_filled{k}") for k in FF}
        h_act = {k: sem(f"h_activated{k}") for k in FF}
        h_hi = {k: sem(f"h_hi{k}") for k in FF}
        h_lo = {k: sem(f"h_lo{k}") for k in FF}
        y_filled = {k: sem(f"y_filled{k}") for k in FF}
        y_added = {k: sem(f"y_added{k}") for k in FF}
        f_in, f_abs, f_sum, f_tern = sem("ffn_loaded"), sem("f_abs"), sem("f_sum"), sem("f_ternary")
        thr_ready = sem("thr_ready")
        stored = sem("stored")
        wo_in, bk_in, wo_hi, wo_lo = sem("wo_loaded"), sem("bk_loaded"), sem("wo_hi"), sem("wo_lo")
        xr_hi, xr_lo, xr_one = sem("rows_hi"), sem("rows_lo"), sem("rows_ones")
        ws_filled, ws_read = sem("wosum_filled"), sem("wosum_read")
        gr_filled, gr_hi, gr_lo = sem("gram_filled"), sem("gram_hi"), sem("gram_lo")
        sx_ready, sx_hi, sx_lo = sem("sx_ready"), sem("sx_hi"), sem("sx_lo")
        raw_in = {k: sem(f"raw{k}_loaded") for k in "qkv"}
        w_hi = {k: sem(f"w{k}_hi") for k in "qkv"}
        w_lo = {k: sem(f"w{k}_lo") for k in "qkv"}
        b_filled, b_taken, b_hi, b_lo = sem("b_filled"), sem("b_taken"), sem("b_hi"), sem("b_lo")
        s_filled, s_ready, s_max, s_neg = sem("s_filled"), sem("s_ready"), sem("s_max"), sem("s_neg")
        e_ready, r_ready, p_ready = sem("exp_ready"), sem("rsum_ready"), sem("p_ready")
        t_filled, pt_hi, pt_lo = sem("t_filled"), sem("pt_hi"), sem("pt_lo")
        z_filled, z_ready, z_hi, z_lo = sem("z_filled"), sem("z_ready"), sem("z_hi"), sem("z_lo")
        o_filled, o_added = sem("o_filled"), sem("o_added")

        def wait(eng, s, v):
            if v > 0:
                eng.wait_ge(s, v)

        def f32(ap):
            return ap.bitcast(F32)

        def x_final(k, g):
            if k == 0:
                return x_in_s[g], 16
            if k == 1:
                return x1_added, 2 * (g + 1)
            if k == 2:
                return y_added[1], 2 * (unit_of(1, g, 1) + 1)
            return o_added, QUADS * (1 + g % 2)

        def unit_of(k, g, e):
            return earlier("H", ("H", k, g, e, 0), _1=k) // FT

        def ring_free(k, g):
            n = earlier("N", ("N", k, g)) - 2
            if n < 0:
                return xn_ready, 0
            k2, g2 = [i[1:] for i in PLAN if i[0] == "N"][n]
            if k2 == 2:
                return xr_lo, g2 + 1
            return xT_filled, CH * (turn(("T", k2, g2)) + 1)

        def buffers_free(eng, k, u):
            if k == 1 and u == 0:
                for w in wshape:
                    eng.wait_ge(w0_lo[w], 2 if w == "qkv" else 1)
            if k == 3 and u == 0:
                for w in "kqv":
                    eng.wait_ge(w_lo[w], QUADS)
                eng.wait_ge(b_filled, KB * QUADS)
            if k == 3 and u == 1:
                eng.wait_ge(s_filled, 2 * QUADS)
                eng.wait_ge(z_filled, QH * QUADS)

        def bias_turn(k, g):
            return earlier("B", ("B", k, g)) + 1

        def slot(k, g):
            return earlier("N", ("N", k, g)) % 2

        def span(g):
            return slice(g % 2 * G, (g % 2 + 1) * G)

        def gram_bank(b):
            return 4 if b == 0 else 0

        def turn_bank(item):
            return 2 if item == ("T", 3, 0) else 6

        def key_bank(Q, i):
            return (6 if Q == 0 else 0) + i % 2

        block = ctx.enter_context(nc.Block())

        @block.sync
        def _(sp):
            xv = x_in.rearrange("b (p t) c -> p b t c", p=P)

            def load_x(g):
                sp.dma_start(x[:, g * TPG:(g + 1) * TPG, :],
                             xv[:, g // 2, g % 2 * TPG:(g % 2 + 1) * TPG, :]).then_inc(x_in_s[g], 16)

            for half in range(2):
                tiles = slice(half * 2, half * 2 + 2)
                sp.dma_start(x[:, tiles, :], xv[:, 0, tiles, :]).then_inc((x_in_s[0], x_rest)[half], 16)
            sp.dma_start(ident[:], ident_in).then_inc(id_in, 16)
            wqkv_v = wqkv.rearrange("(c p) n -> p c n", p=P)
            sp.dma_start(raw0["qkv"][:, :, C:], wqkv_v[:, :, C:]).then_inc(w0_in["qkv"], 16)
            load_x(1)
            sp.dma_start(raw0["qkv"][:, :, 0:C], wqkv_v[:, :, 0:C]).then_inc(wq0_in, 16)
            sp.dma_start(rows0[:, 0, :], bproj.partition_broadcast(P)).then_inc(cst_in, 16)
            load_x(2)
            load_x(3)
            sp.dma_start(raw0["proj"][:], wproj.rearrange("(c p) n -> p c n", p=P)).then_inc(w0_in["proj"], 16)
            sp.dma_start(wgs[:], wg.rearrange("(c p) n -> p c n", p=P)).then_inc(cst_in, 16)
            for dst, src in ((b0as[:], b0a), (b1as[:], b1a), (fb1s[:], fb1), (bqcs[:], bqc), (bvcs[:], bvc),
                             (rows0[:, 1, :], b0b.partition_broadcast(P)), (rows0[:, 2, :], b1b.partition_broadcast(P)),
                             (rows1[:, 0, :], bo.partition_broadcast(P)), (rows1[:, 1, :], fb2.partition_broadcast(P))):
                sp.dma_start(dst, src).then_inc(cst_in, 16)
            for k, src in (("w0a", w0a), ("w0b", w0b), ("w1a", w1a), ("w1b", w1b)):
                sp.dma_start(raw0[k][:], src.rearrange("(c p) n -> p c n", p=P)).then_inc(w0_in[k], 16)
            wov = wo.rearrange("(s p t) n -> p t s n", s=2, p=P)
            for s in range(2):
                sp.dma_start(woraw[:, :, s * C:(s + 1) * C], wov[:, :, s, :]).then_inc(wo_in, 16)

            def load_quad(k, Q):
                w = {"q": wq, "k": wk, "v": wv}[k]
                wait(sp, w_lo[k], Q)
                sp.dma_start(raw[k][:], w.rearrange("(c p) n -> p c n", p=P)[:, :, Q * 512:(Q + 1) * 512])\
                  .then_inc(raw_in[k], 16)

            sp.wait_ge(pr_filled, NT // 2)
            for k in "kqv":
                load_quad(k, 0)
            sp.wait_ge(y_filled[1], 2 * UNITS)
            sp.dma_start(bkr[:], bk.partition_broadcast(P)).then_inc(bk_in, 16)
            sp.wait_ge(gr_filled, B)
            sp.dma_start(f1raw[:], f1.rearrange("(c p) n -> p c n", p=P)).then_inc(f_in, 16)
            sp.dma_start(f2raw[:], f2.rearrange("(c p) n -> p c n", p=P)).then_inc(f_in, 16)
            for Q in range(1, QUADS):
                for k in "kqv":
                    load_quad(k, Q)
            ov = out.rearrange("b (p t) c -> p b t c", p=P)
            for kind, *at in PLAN:
                if kind == "Y" and at[0] == 3 and at[2] == 1:
                    k, g, e, q = at
                    sp.wait_ge(y_added[3], 2 * unit_of(k, g, e) + q + 1)
                    t = g % 2 * TPG + 2 * q
                    sp.dma_start(ov[:, g // 2, t:t + 2, :], x[:, g // 2 * TB + t:g // 2 * TB + t + 2, :])\
                      .then_inc(stored, 16)
            sp.wait_ge(stored, 16 * 2 * NG)

        @block.gpsimd
        def _(pool):
            nc.gpsimd.memset(onesf[:], 1.0).then_inc(ones_set, 1)
            nc.gpsimd.memset(mhalf[:], -0.5).then_inc(ones_set, 1)
            pool.wait_ge(ones_set, 2)
            for item in PLAN:
                kind, *at = item
                if kind == "W":
                    k, = at
                    pool.wait_ge(w0_hi[k], 1)
                    if k == "wg":
                        nc.gpsimd.tensor_tensor(wgp[:, :, 2:4], wgs[:], f32(wgp[:, :, 0:2]),
                                                ALU.subtract).then_inc(w0_lo[k], 1)
                    elif k == "qkv":
                        for i, part in enumerate((slice(C, 3 * C), slice(0, C))):
                            pool.wait_ge(w0_hi[k], i + 1)
                            nc.gpsimd.tensor_tensor(wl0[k][:, :, part], raw0[k][:, :, part], f32(wh0[k][:, :, part]),
                                                    ALU.subtract).then_inc(w0_lo[k], 1)
                    else:
                        nc.gpsimd.tensor_tensor(wl0[k][:], raw0[k][:], f32(wh0[k][:]),
                                                ALU.subtract).then_inc(w0_lo[k], 1)
                elif kind == "S":
                    n = earlier("S", item)
                    pool.wait_ge(var_ready, n + 1)
                    nc.gpsimd.tensor_tensor(rstd[:, n % 2, :], vare[:, n % 2, :], mhalf[:],
                                            ALU.pow).then_inc(rstd_ready, 1)
                elif kind == "B":
                    k, g = at
                    n = earlier("N", ("N", k, g))
                    if n == 0:
                        pool.wait_ge(cst_in, 16 * 11)
                    pool.wait_ge(xn_ready, TPG * (n + 1))
                    row = {0: rows0[:, 0:1, :], 2: rows1[:, 0:1, :], 3: rows1[:, 1:2, :]}[k]
                    xs = x[:, g * TPG:(g + 1) * TPG, :]
                    nc.gpsimd.tensor_tensor(xs, xs, row.to_broadcast([P, TPG, C]), ALU.add).then_inc(biased, 1)
                elif kind == "H":
                    k, g, e, f = at
                    u = unit_of(k, g, e)
                    i = FT * u + f
                    hf, hh, hl = FF[k]
                    if f == 0:
                        wait(pool, y_filled[k], 2 * (u - 1))
                        buffers_free(pool, k, u)
                    pool.wait_ge(h_hi[k], i + 1)
                    nc.gpsimd.tensor_tensor(hl[u % 2][:, f, :], hf[:, i % 2, :], f32(hh[u % 2][:, f, :]),
                                            ALU.subtract).then_inc(h_lo[k], 1)
                elif kind == "wo":
                    t, = at
                    pool.wait_ge(wo_hi, t + 1)
                    nc.gpsimd.tensor_tensor(wol[:, t, :], woraw[:, t, :], f32(woh[:, t, :]),
                                            ALU.subtract).then_inc(wo_lo, 1)
                elif kind == "R":
                    k, g = at
                    n = slot(k, g)
                    tiles = slice(g % 2 * TPG, (g % 2 + 1) * TPG)
                    pool.wait_ge(xr_hi, g + 1)
                    nc.gpsimd.tensor_tensor(xrl[g // 2][:, tiles, 0:C], xn[:, n * TPG:(n + 1) * TPG, :],
                                            f32(xrh[g // 2][:, tiles, 0:C]), ALU.subtract).then_inc(xr_lo, 1)
                elif kind == "qw":
                    k, Q = at
                    pool.wait_ge(w_hi[k], Q + 1)
                    nc.gpsimd.tensor_tensor(wl[k][:], raw[k][:], f32(wh[k][:]), ALU.subtract).then_inc(w_lo[k], 1)
                elif kind == "kb" and at[1] < B * CH:
                    Q, i = at
                    n = B * CH * Q + i
                    b, c = i // CH, i % CH
                    pool.wait_ge(b_hi, n + 1)
                    nc.gpsimd.tensor_tensor(Bl[:, b, c, :], Bf[:, n % 2, :], f32(Bh[:, b, c, :]),
                                            ALU.subtract).then_inc(b_lo, 1)
                elif kind == "z":
                    Q, h = at
                    n = QH * Q + h
                    pool.wait_ge(z_hi, n + 1)
                    nc.gpsimd.tensor_tensor(Zl[:, h, :, :], Zf[:, n % 2, :].rearrange("p (b c) -> p b c", b=B),
                                            f32(Zh[:, h, :, :]), ALU.subtract).then_inc(z_lo, 1)

        @block.scalar
        def _(act):
            act.wait_ge(ones_set, 2)
            nc.scalar.activation(ones[:], onesf[:], ACT.Copy).then_inc(ones_set, 1)
            for item in PLAN:
                kind, *at = item
                if kind == "W":
                    k, = at
                    if k == "wg":
                        act.wait_ge(cst_in, 16 * 11)
                        nc.scalar.activation(wgp[:, :, 0:2], wgs[:], ACT.Copy).then_inc(w0_hi[k], 1)
                    elif k == "qkv":
                        for loaded, part in ((w0_in[k], slice(C, 3 * C)), (wq0_in, slice(0, C))):
                            act.wait_ge(loaded, 16)
                            nc.scalar.activation(wh0[k][:, :, part], raw0[k][:, :, part], ACT.Copy).then_inc(w0_hi[k], 1)
                    else:
                        act.wait_ge(w0_in[k], 16)
                        nc.scalar.activation(wh0[k][:], raw0[k][:], ACT.Copy).then_inc(w0_hi[k], 1)
                elif kind in ("T", "OT"):
                    n = turn(item)
                    for c in range(CH):
                        act.wait_ge(xT_filled, CH * n + c + 1)
                        if kind == "T":
                            k, g = at
                            if k == 3 and g // 2 == 1:
                                act.wait_ge(f_tern, 2 * FT)
                            dst = xTh[g // 2][:, c, span(g)]
                        else:
                            wait(act, pr_filled, 2 * at[0])
                            dst = Oh[:, c, :]
                        nc.scalar.activation(dst, ps[:, turn_bank(item) + c, :], ACT.Copy).then_inc(xT_hi, 1)
                elif kind == "kv":
                    i, = at
                    act.wait_ge(kv_filled, i + 1)
                    wait(act, kv_used, i - 1)
                    nc.scalar.activation(Kh[:, i % 2, :], ps[:, i % 2, 0:C], ACT.Relu)
                    nc.scalar.activation(V0[:, i % 2, 0, :, 0:D0],
                                         ps[:, i % 2, C:2 * C].rearrange("p (h d) -> p h d", d=D0),
                                         ACT.Copy).then_inc(kv_hi, 1)
                elif kind == "q":
                    i, = at
                    h, ch = i % 4 // 2, i % 2
                    act.wait_ge(q_filled, i + 1)
                    nc.scalar.activation(Qh[:, h, ch * G:(ch + 1) * G], ps[:, 4 + i % 2, :], ACT.Relu).then_inc(q_hi, 1)
                elif kind == "bd":
                    act.wait_ge(bd_done, at[0] + 1)
                    nc.scalar.activation(BDh[:], BD[:], ACT.Copy).then_inc(bd_hi, 1)
                elif kind == "H":
                    k, g, e, f = at
                    u = unit_of(k, g, e)
                    i = FT * u + f
                    hf, hh, hl = FF[k]
                    bias = (b0as, b1as)[e] if k == 1 else fb1s
                    func = ACT.Relu if k == 1 and e else ACT.Gelu
                    if f == 0:
                        buffers_free(act, k, u)
                    col = f if k == 1 else FT * e + f
                    act.wait_ge(h_filled[k], i + 1)
                    wait(act, h_lo[k], i - 1)
                    nc.scalar.activation(hf[:, i % 2, :], ps[:, i % 2, :], func,
                                         bias=bias[:, col:col + 1]).then_inc(h_act[k], 1)
                elif kind == "wo":
                    t, = at
                    act.wait_ge(pr_filled, NT // 2)
                    act.wait_ge(wo_in, 32)
                    nc.scalar.activation(woh[:, t, :], woraw[:, t, :], ACT.Copy).then_inc(wo_hi, 1)
                elif kind == "R":
                    k, g = at
                    n = slot(k, g)
                    act.wait_ge(xn_ready, TPG * (earlier("N", ("N", k, g)) + 1))
                    act.wait_ge(h_filled[1], FT * (unit_of(1, g // 2 * 2 + 1, 1) + 1))
                    nc.scalar.activation(xrh[g // 2][:, g % 2 * TPG:(g % 2 + 1) * TPG, 0:C],
                                         xn[:, n * TPG:(n + 1) * TPG, :], ACT.Copy).then_inc(xr_hi, 1)
                elif kind == "ws":
                    act.wait_ge(ws_filled, 1)
                    nc.scalar.activation(wosum[:], ps[:, 4, :].rearrange("p (s c) -> p s c", s=2),
                                         ACT.Copy).then_inc(ws_read, 1)
                elif kind == "evR":
                    b, = at
                    for c in range(CH):
                        nc.scalar.activation(Rh[:, c, :, b, :],
                                             ps[:, gram_bank(b) + 2 + c, :].rearrange("p (s c) -> p s c", s=2),
                                             ACT.Copy).then_inc(gr_hi, 1)
                elif kind == "evG":
                    b, = at
                    act.wait_ge(gr_filled, b + 1)
                    for c in range(CH):
                        nc.scalar.activation(Gh[:, b, c, :], ps[:, gram_bank(b) + c, 0:C], ACT.Copy).then_inc(gr_hi, 1)
                    if b == B - 1:
                        act.wait_ge(sx_ready, B * CH)
                        nc.scalar.activation(sxh[:], sx[:].rearrange("p c (b a) -> p c b a", a=1).to_broadcast([P, CH, B, P]),
                                             ACT.Copy).then_inc(sx_hi, 1)
                elif kind == "qw":
                    k, Q = at
                    act.wait_ge(raw_in[k], 16 * (Q + 1))
                    if Q == 0:
                        act.wait_ge(y_filled[1], 2 * UNITS)
                    used, n = {"q": (s_filled, 2 * Q), "k": (b_filled, KB * Q), "v": (z_filled, QH * Q)}[k]
                    wait(act, used, n)
                    nc.scalar.activation(wh[k][:], raw[k][:], ACT.Copy).then_inc(w_hi[k], 1)
                elif kind == "kb" and at[1] < B * CH:
                    Q, i = at
                    n = B * CH * Q + i
                    act.wait_ge(b_taken, KB * Q + i + 1)
                    wait(act, s_filled, 2 * Q)
                    nc.scalar.activation(Bh[:, i // CH, i % CH, :], Bf[:, n % 2, :], ACT.Copy).then_inc(b_hi, 1)
                elif kind == "s":
                    Q, a = at
                    act.wait_ge(s_neg, 2 * Q + a + 1)
                    for h in (2 * a, 2 * a + 1):
                        for b in range(B):
                            nc.scalar.activation(S[:, h, b, :], S[:, h, b, :], ACT.Exp, bias=nmx[:, h, b:b + 1],
                                                 scale=SCALE, accum_out=ssum[:, h, b:b + 1]).then_inc(e_ready, 1)
                elif kind == "z":
                    Q, h = at
                    n = QH * Q + h
                    act.wait_ge(z_ready, n + 1)
                    wait(act, o_filled, 2 * (Q - 1) + h // 2 + 1)
                    nc.scalar.activation(Zh[:, h, :, :], Zf[:, n % 2, :].rearrange("p (b c) -> p b c", b=B),
                                         ACT.Copy).then_inc(z_hi, 1)
                elif kind == "t":
                    Q, a = at
                    act.wait_ge(t_filled, 2 * Q + a + 1)
                    wait(act, o_filled, 2 * (Q - 1) + a + 1)
                    nc.scalar.activation(PTh[:, a, :, :, :], ps[:, 6 + a, :].rearrange("p (h b q) -> p h b q", h=2, b=B),
                                         ACT.Copy).then_inc(pt_hi, 1)
                elif kind == "fa":
                    j, = at
                    act.wait_ge(f_in, 32)
                    half = slice(j % 2 * F1, (j % 2 + 1) * F1)
                    wait(act, f_abs, j)
                    nc.scalar.activation(neg[:], (f1raw, f2raw)[j // 2][:].rearrange("p a b -> p (a b)")[:, half],
                                         ACT.Abs, accum_out=asum[:, j:j + 1]).then_inc(f_abs, 1)

        @block.vector
        def _(dve):
            chain = [0]

            def link(ins):
                chain[0] += 1
                ins.then_inc(dve_chain, 1)
                dve.wait_ge(dve_chain, chain[0])

            dve.wait_ge(ones_set, 2)
            for s in range(2):
                one = onesf[:, 0:H0].rearrange("p (h a) -> p h a", a=1)
                link(nc.vector.tensor_copy(V0[:, s, 0, :, D0:VW], one))
                link(nc.vector.tensor_scalar(V0[:, s, 1, :, D0:VW], one, 0.0, None, ALU.mult))
            link(nc.vector.memset(BD[:], 0.0))
            for item in PLAN:
                kind, *at = item
                if kind == "S":
                    k, g = at
                    n = earlier("S", item)
                    dve.wait_ge(*x_final(k, g))
                    for i in range(TPG):
                        if k == 0 and g == 0 and i == 2:
                            dve.wait_ge(x_rest, 16)
                        last = nc.vector.bn_stats(stats[:, i, :], x[:, g * TPG + i, :])
                    link(last)
                    for i in range(TPG):
                        last = nc.vector.bn_aggr(mv[:, n % 2, i, :], stats[:, i, :])
                    link(last)
                    wait(dve, rstd_ready, n - 1)
                    nc.vector.tensor_scalar(vare[:, n % 2, :], mv[:, n % 2, :, 1], EPS_LN, None,
                                            ALU.add).then_inc(var_ready, 1)
                elif kind == "N":
                    k, g = at
                    n = earlier("N", item)
                    dve.wait_ge(rstd_ready, n + 1)
                    wait(dve, *ring_free(k, g))
                    if k == 3 and slot(k, g) == 1:
                        dve.wait_ge(f_tern, 2 * FT)
                    for i in range(TPG):
                        nc.vector.tensor_scalar(xn[:, (n % 2) * TPG + i, :], x[:, g * TPG + i, :],
                                                mv[:, n % 2, i, 0:1], rstd[:, n % 2, i:i + 1],
                                                ALU.subtract, ALU.mult).then_inc(xn_ready, 1)
                elif kind in ("T", "OT"):
                    n = turn(item)
                    for c in range(CH):
                        dve.wait_ge(xT_hi, CH * n + c + 1)
                        if kind == "T":
                            hi, lo = (m[at[1] // 2][:, c, span(at[1])] for m in (xTh, xTl))
                        else:
                            hi, lo = Oh[:, c, :], Ol[:, c, :]
                        nc.vector.tensor_tensor(lo, ps[:, turn_bank(item) + c, :], f32(hi), ALU.subtract).then_inc(xT_lo, 1)
                elif kind == "kv":
                    i, = at
                    dve.wait_ge(kv_hi, i + 1)
                    nc.vector.scalar_tensor_tensor(Kl[:, i % 2, :], ps[:, i % 2, 0:C], 0.0, f32(Kh[:, i % 2, :]),
                                                   ALU.max, ALU.subtract)
                    nc.vector.tensor_tensor(V0[:, i % 2, 1, :, 0:D0],
                                            ps[:, i % 2, C:2 * C].rearrange("p (h d) -> p h d", d=D0),
                                            f32(V0[:, i % 2, 0, :, 0:D0]), ALU.subtract).then_inc(kv_lo, 1)
                elif kind == "q":
                    i, = at
                    h, ch = i % 4 // 2, i % 2
                    dve.wait_ge(q_hi, i + 1)
                    nc.vector.scalar_tensor_tensor(Ql[:, h, ch * G:(ch + 1) * G], ps[:, 4 + i % 2, :], 0.0,
                                                   f32(Qh[:, h, ch * G:(ch + 1) * G]),
                                                   ALU.max, ALU.subtract).then_inc(q_lo, 1)
                elif kind == "bd":
                    b, = at
                    dve.wait_ge(kv_used, TB * (b + 1))
                    wait(dve, bd_lo, b)
                    for h in range(CH):
                        for r in range(HPH):
                            rs_ = slice(D0 * r, D0 * r + D0)
                            nc.vector.tensor_copy(BD[rs_, h, rs_], ps[rs_, 2 + h, VW * r:VW * r + D0])
                            last = nc.vector.tensor_copy(BD[rs_, h, P + r:P + r + 1],
                                                         ps[rs_, 2 + h, VW * r + D0:VW * r + VW])
                    link(last)
                    for h in range(CH):
                        for r in range(HPH):
                            rs_, lo = slice(D0 * r, D0 * r + D0), HPH * VW + VW * r
                            last = nc.vector.tensor_tensor(BD[rs_, h, rs_], BD[rs_, h, rs_], ps[rs_, 2 + h, lo:lo + D0],
                                                           ALU.add)
                    last.then_inc(bd_done, 1)
                    dve.wait_ge(bd_hi, b + 1)
                    nc.vector.tensor_tensor(BDl[:], BD[:], f32(BDh[:]), ALU.subtract).then_inc(bd_lo, 1)
                elif kind == "nd":
                    t, = at
                    dve.wait_ge(nd_filled, t + 1)
                    if t % TPG == 0 and t >= 2 * TPG:
                        dve.wait_ge(xT_filled, CH * (turn(("OT", t // TPG - 2)) + 1))
                    nd = ps[:, 5, 0:CH * NW].rearrange("p (h n) -> p h n", h=CH)
                    wait(dve, o_norm, t)
                    link(nc.vector.tensor_scalar(rd[:, 0, :, :], nd[:, :, P:NW], EPS_A, None, ALU.add))
                    link(nc.vector.reciprocal(rd[:, 1, :, :], rd[:, 0, :, :]))
                    nc.vector.tensor_tensor(
                        on[:, t % (2 * TPG), :].rearrange("p (h r d) -> p h r d", h=CH, r=HPH),
                        nd[:, :, 0:P].rearrange("p h (r d) -> p h r d", r=HPH),
                        rd[:, 1, :, :].rearrange("p h (r a) -> p h r a", a=1).to_broadcast([P, CH, HPH, D0]),
                        ALU.mult).then_inc(o_norm, 1)
                elif kind == "pr":
                    i, = at
                    t = 2 * i
                    dve.wait_ge(biased, bias_turn(0, i // 2))
                    dve.wait_ge(pr_filled, i + 1)
                    nc.vector.tensor_tensor(x[:, t:t + 2, :], ps[:, 4, :].rearrange("p (t c) -> p t c", t=2),
                                            x[:, t:t + 2, :], ALU.add).then_inc(x1_added, 1)
                elif kind == "H":
                    k, g, e, f = at
                    u = unit_of(k, g, e)
                    i = FT * u + f
                    hf, hh, hl = FF[k]
                    if f == 0:
                        wait(dve, y_filled[k], 2 * (u - 1))
                        buffers_free(dve, k, u)
                    dve.wait_ge(h_act[k], i + 1)
                    nc.vector.tensor_copy(hh[u % 2][:, f, :], hf[:, i % 2, :]).then_inc(h_hi[k], 1)
                elif kind == "mk":
                    g, = at
                    dve.wait_ge(gate_filled, g + 1)
                    lg = ps[:, 5, 0:4 * TPG].rearrange("p (t e) -> p t e", e=4)
                    t0 = g * TPG
                    link(nc.vector.tensor_copy(mask[:, t0:t0 + TPG, :], lg[:, :, 0:2]))
                    link(nc.vector.tensor_tensor(mask[:, t0:t0 + TPG, :], mask[:, t0:t0 + TPG, :], lg[:, :, 2:4], ALU.add))
                    l0, l1 = mask[:, t0:t0 + TPG, 0], mask[:, t0:t0 + TPG, 1]
                    link(nc.vector.tensor_tensor(l0, l0, l1, ALU.is_ge))
                    nc.vector.tensor_scalar(l1, l0, -1.0, 1.0, ALU.mult, ALU.add).then_inc(mask_ready, 1)
                elif kind == "mb":
                    g, = at
                    dve.wait_ge(mask_ready, g + 1)
                    for m in range(2):
                        for t in range(g * TPG, (g + 1) * TPG):
                            last = nc.vector.scalar_tensor_tensor(x[:, t, :], rows0[:, 1 + m, :], mask[:, t, m:m + 1],
                                                                  x[:, t, :], ALU.mult, ALU.add)
                        link(last)
                elif kind == "Y":
                    k, g, e, q = at
                    u = unit_of(k, g, e)
                    t = g * TPG + 2 * q
                    wait(dve, y_added[k], 2 * (u - 1) + q + 1)
                    dve.wait_ge(y_filled[k], 2 * u + q + 1)
                    if k != 1:
                        dve.wait_ge(biased, bias_turn(k, g))
                    if k == 1:
                        nc.vector.scalar_tensor_tensor(x[:, t, :], ps[:, 2 + q, 0:C], mask[:, t, e:e + 1], x[:, t, :],
                                                       ALU.mult, ALU.add)
                        nc.vector.scalar_tensor_tensor(x[:, t + 1, :], ps[:, 2 + q, C:2 * C],
                                                       mask[:, t + 1, e:e + 1], x[:, t + 1, :],
                                                       ALU.mult, ALU.add).then_inc(y_added[k], 1)
                    else:
                        nc.vector.tensor_tensor(x[:, t:t + 2, :], ps[:, 2 + q, :].rearrange("p (t c) -> p t c", t=2),
                                                x[:, t:t + 2, :], ALU.add).then_inc(y_added[k], 1)
                elif kind == "R" and at[1] % 2 == 0:
                    b = at[1] // 2
                    dve.wait_ge(h_filled[1], FT * (unit_of(1, 2 * b + 1, 1) + 1))
                    one = onesf[:, 0:TB].rearrange("p (t a) -> p t a", a=1)
                    link(nc.vector.tensor_copy(xrh[b][:, :, C:C + 1], one))
                    link(nc.vector.tensor_scalar(xrh[b][:, :, C + 1:XW], one, 0.0, None, ALU.mult))
                    nc.vector.tensor_scalar(xrl[b][:, :, C:XW], onesf[:, 0:2 * TB].rearrange("p (t a) -> p t a", a=2), 0.0,
                                            None, ALU.mult).then_inc(xr_one, 1)
                elif kind == "evR":
                    b, = at
                    for c in range(CH):
                        dve.wait_ge(gr_hi, 2 * CH * b + CH + c + 1)
                        nc.vector.tensor_tensor(Rl[:, c, :, b, :],
                                                ps[:, gram_bank(b) + 2 + c, :].rearrange("p (s c) -> p s c", s=2),
                                                f32(Rh[:, c, :, b, :]), ALU.subtract).then_inc(gr_lo, 1)
                elif kind == "evG":
                    b, = at
                    dve.wait_ge(gr_filled, b + 1)
                    for c in range(CH):
                        dve.wait_ge(gr_hi, 2 * CH * b + c + 1)
                        nc.vector.tensor_copy(sx[:, c, b:b + 1], ps[:, gram_bank(b) + c, C:C + 1]).then_inc(sx_ready, 1)
                        nc.vector.tensor_tensor(Gl[:, b, c, :], ps[:, gram_bank(b) + c, 0:C], f32(Gh[:, b, c, :]),
                                                ALU.subtract).then_inc(gr_lo, 1)
                    if b == B - 1:
                        dve.wait_ge(sx_hi, 1)
                        nc.vector.tensor_tensor(sxl[:], sx[:].rearrange("p c (b a) -> p c b a", a=1).to_broadcast([P, CH, B, P]),
                                                f32(sxh[:]), ALU.subtract).then_inc(sx_lo, 1)
                elif kind == "kb":
                    Q, i = at
                    if Q == 0 and i == 0:
                        dve.wait_ge(bk_in, 16)
                    dve.wait_ge(b_filled, KB * Q + i + 1)
                    row = bkr[:, Q * 512:(Q + 1) * 512]
                    bank = ps[:, key_bank(Q, i), :]
                    if i >= B * CH:
                        wait(dve, s_ready, 2 * Q)
                        nc.vector.scalar_tensor_tensor(ksum[:, i - B * CH, :], row, float(T), bank, ALU.mult,
                                                       ALU.add).then_inc(b_taken, 1)
                    else:
                        n = B * CH * Q + i
                        b, c = i // CH, i % CH
                        wait(dve, b_lo, n - 1)
                        nc.vector.scalar_tensor_tensor(Bf[:, n % 2, :], row, sx[:, c, b:b + 1], bank, ALU.mult,
                                                       ALU.add).then_inc(b_taken, 1)
                elif kind == "s":
                    Q, a = at
                    n = 2 * Q + a
                    dve.wait_ge(s_filled, n + 1)
                    dve.wait_ge(b_taken, KB * (Q + 1))
                    wait(dve, t_filled, n - 1)
                    for h in (2 * a, 2 * a + 1):
                        last = nc.vector.scalar_tensor_tensor(
                            S[:, h, :, :], ksum[:, :, h * D1:(h + 1) * D1], bqcs[:, Q * QH + h:Q * QH + h + 1],
                            ps[:, 2 + a, h % 2 * B * D1:(h % 2 + 1) * B * D1].rearrange("p (b n) -> p b n", b=B),
                            ALU.mult, ALU.add)
                    last.then_inc(s_ready, 1)
                    hs = slice(2 * a, 2 * a + 2)
                    dve.wait_ge(s_ready, n + 1)
                    nc.vector.reduce_max(mx[:, hs, :], S[:, hs, :, :], AX.X).then_inc(s_max, 1)
                    dve.wait_ge(s_max, n + 1)
                    nc.vector.tensor_scalar(nmx[:, hs, :], mx[:, hs, :], -SCALE, None, ALU.mult).then_inc(s_neg, 1)
                elif kind == "p":
                    Q, a = at
                    n = 2 * Q + a
                    hs = slice(2 * a, 2 * a + 2)
                    dve.wait_ge(e_ready, 2 * B * (n + 1))
                    nc.vector.reciprocal(rs[:, hs, :], ssum[:, hs, :]).then_inc(r_ready, 1)
                    dve.wait_ge(r_ready, n + 1)
                    nc.vector.tensor_tensor(S[:, hs, :, :], S[:, hs, :, :],
                                            rs[:, hs, :].rearrange("p h (b a) -> p h b a", a=1).to_broadcast([P, 2, B, D1]),
                                            ALU.mult).then_inc(p_ready, 1)
                elif kind == "z":
                    Q, h = at
                    n = QH * Q + h
                    if n == 0:
                        dve.wait_ge(ws_read, 1)
                    dve.wait_ge(z_filled, n + 1)
                    wait(dve, z_lo, n - 1)
                    nc.vector.scalar_tensor_tensor(Zf[:, n % 2, :].rearrange("p (b c) -> p b c", b=B),
                                                   wosum[:, h % 2:h % 2 + 1, :].to_broadcast([P, B, C]), bvcs[:, n:n + 1],
                                                   ps[:, 4 + n % 2, :].rearrange("p (b c) -> p b c", b=B),
                                                   ALU.mult, ALU.add).then_inc(z_ready, 1)
                elif kind == "t":
                    Q, a = at
                    dve.wait_ge(pt_hi, 2 * Q + a + 1)
                    nc.vector.tensor_tensor(PTl[:, a, :, :, :], ps[:, 6 + a, :].rearrange("p (h b q) -> p h b q", h=2, b=B),
                                            f32(PTh[:, a, :, :, :]), ALU.subtract).then_inc(pt_lo, 1)
                elif kind == "o":
                    Q, a = at
                    if Q == 0:
                        dve.wait_ge(biased, bias_turn(2, NG - 1))
                    dve.wait_ge(o_filled, 2 * Q + a + 1)
                    xs = x[:].rearrange("p (b t) c -> p b t c", b=B)[:, :, 2 * Q + a, :]
                    nc.vector.tensor_tensor(xs, ps[:, 6 + a, :].rearrange("p (b c) -> p b c", b=B), xs,
                                            ALU.add).then_inc(o_added, 1)
                elif kind == "fs":
                    dve.wait_ge(f_sum, 1)
                    link(nc.vector.reduce_sum(thr[:], ps[:, 4, 0:4].rearrange("p (i j) -> p i j", j=2), AX.X))
                    link(nc.vector.tensor_scalar(thr[:], thr[:], 1.0 / (C * F1), 1e-8, ALU.mult, ALU.max))
                    link(nc.vector.tensor_scalar(thr[:], thr[:], 0.5, None, ALU.mult))
                    nc.vector.tensor_scalar(nthr[:], thr[:], -1.0, None, ALU.mult).then_inc(thr_ready, 1)
                elif kind == "ft":
                    j, = at
                    if j == 0:
                        dve.wait_ge(thr_ready, 1)
                    i, part = j // FT, slice(j % FT * G, (j % FT + 1) * G)
                    r, t = ((f1raw, f1t), (f2raw, f2t))[i]
                    r, t = (m[:].rearrange("p a b -> p (a b)")[:, part] for m in (r, t))
                    below = neg[:, j % 2 * G:(j % 2 + 1) * G]
                    wait(dve, f_tern, j - 1)
                    link(nc.vector.tensor_scalar(below, r, nthr[:, i:i + 1], None, ALU.is_lt))
                    nc.vector.scalar_tensor_tensor(t, r, thr[:, i:i + 1], below, ALU.is_gt,
                                                   ALU.subtract).then_inc(f_tern, 1)

        @block.tensor
        def _(pe):
            mm = nc.tensor.matmul

            def product(dst, terms):
                for i, (a, b) in enumerate(terms):
                    last = mm(dst, a, b, start=(i == 0), stop=(i == len(terms) - 1))
                return last

            def three(ah, al, bh, bl):
                return [(ah, bh), (ah, bl), (al, bh)]

            def x_tile(t):
                s = slice(t % TB * P, (t % TB + 1) * P)
                return [(xTh[t // TB][:, c, s], xTl[t // TB][:, c, s]) for c in range(CH)]

            pe.wait_ge(id_in, 16)
            pe.wait_ge(ones_set, 3)
            for item in PLAN:
                kind, *at = item
                if kind in ("T", "OT"):
                    n = turn(item)
                    if kind == "T":
                        rows, done, src, r = xn_ready, TPG * earlier("N", ("N", *at)), xn, slot(*at)
                        wait(pe, s_ready, earlier("s", item))
                        wait(pe, o_added, earlier("o", item))
                    else:
                        rows, done, src, r = o_norm, TPG * at[0], on, at[0] % 2
                    for c in range(CH):
                        wait(pe, xT_lo, CH * (n - 1) + c + 1)
                        for t in range(TPG):
                            pe.wait_ge(rows, done + t + 1)
                            last = nc.tensor.transpose(ps[:, turn_bank(item) + c, t * P:(t + 1) * P],
                                                       src[:, r * TPG + t, c * P:(c + 1) * P], ident[:])
                        last.then_inc(xT_filled, 1)
                elif kind == "kv":
                    i, = at
                    if i == 0:
                        pe.wait_ge(w0_lo["qkv"], 1)
                    if i % TPG == 0:
                        pe.wait_ge(xT_lo, CH * (turn(("T", 0, i // TPG)) + 1))
                    wait(pe, kv_lo, i - 1)
                    terms = []
                    for c, (xh_, xl_) in enumerate(x_tile(i)):
                        terms += three(xh_, xl_, wh0["qkv"][:, c, C:3 * C], wl0["qkv"][:, c, C:3 * C])
                    product(ps[:, i % 2, :], terms).then_inc(kv_filled, 1)
                elif kind == "vk":
                    i, = at
                    t = i % TB
                    pe.wait_ge(kv_lo, i + 1)
                    if t == 0:
                        wait(pe, bd_done, i // TB)
                    for h in range(CH):
                        ks, vs = slice(h * P, (h + 1) * P), slice(h * HPH, (h + 1) * HPH)
                        mm(ps[:, 2 + h, 0:2 * HPH * VW], Kh[:, i % 2, ks],
                           V0[:, i % 2, :, vs, :].rearrange("p s h d -> p s (h d)"), start=(t == 0), stop=False)
                        last = mm(ps[:, 2 + h, 0:HPH * VW], Kl[:, i % 2, ks],
                                  V0[:, i % 2, 0, vs, :].rearrange("p h d -> p (h d)"), start=False, stop=(t == TB - 1))
                    last.then_inc(kv_used, 1)
                elif kind == "q":
                    i, = at
                    b, h, ch = i // 4, i % 4 // 2, i % 2
                    if i == 0:
                        pe.wait_ge(w0_lo["qkv"], 2)
                    wait(pe, q_lo, i - 1)
                    if i % 2 == 0:
                        wait(pe, x1_added, earlier("pr", item))
                    else:
                        wait(pe, o_norm, earlier("nd", item))
                        wait(pe, mask_ready, earlier("gate", item))
                    if i % 4 == 0 and b:
                        pe.wait_ge(o_norm, TB * b)
                    if h == 0:
                        pe.wait_ge(xT_lo, CH * (turn(("T", 0, 2 * b + ch)) + 1))
                    terms = []
                    for c in range(CH):
                        ws, s = slice(h * P, (h + 1) * P), slice(ch * G, (ch + 1) * G)
                        terms += three(wh0["qkv"][:, c, ws], wl0["qkv"][:, c, ws], xTh[b][:, c, s], xTl[b][:, c, s])
                    product(ps[:, 4 + i % 2, :], terms).then_inc(q_filled, 1)
                elif kind == "nd":
                    t, = at
                    if t % TB == 0:
                        pe.wait_ge(bd_lo, t // TB + 1)
                        pe.wait_ge(q_lo, 4 * (t // TB + 1))
                    wait(pe, o_norm, t)
                    wait(pe, mask_ready, earlier("gate", item))
                    s = slice(t % TB * P, (t % TB + 1) * P)
                    for h in range(CH):
                        last = product(ps[:, 5, h * NW:(h + 1) * NW], three(Qh[:, h, s], Ql[:, h, s],
                                                                           BDh[:, h, :], BDl[:, h, :]))
                    last.then_inc(nd_filled, 1)
                elif kind == "pr":
                    i, = at
                    if i == 0:
                        pe.wait_ge(w0_lo["proj"], 1)
                    pe.wait_ge(xT_lo, CH * (turn(("OT", i // 2)) + 1))
                    pe.wait_ge(q_lo, earlier("q", item))
                    wait(pe, x1_added, i)
                    for tt in range(2):
                        s = slice((2 * (i % 2) + tt) * P, (2 * (i % 2) + tt + 1) * P)
                        terms = []
                        for h in range(CH):
                            terms += three(Oh[:, h, s], Ol[:, h, s], wh0["proj"][:, h, :], wl0["proj"][:, h, :])
                        last = product(ps[:, 4, tt * C:(tt + 1) * C], terms)
                    last.then_inc(pr_filled, 1)
                elif kind == "gate":
                    g, = at
                    if g == 0:
                        pe.wait_ge(w0_lo["wg"], 1)
                    pe.wait_ge(xT_lo, CH * (turn(("T", 1, g)) + 1))
                    wait(pe, o_norm, earlier("nd", item))
                    wait(pe, q_lo, earlier("q", item))
                    wait(pe, mask_ready, g)
                    for t in range(TPG):
                        terms = []
                        for c, (xh_, xl_) in enumerate(x_tile(g * TPG + t)):
                            terms += [(xh_, wgp[:, c, :]), (xl_, wgp[:, c, :])]
                        last = product(ps[:, 5, 4 * t:4 * t + 4], terms)
                    last.then_inc(gate_filled, 1)
                elif kind == "H":
                    k, g, e, f = at
                    u = unit_of(k, g, e)
                    i = FT * u + f
                    pe.wait_ge(xT_lo, CH * (turn(("T", k, g)) + 1))
                    if u < 2 and f == 0:
                        if k == 1:
                            pe.wait_ge(w0_lo[("w0a", "w1a")[e]], 1)
                            pe.wait_ge(kv_lo, NT)
                        else:
                            pe.wait_ge(f_tern, FT)
                            pe.wait_ge(b_taken, KB * QUADS)
                    wait(pe, h_act[k], i - 1)
                    terms = []
                    for c in range(CH):
                        xh_, xl_ = xTh[g // 2][:, c, span(g)], xTl[g // 2][:, c, span(g)]
                        if k == 1:
                            w, fs = ("w0a", "w1a")[e], slice(f * P, (f + 1) * P)
                            terms += three(wh0[w][:, c, fs], wl0[w][:, c, fs], xh_, xl_)
                        else:
                            fs = slice((FT * e + f) * P, (FT * e + f + 1) * P)
                            terms += [(f1t[:, c, fs], xh_), (f1t[:, c, fs], xl_)]
                    product(ps[:, i % 2, :], terms).then_inc(h_filled[k], 1)
                elif kind == "Y":
                    k, g, e, q = at
                    u = unit_of(k, g, e)
                    hf, hh, hl = FF[k]
                    pe.wait_ge(h_lo[k], FT * (u + 1))
                    if u < 2 and q == 0:
                        if k == 1:
                            pe.wait_ge(w0_lo[("w0b", "w1b")[e]], 1)
                            pe.wait_ge(bd_done, B)
                        else:
                            pe.wait_ge(s_ready, 2 * QUADS)
                            pe.wait_ge(f_tern, 2 * FT)
                    wait(pe, y_added[k], 2 * (u - 1) + q + 1)
                    for tt in range(2):
                        ts = slice((2 * q + tt) * P, (2 * q + tt + 1) * P)
                        terms = []
                        for f in range(FT):
                            a, l = hh[u % 2][:, f, ts], hl[u % 2][:, f, ts]
                            if k == 1:
                                w = ("w0b", "w1b")[e]
                                terms += three(a, l, wh0[w][:, f, :], wl0[w][:, f, :])
                            else:
                                w = f2t[:, FT * e + f, :]
                                terms += [(a, w), (l, w)]
                        last = product(ps[:, 2 + q, tt * C:(tt + 1) * C], terms)
                    last.then_inc(y_filled[k], 1)
                elif kind == "ws":
                    pe.wait_ge(wo_lo, TB)
                    pe.wait_ge(x1_added, NT // 2)
                    terms = []
                    for t in range(TB):
                        terms += [(ones[:], woh[:, t, :]), (ones[:], wol[:, t, :])]
                    product(ps[:, 4, :], terms).then_inc(ws_filled, 1)
                elif kind == "gr":
                    g, = at
                    b = g // 2
                    pe.wait_ge(xr_lo, g + 1)
                    pe.wait_ge(xr_one, b + 1)
                    if g == 0:
                        pe.wait_ge(ws_read, 1)
                        pe.wait_ge(mask_ready, NG)
                        pe.wait_ge(xT_lo, CH * (turn(("T", 1, NG - 1)) + 1))
                    if g == 2:
                        pe.wait_ge(h_act[1], FT * UNITS)
                        pe.wait_ge(y_added[1], 2 * UNITS)
                    for t in range(g * TPG, (g + 1) * TPG):
                        i = t % TB
                        for c in range(CH):
                            cs = slice(c * P, (c + 1) * P)
                            for bank, rh, rl, w in ((gram_bank(b) + c, xrh[b][:, i, :], xrl[b][:, i, :], XW),
                                                    (gram_bank(b) + 2 + c, woh[:, i, :], wol[:, i, :], 2 * C)):
                                for n, (a, r) in enumerate(three(xrh[b][:, i, cs], xrl[b][:, i, cs], rh, rl)):
                                    last = mm(ps[:, bank, 0:w], a, r, start=(i == 0 and n == 0),
                                              stop=(i == TB - 1 and n == 2))
                    if g % 2:
                        last.then_inc(gr_filled, 1)
                elif kind == "kb":
                    Q, i = at
                    n = KB * Q + i
                    if Q == 0 and i < B * CH:
                        pe.wait_ge(gr_lo, 2 * CH if i < CH else 3 * CH)
                    if i == 0:
                        pe.wait_ge(w_lo["k"], Q + 1)
                    if n == B * CH:
                        pe.wait_ge(sx_lo, 1)
                    wait(pe, b_taken, n - 1)
                    terms = []
                    for c in range(CH):
                        if i >= B * CH:
                            a = (sxh[:, c, i - B * CH, :], sxl[:, c, i - B * CH, :])
                        else:
                            b, cs = i // CH, slice(i % CH * P, (i % CH + 1) * P)
                            a = (Gh[:, b, c, cs], Gl[:, b, c, cs])
                        terms += three(*a, wh["k"][:, c, :], wl["k"][:, c, :])
                    product(ps[:, key_bank(Q, i), :], terms).then_inc(b_filled, 1)
                elif kind == "s":
                    Q, a = at
                    n = 2 * Q + a
                    pe.wait_ge(b_lo, B * CH * (Q + 1))
                    pe.wait_ge(w_lo["q"], Q + 1)
                    pe.wait_ge(gr_lo, 2 * CH * B)
                    wait(pe, s_ready, n - 1)
                    wait(pe, xT_lo, CH * turn(item))
                    for h in (2 * a, 2 * a + 1):
                        hs = slice(h * D1, (h + 1) * D1)
                        terms = []
                        for c in range(CH):
                            terms += three(wh["q"][:, c, hs], wl["q"][:, c, hs], Bh[:, :, c, hs], Bl[:, :, c, hs])
                        last = product(ps[:, 2 + a, h % 2 * B * D1:(h % 2 + 1) * B * D1], terms)
                    last.then_inc(s_filled, 1)
                elif kind == "z":
                    Q, h = at
                    n = QH * Q + h
                    pe.wait_ge(w_lo["v"], Q + 1)
                    if n == 0:
                        pe.wait_ge(gr_lo, 2 * CH * B)
                    wait(pe, z_ready, n - 1)
                    wait(pe, thr_ready, earlier("fs", item))
                    hs = slice(h * D1, (h + 1) * D1)
                    terms = []
                    for c in range(CH):
                        r = [m[:, c, h % 2, :, :].rearrange("p b c -> p (b c)") for m in (Rh, Rl)]
                        terms += three(wh["v"][:, c, hs], wl["v"][:, c, hs], *r)
                    product(ps[:, 4 + n % 2, :], terms).then_inc(z_filled, 1)
                elif kind == "t":
                    Q, a = at
                    n = 2 * Q + a
                    pe.wait_ge(p_ready, n + 1)
                    wait(pe, o_added, n - 1)
                    wait(pe, xT_lo, CH * turn(item))
                    for i in range(2 * B):
                        last = nc.tensor.transpose(ps[:, 6 + a, i * D1:(i + 1) * D1], S[:, 2 * a + i // B, i % B, :], ident[:])
                    last.then_inc(t_filled, 1)
                elif kind == "o":
                    Q, a = at
                    pe.wait_ge(z_lo, QH * Q + 2 * a + 2)
                    pe.wait_ge(pt_lo, 2 * Q + a + 1)
                    for b in range(B):
                        terms = []
                        for i in range(2):
                            terms += three(PTh[:, a, i, b, :], PTl[:, a, i, b, :], Zh[:, 2 * a + i, b, :], Zl[:, 2 * a + i, b, :])
                        last = product(ps[:, 6 + a, b * C:(b + 1) * C], terms)
                    last.then_inc(o_filled, 1)
                elif kind == "fs":
                    pe.wait_ge(f_abs, 4)
                    pe.wait_ge(z_ready, (earlier("z", item) - 1) // 2 * 2 + 1)
                    mm(ps[:, 4, 0:4], onesf[:], asum[:], start=True, stop=True).then_inc(f_sum, 1)


def kernel(**inputs):
    import numpy as np
    import concourse.bacc as bacc
    from concourse.bass_utils import run_bass_kernel_spmd

    a = {k: np.asarray(v) for k, v in inputs.items()}
    heads = lambda w: w.reshape(C, D1, H1).transpose(0, 2, 1).reshape(C, H1 * D1)
    columns = lambda v: v.reshape(-1, P).T
    arrays = {
        "x": a["L0_attn_x"],
        "wqkv": a["L0_attn_w_qkv"].T, "wproj": a["L0_attn_w_proj"].T, "bproj": a["L0_attn_b_proj"],
        "wg": a["L0_ffn_Wg"].T,
        "w0a": a["L0_ffn_W0a"].T, "b0a": columns(a["L0_ffn_b0a"]), "w0b": a["L0_ffn_W0b"].T, "b0b": a["L0_ffn_b0b"],
        "w1a": a["L0_ffn_W1a"].T, "b1a": columns(a["L0_ffn_b1a"]), "w1b": a["L0_ffn_W1b"].T, "b1b": a["L0_ffn_b1b"],
        "wq": heads(a["L1_attn_Wq"]), "wk": heads(a["L1_attn_Wk"]), "wv": heads(a["L1_attn_Wv"]), "wo": a["L1_attn_Wo"],
        "bk": a["L1_attn_bk"].reshape(D1, H1).T.reshape(-1),
        "bqc": a["L1_attn_bq"].reshape(D1, H1), "bvc": a["L1_attn_bv"].reshape(D1, H1), "bo": a["L1_attn_bo"],
        "f1": a["L1_ffn_w1"].T, "fb1": columns(a["L1_ffn_b1"]), "f2": a["L1_ffn_w2"].T, "fb2": a["L1_ffn_b2"],
        "ident": np.eye(P, dtype=np.float32),
    }
    nc = bacc.Bacc("TRN2", target_bir_lowering=False, num_devices=1)
    data, args = {}, []
    for name, v in arrays.items():
        data[f"in_{name}"] = np.ascontiguousarray(v)
        args.append(nc.dram_tensor(f"in_{name}", v.shape, mybir.dt.from_np(v.dtype), kind="ExternalInput").ap())
    args.append(nc.dram_tensor("out", (B, T, C), F32, kind="ExternalOutput").ap())
    transformer(nc, *args)
    return run_bass_kernel_spmd(nc, [data], core_ids=[0]).results[0]["out"]
```
